# Optimizing a Trainium2 kernel written in Bass

```python
import numpy as np
import jax
import jax.numpy as jnp

def _softmax(x, axis=-1):
    return jax.nn.softmax(x, axis=axis)

def _gelu(x):
    return jax.nn.gelu(x, approximate=True)

def _silu(x):
    return jax.nn.silu(x)

def _sigmoid(x):
    return jax.nn.sigmoid(x)

def _layernorm(x, axis=-1, eps=1e-05):
    m = jnp.mean(x, axis=axis, keepdims=True)
    v = jnp.var(x, axis=axis, keepdims=True)
    return (x - m) / jnp.sqrt(v + eps)

def _scatter_add(tgt, idx, src, axis=0):
    return tgt.at[idx].add(src)

def _segment_sum(src, seg, n):
    return jax.ops.segment_sum(src, seg, n)
kernel_name = 'mk_gnn_ffn_d2_gnn_r8_5ac095'

def setup_inputs(seed: int=0):
    np.random.seed(seed)
    _w = jnp.asarray

    def _rec_inputs():
        import jax
        import jax.numpy as jnp
        _gk = jax.random.key(seed)
        x = -0.0002117 + 1 * jax.random.normal(jax.random.fold_in(_gk, 1), (6250, 256), jnp.float32)
        src = jax.random.randint(jax.random.fold_in(_gk, 2), (200000,), 0, 6250, jnp.int32)
        dst = jax.random.randint(jax.random.fold_in(_gk, 3), (200000,), 0, 6250, jnp.int32)
        _o = jnp.argsort(dst, stable=True)
        src = src[_o]
        dst = dst[_o]
        edge_weight = jax.random.uniform(jax.random.fold_in(_gk, 13), (200000,), jnp.float32, 0.0, 1)
        return (x, src, dst, edge_weight)
    x, src, dst, edge_weight = _rec_inputs()

    def _L0_gnn_setup():
        import jax, jax.numpy as jnp
        import numpy as np
        BN_EPS = 1e-05

        def _batchnorm(h, gamma, beta):
            mean = jnp.mean(h, axis=0, keepdims=True)
            var = jnp.var(h, axis=0, keepdims=True)
            return (h - mean) * jax.lax.rsqrt(var + BN_EPS) * gamma + beta
        key = jax.random.key(seed)
        ks = jax.random.split(key, 10)
        N, E, D = (12500, 400000, 256)
        x = jax.random.normal(ks[0], (N, D), dtype=jnp.float32)
        edge_src = jax.random.randint(ks[1], (E,), 0, N, dtype=jnp.int32)
        edge_dst = jax.random.randint(ks[2], (E,), 0, N, dtype=jnp.int32)
        edge_vals = jnp.ones((E,), dtype=jnp.float32)
        n_norm = jax.random.uniform(ks[3], (N, 1), dtype=jnp.float32)
        s = 1.0 / np.sqrt(D)
        w1 = jax.random.uniform(ks[4], (D, D), jnp.float32, -s, s)
        gamma1 = jnp.ones((D,), jnp.float32)
        beta1 = jnp.zeros((D,), jnp.float32)
        w2 = jax.random.uniform(ks[5], (D, D), jnp.float32, -s, s)
        eps_weight = jnp.zeros((1,), jnp.float32)
        gamma_h = jnp.ones((D,), jnp.float32)
        beta_h = jnp.zeros((D,), jnp.float32)
        return {'x': x, 'edge_src': edge_src, 'edge_dst': edge_dst, 'edge_vals': edge_vals, 'n_norm': n_norm, 'w1': w1, 'gamma1': gamma1, 'beta1': beta1, 'w2': w2, 'eps_weight': eps_weight, 'gamma_h': gamma_h, 'beta_h': beta_h}
    _L0_gnn_all = _L0_gnn_setup()
    _L0_gnn_in = {k: v for k, v in _L0_gnn_all.items() if k in ('w1', 'gamma1', 'beta1', 'w2', 'eps_weight', 'gamma_h', 'beta_h')}
    del _L0_gnn_all

    def _L0_ffn_setup():
        import math
        import jax, jax.numpy as jnp
        import numpy as np
        CAPACITY_FACTOR = 1.25
        TOP_K = 2
        LN_EPS = 1e-05

        def _layer_norm(x, gamma, beta):
            mu = jnp.mean(x, axis=-1, keepdims=True)
            var = jnp.var(x, axis=-1, keepdims=True)
            return (x - mu) * jax.lax.rsqrt(var + LN_EPS) * gamma + beta
        key = jax.random.key(seed)
        ks = jax.random.split(key, 4)
        B, S, D, F, E = (8, 512, 256, 512, 8)
        x = jax.random.normal(ks[0], (B, S, D), dtype=jnp.float32)
        Wr = jax.random.normal(ks[1], (D, E), dtype=jnp.float32) / np.sqrt(D)
        br = jnp.zeros((E,), jnp.float32)
        W1 = jax.random.normal(ks[2], (E, D, F), dtype=jnp.float32) / np.sqrt(D)
        b1 = jnp.zeros((E, F), jnp.float32)
        W2 = jax.random.normal(ks[3], (E, F, D), dtype=jnp.float32) / np.sqrt(F)
        b2 = jnp.zeros((E, D), jnp.float32)
        gamma = jnp.ones((D,), jnp.float32)
        beta = jnp.zeros((D,), jnp.float32)
        return {'x': x, 'Wr': Wr, 'br': br, 'W1': W1, 'b1': b1, 'W2': W2, 'b2': b2, 'gamma': gamma, 'beta': beta}
    _L0_ffn_all = _L0_ffn_setup()
    _L0_ffn_in = {k: v for k, v in _L0_ffn_all.items() if k in ('Wr', 'br', 'W1', 'b1', 'W2', 'b2', 'gamma', 'beta')}
    del _L0_ffn_all

    def _L1_gnn_setup():
        import jax, jax.numpy as jnp
        import numpy as np
        from jax.ops import segment_sum, segment_max
        N_NODES = 6250
        N_EDGES = 100000
        IN_DIM = 256
        OUT_DIM = 64
        N_HEADS = 4
        key = jax.random.key(seed)
        k1, k2, k3, k4, k5, k6 = jax.random.split(key, 6)
        h = jax.random.normal(k1, (N_NODES, IN_DIM), dtype=jnp.float32)
        src = jax.random.randint(k2, (N_EDGES,), 0, N_NODES, dtype=jnp.int32)
        dst = jax.random.randint(k3, (N_EDGES,), 0, N_NODES, dtype=jnp.int32)
        W = jax.random.normal(k4, (N_HEADS, IN_DIM, OUT_DIM), dtype=jnp.float32) * 0.05
        a_src = jax.random.normal(k5, (N_HEADS, OUT_DIM), dtype=jnp.float32) * 0.05
        a_dst = jax.random.normal(k6, (N_HEADS, OUT_DIM), dtype=jnp.float32) * 0.05
        return {'h': h, 'src': src, 'dst': dst, 'W': W, 'a_src': a_src, 'a_dst': a_dst}
    _L1_gnn_all = _L1_gnn_setup()
    _L1_gnn_in = {k: v for k, v in _L1_gnn_all.items() if k in ('W', 'a_src', 'a_dst')}
    del _L1_gnn_all

    def _L1_ffn_setup():
        import jax, jax.numpy as jnp
        import numpy as np
        DIM = 256
        H = 8
        D = 64
        G = 64
        INNER = H * D
        SCALE = D ** (-0.5)
        key = jax.random.key(seed)
        ks = jax.random.split(key, 12)
        B, N = (4, 2048)
        x = jax.random.normal(ks[0], (B, N, DIM), dtype=jnp.float32)
        s = lambda fan_in: 1.0 / np.sqrt(fan_in)
        W_fx = jax.random.normal(ks[1], (DIM, INNER), dtype=jnp.float32) * s(DIM)
        b_fx = jnp.zeros((INNER,), dtype=jnp.float32)
        W_x = jax.random.normal(ks[2], (DIM, INNER), dtype=jnp.float32) * s(DIM)
        b_x = jnp.zeros((INNER,), dtype=jnp.float32)
        A = jax.random.normal(ks[3], (G, D), dtype=jnp.float32)
        Q, _ = jnp.linalg.qr(A.T)
        W_slice = Q[:, :G].astype(jnp.float32)
        b_slice = jnp.zeros((G,), dtype=jnp.float32)
        W_q = jax.random.normal(ks[4], (D, D), dtype=jnp.float32) * s(D)
        W_k = jax.random.normal(ks[5], (D, D), dtype=jnp.float32) * s(D)
        W_v = jax.random.normal(ks[6], (D, D), dtype=jnp.float32) * s(D)
        W_out = jax.random.normal(ks[7], (INNER, DIM), dtype=jnp.float32) * s(INNER)
        b_out = jnp.zeros((DIM,), dtype=jnp.float32)
        temperature = jnp.ones((1, H, 1, 1), dtype=jnp.float32) * 0.5
        return {'x': x, 'W_fx': W_fx, 'b_fx': b_fx, 'W_x': W_x, 'b_x': b_x, 'W_slice': W_slice, 'b_slice': b_slice, 'W_q': W_q, 'W_k': W_k, 'W_v': W_v, 'W_out': W_out, 'b_out': b_out, 'temperature': temperature}
    _L1_ffn_all = _L1_ffn_setup()
    _L1_ffn_in = {k: v for k, v in _L1_ffn_all.items() if k in ('W_fx', 'b_fx', 'W_x', 'b_x', 'W_slice', 'b_slice', 'W_q', 'W_k', 'W_v', 'W_out', 'b_out', 'temperature')}
    del _L1_ffn_all
    return {'x': x, 'src': src, 'dst': dst, 'edge_weight': edge_weight, 'L0_gnn_w1': _L0_gnn_in['w1'], 'L0_gnn_gamma1': _L0_gnn_in['gamma1'], 'L0_gnn_beta1': _L0_gnn_in['beta1'], 'L0_gnn_w2': _L0_gnn_in['w2'], 'L0_gnn_eps_weight': _L0_gnn_in['eps_weight'], 'L0_gnn_gamma_h': _L0_gnn_in['gamma_h'], 'L0_gnn_beta_h': _L0_gnn_in['beta_h'], 'L0_ffn_Wr': _L0_ffn_in['Wr'], 'L0_ffn_br': _L0_ffn_in['br'], 'L0_ffn_W1': _L0_ffn_in['W1'], 'L0_ffn_b1': _L0_ffn_in['b1'], 'L0_ffn_W2': _L0_ffn_in['W2'], 'L0_ffn_b2': _L0_ffn_in['b2'], 'L0_ffn_gamma': _L0_ffn_in['gamma'], 'L0_ffn_beta': _L0_ffn_in['beta'], 'L1_gnn_W': _L1_gnn_in['W'], 'L1_gnn_a_src': _L1_gnn_in['a_src'], 'L1_gnn_a_dst': _L1_gnn_in['a_dst'], 'L1_ffn_W_fx': _L1_ffn_in['W_fx'], 'L1_ffn_b_fx': _L1_ffn_in['b_fx'], 'L1_ffn_W_x': _L1_ffn_in['W_x'], 'L1_ffn_b_x': _L1_ffn_in['b_x'], 'L1_ffn_W_slice': _L1_ffn_in['W_slice'], 'L1_ffn_b_slice': _L1_ffn_in['b_slice'], 'L1_ffn_W_q': _L1_ffn_in['W_q'], 'L1_ffn_W_k': _L1_ffn_in['W_k'], 'L1_ffn_W_v': _L1_ffn_in['W_v'], 'L1_ffn_W_out': _L1_ffn_in['W_out'], 'L1_ffn_b_out': _L1_ffn_in['b_out'], 'L1_ffn_temperature': _L1_ffn_in['temperature']}

def reference(x, src, dst, edge_weight, L0_gnn_w1, L0_gnn_gamma1, L0_gnn_beta1, L0_gnn_w2, L0_gnn_eps_weight, L0_gnn_gamma_h, L0_gnn_beta_h, L0_ffn_Wr, L0_ffn_br, L0_ffn_W1, L0_ffn_b1, L0_ffn_W2, L0_ffn_b2, L0_ffn_gamma, L0_ffn_beta, L1_gnn_W, L1_gnn_a_src, L1_gnn_a_dst, L1_ffn_W_fx, L1_ffn_b_fx, L1_ffn_W_x, L1_ffn_b_x, L1_ffn_W_slice, L1_ffn_b_slice, L1_ffn_W_q, L1_ffn_W_k, L1_ffn_W_v, L1_ffn_W_out, L1_ffn_b_out, L1_ffn_temperature):
    import jax
    import jax.numpy as jnp

    def _L0_gnn_ref(x, edge_src, edge_dst, edge_vals, n_norm, w1, gamma1, beta1, w2, eps_weight, gamma_h, beta_h):
        import jax, jax.numpy as jnp
        import numpy as np
        BN_EPS = 1e-05

        def _batchnorm(h, gamma, beta):
            mean = jnp.mean(h, axis=0, keepdims=True)
            var = jnp.var(h, axis=0, keepdims=True)
            return (h - mean) * jax.lax.rsqrt(var + BN_EPS) * gamma + beta
        N = x.shape[0]
        msgs = edge_vals[:, None] * x[edge_src]
        agg = jax.ops.segment_sum(msgs, edge_dst, num_segments=N)
        y = agg + eps_weight * x
        h = jax.nn.relu(_batchnorm(y @ w1.T, gamma1, beta1))
        y = h @ w2.T
        y = y * n_norm
        y = _batchnorm(y, gamma_h, beta_h)
        y = jax.nn.relu(y)
        y = y + x
        return y

    def _L0_ffn_ref(x, Wr, br, W1, b1, W2, b2, gamma, beta):
        import math
        import jax, jax.numpy as jnp
        import numpy as np
        CAPACITY_FACTOR = 1.25
        TOP_K = 2
        LN_EPS = 1e-05

        def _layer_norm(x, gamma, beta):
            mu = jnp.mean(x, axis=-1, keepdims=True)
            var = jnp.var(x, axis=-1, keepdims=True)
            return (x - mu) * jax.lax.rsqrt(var + LN_EPS) * gamma + beta
        B, S, D = x.shape
        E = Wr.shape[1]
        N = B * S
        K = TOP_K
        logits = jnp.mean(x, axis=1) @ Wr + br
        routing_weights = jax.nn.softmax(logits, axis=-1)
        capacity = float(math.ceil(N * CAPACITY_FACTOR / E))
        expected_loads = routing_weights.sum(axis=0) * (N / B)
        scale = jnp.where(expected_loads > capacity, capacity / expected_loads, 1.0)
        routing_weights = jax.nn.softmax(routing_weights * scale, axis=-1)
        rw_tok = jnp.broadcast_to(routing_weights[:, None, :], (B, S, E)).reshape(N, E)
        top_w, top_i = jax.lax.top_k(rw_tok, K)
        top_w = jax.nn.softmax(top_w, axis=-1)
        xf = x.reshape(N, D)
        h = jax.nn.gelu(jnp.einsum('nd,edf->enf', xf, W1) + b1[:, None, :], approximate=False)
        y = jnp.einsum('enf,efd->end', h, W2) + b2[:, None, :]
        w_dense = jnp.zeros((N, E), x.dtype).at[jnp.arange(N)[:, None], top_i].add(top_w)
        out = jnp.einsum('ne,end->nd', w_dense, y).reshape(B, S, D)
        out = _layer_norm(out + x, gamma, beta)
        return out

    def _L1_gnn_ref(h, src, dst, W, a_src, a_dst):
        import jax, jax.numpy as jnp
        import numpy as np
        from jax.ops import segment_sum, segment_max
        N_NODES = 6250
        N_EDGES = 100000
        IN_DIM = 256
        OUT_DIM = 64
        N_HEADS = 4
        n = h.shape[0]
        z = jnp.einsum('ni,hio->nho', h, W)
        e_src = jnp.einsum('nho,ho->nh', z, a_src)
        e_dst = jnp.einsum('nho,ho->nh', z, a_dst)
        e = jax.nn.leaky_relu(e_src[src] + e_dst[dst], negative_slope=0.01)
        m = segment_max(e, dst, num_segments=n)
        e_exp = jnp.exp(e - m[dst])
        denom = segment_sum(e_exp, dst, num_segments=n)
        alpha = e_exp / denom[dst]
        msg = alpha[:, :, None] * z[src]
        out = segment_sum(msg, dst, num_segments=n)
        return out.reshape(n, N_HEADS * OUT_DIM)

    def _L1_ffn_ref(x, W_fx, b_fx, W_x, b_x, W_slice, b_slice, W_q, W_k, W_v, W_out, b_out, temperature):
        import jax, jax.numpy as jnp
        import numpy as np
        DIM = 256
        H = 8
        D = 64
        G = 64
        INNER = H * D
        SCALE = D ** (-0.5)
        B, N, _ = x.shape
        fx_mid = (x @ W_fx + b_fx).reshape(B, N, H, D).transpose(0, 2, 1, 3)
        x_mid = (x @ W_x + b_x).reshape(B, N, H, D).transpose(0, 2, 1, 3)
        temp = jnp.clip(temperature, 0.1, 5.0)
        slice_weights = jax.nn.softmax((x_mid @ W_slice + b_slice) / temp, axis=-1)
        slice_norm = slice_weights.sum(axis=2)
        slice_token = jnp.einsum('bhnc,bhng->bhgc', fx_mid, slice_weights)
        slice_token = slice_token / (slice_norm[..., None] + 1e-05)
        q = slice_token @ W_q
        k = slice_token @ W_k
        v = slice_token @ W_v
        attn = jax.nn.softmax(jnp.einsum('bhgc,bhkc->bhgk', q, k) * SCALE, axis=-1)
        out_slice = jnp.einsum('bhgk,bhkc->bhgc', attn, v)
        out_x = jnp.einsum('bhgc,bhng->bhnc', out_slice, slice_weights)
        out_x = out_x.transpose(0, 2, 1, 3).reshape(B, N, INNER)
        return out_x @ W_out + b_out
    deg = jnp.maximum(jax.ops.segment_sum(jnp.ones(dst.shape, jnp.float32), dst, num_segments=6250), 1.0)
    deg_isqrt = deg ** (-0.5)
    x = x + _L0_gnn_ref(_layernorm(x, axis=-1), src, dst, edge_weight, deg_isqrt[:, None], L0_gnn_w1, L0_gnn_gamma1, L0_gnn_beta1, L0_gnn_w2, L0_gnn_eps_weight, L0_gnn_gamma_h, L0_gnn_beta_h)
    x = x + _L0_ffn_ref(_layernorm(x, axis=-1)[None], L0_ffn_Wr, L0_ffn_br, L0_ffn_W1, L0_ffn_b1, L0_ffn_W2, L0_ffn_b2, L0_ffn_gamma, L0_ffn_beta)[0]
    x = x + _L1_gnn_ref(_layernorm(x, axis=-1), src, dst, L1_gnn_W, L1_gnn_a_src, L1_gnn_a_dst)
    x = x + _L1_ffn_ref(_layernorm(x, axis=-1)[None], L1_ffn_W_fx, L1_ffn_b_fx, L1_ffn_W_x, L1_ffn_b_x, L1_ffn_W_slice, L1_ffn_b_slice, L1_ffn_W_q, L1_ffn_W_k, L1_ffn_W_v, L1_ffn_W_out, L1_ffn_b_out, L1_ffn_temperature)[0]
    return x

_drawn_inputs = setup_inputs


def setup_inputs(seed=0):
    import zlib

    import numpy as np

    out = dict(_drawn_inputs(seed))
    spreads = {'L0_gnn_gamma1': (1.0, 0.2),
     'L0_gnn_beta1': (0.0, 0.289),
     'L0_gnn_gamma_h': (1.0, 0.2),
     'L0_gnn_beta_h': (0.0, 0.1),
     'L0_ffn_br': (0.0, 0.8),
     'L0_ffn_b1': (0.0, 0.545),
     'L0_ffn_b2': (0.0, 0.355),
     'L0_ffn_gamma': (1.0, 0.2),
     'L0_ffn_beta': (0.0, 0.1),
     'L1_ffn_b_fx': (0.0, 0.1),
     'L1_ffn_b_x': (0.0, 2.0),
     'L1_ffn_b_slice': (0.0, 2.0),
     'L1_ffn_b_out': (0.0, 0.1),
     'L1_ffn_temperature': (0.5, 0.6)}
    factors = {'L0_ffn_Wr': 8.0,
     'L1_gnn_a_src': 4.391,
     'L1_gnn_a_dst': 8.0,
     'L1_ffn_W_x': 8.0,
     'L1_ffn_W_slice': 8.0,
     'L1_ffn_W_q': 8.0,
     'L1_ffn_W_k': 8.0}
    for name, (base, spread) in spreads.items():
        noise = np.random.default_rng([zlib.crc32(name.encode()), seed]).standard_normal(out[name].shape)
        drawn = base * np.exp(spread * noise) if base else spread * noise
        out[name] = jnp.asarray(drawn.astype(out[name].dtype))
    for name, factor in factors.items():
        out[name] = (out[name] * factor).astype(out[name].dtype)
    return out
```

```python
import concourse.bass as bass
from concourse import mybir
from contextlib import ExitStack

P = 128
N, D, E = 6250, 256, 200000
KC = D // P
T = -(-N // P)
LAST = N - (T - 1) * P
BLK = 256
SUB = BLK // P
HALF = 4
NB = -(-E // BLK)
GROUPS = -(-(NB + T - 1) // (2 * HALF)) * 2 * HALF
GC = -(-GROUPS // P)
NBP = NB + GROUPS - (NB + T - 1)
NODST = 1 << 20
NS = HALF * SUB
BODIES = GROUPS // HALF
NPAR = 17
NX = 8
F1 = 512
TOPK = 2
CAP = float(-(-N * 5 // (4 * NX)))
GH, GO = 4, 64
ROW = D + GH
SH, SG = 8, 64
INNER = SH * 64
PAIRS = SH // 2
EPS = 1e-5
CHUNKS = (T - 1) // 4


def over_pairs(eng, pairs, tail, body):
    body(0, 0, False)
    body(1, 1, False)
    with eng.Fori(1, pairs) as i:
        for u in range(2):
            body(i * 2 + u, u, True)
    for t in range(2 * pairs, 2 * pairs + tail):
        body(t, t % 2, True)


def wait_apart(eng, sem, value, turn):
    eng.wait_ge(sem, value)
    eng.sem_inc(turn, 1)


class Chain:

    def __init__(self, eng, sem):
        self.eng, self.sem, self.at = eng, sem, 0

    def __call__(self, ins):
        ins.then_inc(self.sem, 1)
        self.at = self.at + 1
        self.eng.wait_ge(self.sem, self.at)


def build(nc, STAGE, x, src, dst, ew, w1T, w2T, gamma1, beta1, epsw, gamma_h, beta_h,
          Wr, br, W1, b1, W2, b2, gamma, beta, gW, ga_src, ga_dst,
          W_fx, b_fx, W_xT, b_x, W_slice, b_slice, W_q, W_k, W_v, W_out, b_out, temperature, out):
    fp32, bf16, i32 = mybir.dt.float32, mybir.dt.bfloat16, mybir.dt.int32
    ALU, ACT, AX = mybir.AluOpType, mybir.ActivationFunctionType, mybir.AxisListType
    ds = bass.ds

    hTab = nc.dram_tensor("hTab", (T * P, D), fp32, kind="Internal").ap()
    zTab = nc.dram_tensor("zTab", (T * P, ROW), fp32, kind="Internal").ap()
    dlTab = nc.dram_tensor("dlTab", (GC * P, BLK), fp32, kind="Internal").ap()

    ctx = ExitStack()
    with ctx:
        ctx.enter_context(nc.allow_non_contiguous_dma("small parameters and strided rows"))

        def sb(name, shape, dt=fp32):
            return ctx.enter_context(nc.sbuf_tensor(name, shape, dt))

        def sem(name):
            return ctx.enter_context(nc.semaphore(name))

        PB = [ctx.enter_context(nc.psum_tensor(f"PB{i}", [P, 512], fp32)) for i in range(8)]

        XH = sb("XH", [P, T, D])
        ARENA = T * 512
        A = sb("A", [P, ARENA])
        YD = A[:, 0:T * 384].rearrange("p (t c n) -> p t c n", c=3, n=P)
        tab = ARENA - 3 * GC * BLK
        SRCT = A[:, tab:tab + GC * 256].bitcast(i32)
        DLT = A[:, tab + GC * 256:tab + 2 * GC * 256]
        WT = A[:, tab + 2 * GC * 256:tab + 3 * GC * 256]
        G = sb("G", [P, 2 * NS * ROW])
        GR = G[:, :].rearrange("p (s r) -> p s r", r=ROW)
        tg = G[:, 0:2 * 3 * BLK].rearrange("p (s a e) -> p s a e", s=2, a=3)
        tf = G[:, 2 * 3 * BLK:4 * 3 * BLK].rearrange("p (s a e) -> p s a e", s=2, a=3)
        TK = sb("TK", [P, GC * P], i32)
        S = sb("S", [P, 2, SUB, P])
        ST = sb("ST", [P, 2, BLK])
        iint = ST[:, 0, 0:P].bitcast(i32)
        S1 = sb("S1", [P, 2, SUB, P], bf16)
        IDX = sb("IDX", [P, 2, NS], i32)
        DLS = sb("DLS", [P, 2, NS])
        WS = sb("WS", [P, 2, NS])
        ident = sb("ident", [P, P])
        iota = sb("iota", [P, P])
        iotap = sb("iotap", [P, 1])
        ipint = sb("ipint", [P, 1], i32)
        ones = sb("ones", [P, P])
        onesb = sb("onesb", [P, P], bf16)
        valid = sb("valid", [P, 2])
        work = A[:, 0:2048]
        lastI = A[0:1, 3072:3072 + NBP].bitcast(i32)
        lastF = A[0:1, 4096:4096 + NBP]
        cmp = work[0:T - 1, 0:NBP]
        kki = work[:, 1024:1024 + GC * P].bitcast(i32)
        kk = A[:, 2048:2048 + GC * P]
        tcmp = work[0:T - 1, 0:GC * P]
        thr = sb("thr", [P, 2])
        cols = sb("cols", [P, 5, GC])
        cidx = sb("cidx", [P, GC], i32)
        kci = sb("kci", [P, GC], i32)
        BS = sb("BS", [P, T, 6])
        MV = sb("MV", [P, T, 2])
        RS = sb("RS", [P, T])
        HS = sb("HS", [P, 2, D])
        w12 = sb("w12", [P, 2, KC, D])
        bnp = sb("bnp", [P, 5, KC])
        BSF = sb("BSF", [P, KC, CHUNKS + 1, 6])
        MVF = sb("MVF", [P, KC, 2])
        bns = sb("bns", [P, 4, KC])

        T1T = A[:, 0:KC * T * P].rearrange("p (k n) -> p k n", k=KC)
        ew0 = KC * T * P
        EW1 = A[:, ew0:ew0 + TOPK * KC * F1].rearrange("p (j k f) -> p j k f", j=TOPK, k=KC)
        FQ = F1 // P
        ew1 = ew0 + TOPK * KC * F1
        EW2 = A[:, ew1:ew1 + TOPK * FQ * D].rearrange("p (j q d) -> p j q d", j=TOPK, q=FQ)
        HID = G[:, 0:TOPK * FQ * 512].rearrange("p (j q n) -> p j q n", j=TOPK, q=FQ)
        ms = sb("ms", [P, KC])
        MSB = sb("MSB", [P, KC, P])
        wr = sb("wr", [P, KC, NX])
        rt = sb("rt", [P, 16, NX])
        r1 = sb("r1", [P, 16])
        ohs = sb("ohs", [P, 3, NX])
        ohT = sb("ohT", [NX, 3, P])
        emul = sb("emul", [P, 6])
        ebase = sb("ebase", [P, 6])
        EI = sb("EI", [P, TOPK, 6], i32)
        b1s = sb("b1s", [NX, F1])
        b2s = sb("b2s", [NX, D])
        b1c = sb("b1c", [P, TOPK * FQ])
        B2M = sb("B2M", [P, D])
        rows4 = sb("rows4", [P, 4, D])
        gbB, aB = rows4[:, 0:2, :], rows4[:, 2:4, :]
        nmr = sb("nmr", [P, T])
        vst = sb("vst", [P, 2, 6])
        vmv = sb("vmv", [P, 2, 2])
        vrs = sb("vrs", [P, 2])
        mhalf = sb("mhalf", [P, 1])
        WZ = sb("WZ", [P, KC, D + 2 * GH])
        zS = sb("zS", [P, 2, D + 2 * GH])
        TT = sb("TT", [P, 2, KC, P])
        EM = sb("EM", [P, T, 2 * GH])

        H2 = A[:, 0:T * ROW].rearrange("p (t r) -> p t r", r=ROW)
        us0 = T * ROW
        US = A[:, us0:us0 + 2 * NS * ROW].rearrange("p (s r) -> p s r", r=ROW)
        rb0 = us0 + 2 * NS * ROW
        ROWB = A[:, rb0:rb0 + 2 * HALF * BLK].rearrange("p (s g e) -> p s g e", s=2, g=HALF)
        sc = sb("sc", [P, 4, NS * GH])
        scn = sb("scn", [P, NS, 2 * GH])
        gm = sb("gm", [P, GH])
        gm4 = sb("gm4", [GH, 1 + GH])
        RD = sb("RD", [P, T, GH])

        SWT = A[:, :].rearrange("p (t q n) -> p t q n", q=PAIRS, n=P)
        WXT = A[:, ARENA - 1024:ARENA].rearrange("p (q k) -> p q k", q=PAIRS)
        WSL = G[:, 0:1024].rearrange("p (k f) -> p k f", k=KC)
        VV = G[:, 0:1024].rearrange("p (q d) -> p q d", q=PAIRS)
        BSL = G[:, 1024:1536]
        SWS = G[:, 1536:2560].rearrange("p (s f) -> p s f", s=2)
        SWsum = G[:, 2560:3072]
        XS = G[:, 3072:4096].rearrange("p (k f) -> p k f", k=KC)
        WFX = w12[:, :, :, :].rearrange("p a k f -> p (a k f)").rearrange("p (k f) -> p k f", k=KC)
        WOUT = rows4
        WBD = sb("WBD", [P, 4, P])
        bm = sb("bm", [P, 2, P])
        it = sb("it", [P, SH])
        bxc = sb("bxc", [P, PAIRS])
        bxB = S[:, :, :, :].rearrange("p a b n -> p (a b) n")
        bsB = MSB[:, 0, 0:SG]
        boutB = B2M
        bfx = b1s[0:1, :]
        nrow = zS[0:1, :, :].rearrange("p a b -> p (a b)")[:, 0:INNER]
        sden = sb("sden", [P, PAIRS])
        ax = sb("ax", [P, 4, SH])
        q4 = [b[:, :, :, :].rearrange("p a b n -> p (a b) n") for b in (TT, S)]
        STK = ST[:, :, :].rearrange("p a (b n) -> p (a b) n", n=P)
        STT = HS[:, :, :].rearrange("p a (b n) -> p (a b) n", n=P)
        QT, KT = SWS[:, 0, :].rearrange("p (q n) -> p q n", n=P), SWS[:, 1, :].rearrange("p (q n) -> p q n", n=P)
        VS, AT = XS[:, 0, :].rearrange("p (q n) -> p q n", n=P), XS[:, 1, :].rearrange("p (q n) -> p q n", n=P)
        ATT, OST = q4

        x_in = [sem(f"x_in{i}") for i in range(4)]
        par_in = sem("par_in")
        last_in = sem("last_in")
        consts_ready = sem("consts_ready")
        pool_step = sem("pool_step")
        dve_step = sem("dve_step")
        act_step = sem("act_step")
        lastf_ready = sem("lastf_ready")
        lastrow_ready = sem("lastrow_ready")
        tcmp_ready = sem("tcmp_ready")
        tk_psum = sem("tk_psum")
        cidx_ready = sem("cidx_ready")
        tab_in = [sem(f"tab_in{i}") for i in range(2)]
        tabf_ready = sem("tabf_ready")
        tab_turned = sem("tab_turned")
        tab_kept = sem("tab_kept")
        dl_stored = sem("dl_stored")
        veps_ready = sem("veps_ready")
        sqrt_ready = sem("sqrt_ready")
        h_ready = sem("h_ready")
        h_stored = [sem(f"h_stored{i}") for i in range(2)]
        h_turned = sem("h_turned")
        h_kept = sem("h_kept")
        h_added = sem("h_added")
        idx_ready = sem("idx_ready")
        rows_in = [sem(f"rows_in{i}") for i in range(2)]
        rows_used = sem("rows_used")
        gather_turn = sem("gather_turn")
        act_turn = sem("act_turn")
        onehot_ready = sem("onehot_ready")
        part_ready = sem("part_ready")
        part_added = sem("part_added")
        lin_ready = sem("lin_ready")
        lin_stat = sem("lin_stat")
        lin_kept = sem("lin_kept")
        degmax = sem("degmax")
        degsqrt = sem("degsqrt")
        bn_var = sem("bn_var")
        bn_sqrt = sem("bn_sqrt")
        bn_ready = sem("bn_ready")
        relu_ready = sem("relu_ready")
        r_ready = sem("r_ready")
        r_turned = sem("r_turned")
        x1_ready = sem("x1_ready")
        out_stored = sem("out_stored")
        dve_turn = sem("dve_turn")
        t1_ready = sem("t1_ready")
        t1_turned = sem("t1_turned")
        t1_kept = sem("t1_kept")
        sums_ready = sem("sums_ready")
        msb_ready = sem("msb_ready")
        logits_ready = sem("logits_ready")
        exp_in = sem("exp_in")
        exp_out = sem("exp_out")
        chosen = sem("chosen")
        ohs_turned = sem("ohs_turned")
        ohT_ready = sem("ohT_ready")
        b_picked = sem("b_picked")
        b_kept = sem("b_kept")
        ew_in = sem("ew_in")
        ew_ready = sem("ew_ready")
        s1_ready = sem("s1_ready")
        gelu_ready = sem("gelu_ready")
        hid_used = sem("hid_used")
        moe_ready = sem("moe_ready")
        moe_kept = sem("moe_kept")
        var_ready = sem("var_ready")
        rs_ready = sem("rs_ready")
        v_ready = sem("v_ready")
        x2_ready = sem("x2_ready")
        t2_ready = sem("t2_ready")
        t2_turned = sem("t2_turned")
        t2_kept = sem("t2_kept")
        z_ready = sem("z_ready")
        z_kept = sem("z_kept")
        em_ready = sem("em_ready")
        h2_zero = sem("h2_zero")
        gm_step = sem("gm_step")
        gm_turned = sem("gm_turned")
        gm_spread = sem("gm_spread")
        rowb_in = [sem(f"rowb_in{i}") for i in range(2)]
        idx2_ready = sem("idx2_ready")
        rows2_in = [sem(f"rows2_in{i}") for i in range(2)]
        st_ready = sem("st_ready")
        edm_ready = sem("edm_ready")
        edm_used = sem("edm_used")
        small_step = sem("small_step")
        expo_in = sem("expo_in")
        expo_out = sem("expo_out")
        us_ready = sem("us_ready")
        sum_ready = sem("sum_ready")
        sum_added = sem("sum_added")
        x3_ready = sem("x3_ready")
        onehot2_ready = sem("onehot2_ready")
        wbd_zero = sem("wbd_zero")
        par2_in = sem("par2_in")
        slp_turn = sem("slp_turn")
        wsl_psum = sem("wsl_psum")
        wsl_ready = sem("wsl_ready")
        t3_ready = sem("t3_ready")
        t3_turned = sem("t3_turned")
        t3_kept = sem("t3_kept")
        l_ready = sem("l_ready")
        l_kept = sem("l_kept")
        l_max = sem("l_max")
        l_less = sem("l_less")
        l_exp = sem("l_exp")
        sw_ready = sem("sw_ready")
        sw_turned = sem("sw_turned")
        sw_kept = sem("sw_kept")
        sw_summed = sem("sw_summed")
        tok_pe = sem("tok_pe")
        tok_dve = sem("tok_dve")
        tok_exp = sem("tok_exp")
        swt_staged = sem("swt_staged")
        mix_ready = sem("mix_ready")
        fin_ready = sem("fin_ready")
        z_stored = [sem(f"z_stored{i}") for i in range(2)]

        block = ctx.enter_context(nc.Block())

        @block.sync
        def _(sp):
            xv = x[0:(T - 1) * P, :].rearrange("(t p) d -> p t d", p=P)
            sp.dma_start(lastI[:, :], dst.rearrange("(a b e) -> a b e", a=1, e=BLK)[:, :, BLK - 1]).then_inc(last_in, 16)
            for i in range(3):
                sp.dma_start(XH[:, 16 * i:16 * (i + 1), :], xv[:, 16 * i:16 * (i + 1), :]).then_inc(x_in[i], 16)
            sp.dma_start(XH[:, T - 1, :], x[(T - 1) * P:T * P, :]).then_inc(x_in[3], 16)
            sp.dma_start(w12[:, 0, :, :], w1T.rearrange("(k p) f -> p k f", p=P)).then_inc(par_in, 16)
            sp.dma_start(w12[:, 1, :, :], w2T.rearrange("(k p) f -> p k f", p=P)).then_inc(par_in, 16)
            for i, v in enumerate((gamma1, beta1, gamma_h, beta_h)):
                sp.dma_start(bnp[:, i, :], v.rearrange("(k p) -> p k", p=P)).then_inc(par_in, 16)
            sp.dma_start(bnp[:, 4, 0:1], epsw.rearrange("(a b) -> a b", a=1).broadcast_to((P, 1))).then_inc(par_in, 16)

            sp.dma_start(wr[:, :, :], Wr.rearrange("(k p) e -> p k e", p=P)).then_inc(par_in, 16)
            sp.dma_start(rt[:, 0, :], br.rearrange("(a b) -> a b", a=1).broadcast_to((P, NX))).then_inc(par_in, 16)
            sp.dma_start(b1s[:, :], b1).then_inc(par_in, 16)
            sp.dma_start(b2s[:, :], b2).then_inc(par_in, 16)
            sp.dma_start(gbB[:, 0, :], gamma.rearrange("(a b) -> a b", a=1).broadcast_to((P, D))).then_inc(par_in, 16)
            sp.dma_start(gbB[:, 1, :], beta.rearrange("(a b) -> a b", a=1).broadcast_to((P, D))).then_inc(par_in, 16)
            for k in range(KC):
                sp.dma_start(WZ[:, k, 0:D].rearrange("p (h o) -> p h o", h=GH), gW[:, k * P:(k + 1) * P, :].rearrange("h i o -> i h o")).then_inc(par_in, 16)
            sp.dma_start(aB[:, 0, :], ga_src.rearrange("(a h) o -> a (h o)", a=1).broadcast_to((P, D))).then_inc(par_in, 16)
            sp.dma_start(aB[:, 1, :], ga_dst.rearrange("(a h) o -> a (h o)", a=1).broadcast_to((P, D))).then_inc(par_in, 16)

            sp.wait_ge(wbd_zero, 1)
            for i, v in enumerate((W_slice, W_q, W_k, W_v)):
                for b in range(2):
                    sp.dma_start(WBD[b * SG:(b + 1) * SG, i, b * SG:(b + 1) * SG], v).then_inc(par2_in, 16)
            sp.dma_start(it[:, :], temperature.rearrange("a h b c -> (a b c) h").broadcast_to((P, SH))).then_inc(par2_in, 16)
            sp.dma_start(bxc[:, :], b_x.rearrange("(q p) -> p q", p=P)).then_inc(par2_in, 16)

            for j in range(GC):
                sp.wait_ge(tabf_ready, j + 1)
                sp.dma_start(dlTab[j * P:(j + 1) * P, :], tf[:, j % 2, 0, :]).then_inc(dl_stored, 16)
                sp.wait_ge(dl_stored, 16 * (j + 1))

            def store_h(t, s, warm):
                sp.wait_ge(h_ready, t + 1)
                sp.dma_start(hTab[ds(t * P, P), :], HS[:, s, :]).then_inc(h_stored[s], 16)
            over_pairs(sp, (T - 1) // 2, 1, store_h)

            def store_z(t, s, warm):
                sp.wait_ge(z_kept, 2 * (t + 1))
                sp.dma_start(zTab[ds(t * P, P), :], zS[:, s, 0:ROW]).then_inc(z_stored[s], 16)
            if STAGE >= 2:
                over_pairs(sp, (T - 1) // 2, 1, store_z)

            if STAGE >= 3:
                def load_rows(n, half, warm):
                    if warm:
                        sp.wait_ge(st_ready, HALF * (n - 1))
                    else:
                        sp.wait_ge(z_kept, 2 * T)
                    sp.dma_start(ROWB[:, half, :, :].rearrange("p g e -> p (g e)"),
                                 dlTab[ds(n * HALF, HALF), :].rearrange("(a g) e -> a (g e)", a=1).broadcast_to((P, HALF * BLK))).then_inc(rowb_in[half], 16)
                over_pairs(sp, BODIES // 2, 1, load_rows)

            if STAGE >= 4:
                sp.wait_ge(sum_ready, GROUPS)
                sp.dma_start(WXT, W_xT.rearrange("(q p) k -> p q k", p=P)).then_inc(par2_in, 16)
                sp.dma_start(WFX, W_fx.rearrange("(k p) f -> p k f", p=P)).then_inc(par2_in, 16)
                sp.dma_start(WOUT[:, :, :], W_out.rearrange("(q p) d -> p q d", p=P)).then_inc(par2_in, 16)
                sp.dma_start(bfx, b_fx.rearrange("(a b) -> a b", a=1)).then_inc(par2_in, 16)
                sp.dma_start(bsB, b_slice.rearrange("(a b) -> a b", a=1).broadcast_to((P, SG))).then_inc(par2_in, 16)
                sp.dma_start(boutB[:, :], b_out.rearrange("(a b) -> a b", a=1).broadcast_to((P, D))).then_inc(par2_in, 16)

                def store(t, s, warm):
                    sp.wait_ge(fin_ready, t + 1)
                    if isinstance(t, int) and t == T - 1:
                        sp.dma_start(out[t * P:N, :], XH[0:LAST, t, :]).then_inc(out_stored, 16)
                    else:
                        sp.dma_start(out[ds(t * P, P), :], XH[:, ds(t, 1), :].rearrange("p t d -> p (t d)")).then_inc(out_stored, 16)
                over_pairs(sp, (T - 1) // 2, 1, store)
                sp.wait_ge(out_stored, 16 * T)

            if STAGE == 3:
                sp.wait_ge(x3_ready, T)
            if STAGE == 1:
                sp.wait_ge(x1_ready, T)
            if STAGE == 2:
                sp.wait_ge(x2_ready, T)
                sp.wait_ge(z_stored[0], 16 * (T // 2 + 1))
                sp.wait_ge(z_stored[1], 16 * (T // 2))
            if STAGE <= 3:
                sp.dma_start(out[0:(T - 1) * P, :].rearrange("(t p) d -> p t d", p=P), XH[:, 0:T - 1, :]).then_inc(out_stored, 16)
                sp.dma_start(out[(T - 1) * P:N, :], XH[0:LAST, T - 1, :]).then_inc(out_stored, 16)
                sp.wait_ge(out_stored, 32)

        @block.gpsimd
        def _(pool):
            step = Chain(pool, pool_step)
            step(nc.gpsimd.memset(ident[:, :], 0.0))
            step(nc.gpsimd.affine_select(out=ident[:, :], in_=ident[:, :], compare_op=ALU.not_equal, fill=1.0,
                                         base=0, pattern=[[-1, P]], channel_multiplier=1))
            step(nc.gpsimd.iota(iint[:, :], [[1, P]], base=0, channel_multiplier=0))
            step(nc.gpsimd.iota(ipint[:, :], [[0, 1]], base=0, channel_multiplier=1))
            step(nc.gpsimd.iota(kki, [[1, GC * P]], base=0, channel_multiplier=0))
            step(nc.gpsimd.iota(kci[:, :], [[P, GC]], base=0, channel_multiplier=1))
            step(nc.gpsimd.tensor_copy(iota[:, :], iint[:, :]))
            step(nc.gpsimd.tensor_copy(iotap[:, :], ipint[:, :]))
            step(nc.gpsimd.tensor_copy(kk[:, :], kki))
            step(nc.gpsimd.tensor_copy(cols[:, 0, :], kci[:, :]))
            step(nc.gpsimd.memset(onesb[:, :], 1.0))
            step(nc.gpsimd.memset(ones[:, :], 1.0))
            step(nc.gpsimd.memset(valid[:, :], 1.0))
            step(nc.gpsimd.tensor_scalar(valid[:, 1:2], iotap[:, :], float(LAST), None, ALU.is_lt))
            step(nc.gpsimd.tensor_scalar(thr[:, 0:1], iotap[:, :], float(P), float(P), ALU.mult, ALU.add))
            step(nc.gpsimd.memset(mhalf[:, :], -0.5))
            step(nc.gpsimd.memset(WBD[:, :, :], 0.0))
            pool.sem_inc(wbd_zero, 1)
            step(nc.gpsimd.tensor_scalar(bm[:, 0, :], iota[:, :], float(SG), None, ALU.is_lt))
            step(nc.gpsimd.tensor_scalar(ms[:, 0:1], iotap[:, :], float(SG), None, ALU.is_lt))
            step(nc.gpsimd.tensor_scalar(bm[:, 0, :], bm[:, 0, :], ms[:, 0:1], None, ALU.is_equal))
            step(nc.gpsimd.tensor_scalar(bm[:, 1, :], bm[:, 0, :], 1.0, 1e30, ALU.subtract, ALU.mult))
            for q in range(6):
                k, m = (q, D) if q < KC else (q - KC, F1)
                step(nc.gpsimd.memset(emul[:, q:q + 1], float(m)))
                step(nc.gpsimd.tensor_scalar(ebase[:, q:q + 1], iotap[:, :], float(k * P), None, ALU.add))
            pool.sem_inc(consts_ready, 1)

            pool.wait_ge(cidx_ready, 1)
            for j in range(GC):
                if j >= 2:
                    pool.wait_ge(tabf_ready, j - 1)
                for a, arr in enumerate((dst, src, ew)):
                    o = tg[:, j % 2, a, :]
                    pool.indirect_dma_start(o if a == 2 else o.bitcast(i32), None,
                                            arr.rearrange("(b e) -> b e", e=BLK),
                                            bass.IndirectOffsetOnAxis(ap=cidx[:, j:j + 1], axis=0)).then_inc(tab_in[j % 2], 16)

            def add_h(t, s, warm):
                pool.wait_ge(h_ready, t + 1)
                nc.gpsimd.tensor_tensor(XH[:, ds(t, 1), :], XH[:, ds(t, 1), :], HS[:, s:s + 1, :], ALU.add).then_inc(h_added, 1)
            over_pairs(pool, (T - 1) // 2, 1, add_h)

            pool.wait_ge(h_stored[0], 16 * (T // 2 + 1))
            pool.wait_ge(h_stored[1], 16 * (T // 2))

            def gather(n, half, warm):
                pool.wait_ge(idx_ready, n + 1)
                if warm:
                    pool.wait_ge(rows_used, n - 1)
                pool.sem_inc(gather_turn, 1)
                for s in range(NS):
                    pool.indirect_dma_start(GR[:, half * NS + s, 0:D], None, hTab,
                                            bass.IndirectOffsetOnAxis(ap=IDX[:, half, s:s + 1], axis=0)).then_inc(rows_in[half], 16)
            over_pairs(pool, BODIES // 2, 0, gather)

            if STAGE >= 2:
                pool.wait_ge(chosen, 1)
                for j in range(TOPK):
                    for q in range(6):
                        tab_, o = (W1, EW1[:, j, q, :]) if q < KC else (W2, EW2[:, j, q - KC, :])
                        pool.indirect_dma_start(o, None, tab_.rearrange("e r c -> (e r) c"),
                                                bass.IndirectOffsetOnAxis(ap=EI[:, j, q:q + 1], axis=0)).then_inc(ew_in, 16)

                def finish(t, s):
                    pool.wait_ge(var_ready, t + 1)
                    nc.gpsimd.tensor_tensor(vrs[:, s:s + 1], vrs[:, s:s + 1], mhalf[:, :], ALU.pow).then_inc(rs_ready, 1)
                    pool.wait_ge(v_ready, t + 1)
                    v = HS[:, s, :]
                    nc.gpsimd.tensor_tensor(v, v, gbB[:, 0, :], ALU.mult).then_inc(pool_step, 1)
                    pool.wait_ge(pool_step, step.at + 2 * t + 1)
                    nc.gpsimd.tensor_tensor(v, v, gbB[:, 1, :], ALU.add).then_inc(pool_step, 1)
                    pool.wait_ge(pool_step, step.at + 2 * t + 2)
                    nc.gpsimd.tensor_tensor(XH[:, ds(t, 1), :], XH[:, ds(t, 1), :], HS[:, s:s + 1, :], ALU.add).then_inc(x2_ready, 1)
                over_pairs(pool, (T - 1) // 2, 1, lambda t, s, warm: finish(t, s))

            if STAGE >= 3:
                pool.wait_ge(s1_ready, TOPK * FQ * (CHUNKS + 1))
                nc.gpsimd.memset(A[:, 0:T * ROW], 0.0).then_inc(h2_zero, 1)
                pool.wait_ge(z_stored[0], 16 * (T // 2 + 1))
                pool.wait_ge(z_stored[1], 16 * (T // 2))

                def gather2(n, half, warm):
                    pool.wait_ge(idx2_ready, n + 1)
                    if warm:
                        pool.wait_ge(us_ready, HALF * (n - 1))
                    pool.sem_inc(gather_turn, 1)
                    for s in range(NS):
                        pool.indirect_dma_start(GR[:, half * NS + s, :], None, zTab,
                                                bass.IndirectOffsetOnAxis(ap=IDX[:, half, s:s + 1], axis=0)).then_inc(rows2_in[half], 16)
                over_pairs(pool, BODIES // 2, 0, gather2)

            if STAGE >= 4:
                pool.wait_ge(us_ready, GROUPS)
                pool.wait_ge(sum_ready, GROUPS)
                nc.gpsimd.memset(SWsum, 0.0).then_inc(sw_summed, 1)

                def slices(t, s, warm):
                    pool.wait_ge(l_max, t + 1)
                    lv = SWS[:, s, :].rearrange("p (h g) -> p h g", h=SH)
                    nc.gpsimd.tensor_tensor(lv, lv, ax[:, s, :].rearrange("p (h a) -> p h a", a=1).broadcast_to((P, SH, SG)), ALU.subtract).then_inc(l_less, 1)
                    if isinstance(t, int) and t == 0:
                        return
                    sum_slices(t - 1, 1 - s, P)

                def sum_slices(t, s, np_):
                    pool.wait_ge(sw_ready, t + 1)
                    pool.wait_ge(sw_summed, t + 1)
                    nc.gpsimd.tensor_tensor(SWsum[0:np_, :], SWsum[0:np_, :], SWS[0:np_, s, :], ALU.add).then_inc(sw_summed, 1)
                over_pairs(pool, (T - 1) // 2, 1, slices)
                sum_slices(T - 1, 0, LAST)

        @block.vector
        def _(dve):
            step = Chain(dve, dve_step)
            dve.wait_ge(last_in, 16)
            nc.vector.tensor_copy(lastF[:, :], lastI[:, :]).then_inc(lastf_ready, 1)
            dve.wait_ge(consts_ready, 1)
            dve.wait_ge(lastrow_ready, 1)
            h = NBP // 2
            for i in range(2):
                step(nc.vector.tensor_scalar(cmp[:, i * h:(i + 1) * h], PB[i][0:T - 1, 0:h], thr[0:T - 1, 0:1], None, ALU.is_lt))
            step(nc.vector.tensor_reduce(thr[0:T - 1, 1:2], cmp, AX.X, ALU.add))
            step(nc.vector.tensor_tensor(thr[0:T - 1, 1:2], thr[0:T - 1, 1:2], iotap[0:T - 1, :], ALU.add))
            nc.vector.tensor_scalar(tcmp, kk[0:T - 1, :], thr[0:T - 1, 1:2], None, ALU.is_gt).then_inc(tcmp_ready, 1)
            dve.wait_ge(tk_psum, 1)
            hk = GC * P // 2
            for i in range(2):
                step(nc.vector.tensor_copy(TK[:, i * hk:(i + 1) * hk], PB[2 + i][:, 0:hk]))
            step(nc.vector.tensor_copy(cols[:, 1, :], PB[4][:, 0:GC]))
            step(nc.vector.tensor_tensor(cols[:, 2, :], cols[:, 0, :], cols[:, 1, :], ALU.subtract))
            step(nc.vector.tensor_scalar_min(cols[:, 2, :], cols[:, 2, :], float(NBP - 1)))
            step(nc.vector.tensor_scalar_mul(cols[:, 3, :], cols[:, 1, :], float(P)))
            nc.vector.tensor_copy(cidx[:, :], cols[:, 2, :]).then_inc(cidx_ready, 1)
            for j in range(GC):
                s = j % 2
                dve.wait_ge(tab_in[s], 48 * (j // 2 + 1))
                if j >= 2:
                    dve.wait_ge(tab_turned, j - 1)
                    dve.wait_ge(dl_stored, 16 * (j - 1))
                step(nc.vector.tensor_scalar(tf[:, s, 0, :], tg[:, s, 0, :].bitcast(i32), cols[:, 3, j:j + 1], None, ALU.subtract))
                step(nc.vector.tensor_copy(tf[:, s, 1, :], tg[:, s, 1, :].bitcast(i32)))
                nc.vector.tensor_copy(tf[:, s, 2, :], tg[:, s, 2, :]).then_inc(tabf_ready, 1)

            def stats(t, s, warm):
                nc.vector.bn_stats(BS[:, ds(t, 1), :], XH[:, ds(t, 1), :]).then_inc(dve_step, 1)

            def row_stats():
                me, mo, m, v, rs = BS[:, :, 1], BS[:, :, 4], MV[:, :, 0], MV[:, :, 1], RS[:, :]
                step(nc.vector.tensor_tensor(m, me, mo, ALU.subtract))
                step(nc.vector.tensor_tensor(m, m, m, ALU.mult))
                step(nc.vector.tensor_tensor(v, BS[:, :, 2], BS[:, :, 5], ALU.add))
                step(nc.vector.tensor_scalar_mul(v, v, 1.0 / D))
                step(nc.vector.scalar_tensor_tensor(v, m, 0.25, v, ALU.mult, ALU.add))
                step(nc.vector.tensor_tensor(m, me, mo, ALU.add))
                step(nc.vector.tensor_scalar_mul(m, m, 0.5))
                nc.vector.tensor_scalar_add(rs, v, EPS).then_inc(veps_ready, 1)

            for i in range(4):
                dve.wait_ge(x_in[i], 16)
            over_pairs(dve, (T - 1) // 2, 1, stats)
            step.at += T
            dve.wait_ge(dve_step, step.at)
            row_stats()
            nc.vector.memset(YD[:, :, 2, :], 0.0).then_inc(dve_step, 1)
            step.at += 1
            dve.wait_ge(sqrt_ready, 1)
            step(nc.vector.reciprocal(RS[:, :], RS[:, :]))

            def norm(t, s, warm):
                if warm:
                    dve.wait_ge(h_turned, t - 1)
                    dve.wait_ge(h_added, t - 1)
                    dve.wait_ge(h_stored[s], (t // 2) * 16 if isinstance(t, int) else t * 8 - 8 * s)
                nc.vector.tensor_scalar(HS[:, s:s + 1, :], XH[:, ds(t, 1), :], MV[:, ds(t, 1), 0], RS[:, ds(t, 1)],
                                        ALU.subtract, ALU.mult).then_inc(h_ready, 1)
            over_pairs(dve, (T - 1) // 2, 1, norm)
            dve.wait_ge(h_kept, T)

            def onehots(n, half, warm, tks):
                dve.wait_ge(idx_ready, n + 1)
                for g in range(HALF):
                    gi = n * HALF + g
                    sl = g % 2
                    if warm or g >= 2:
                        dve.wait_ge(part_ready, gi - 1)
                    for b in range(SUB):
                        c = g * SUB + b
                        nc.vector.tensor_scalar(S[:, sl, b, :], iota[:, :], DLS[:, half, c:c + 1], WS[:, half, c:c + 1],
                                                ALU.is_equal, ALU.mult).then_inc(onehot_ready, 1)
                        nc.vector.tensor_scalar(S1[:, sl, b, :], iota[:, :], DLS[:, half, c:c + 1], None,
                                                ALU.is_equal).then_inc(onehot_ready, 1)
                    if warm or g >= 1:
                        add_part(gi - 1, (g - 1) % 2, tks[g])

            def add_part(gi, sl, tk):
                dve.wait_ge(part_ready, gi + 1)
                if not isinstance(gi, int) or gi >= 1:
                    dve.wait_ge(part_added, gi)
                y = A[:, ds(tk * 384, 384)]
                nc.vector.tensor_tensor(y, y, PB[sl][:, 0:384], ALU.add).then_inc(part_added, 1)

            def tiles_of(n):
                _, v = nc.values_load_multi_w_load_instructions(TK[0:1, ds(n * HALF + 1, HALF)], [mybir.EngineType.DVE], min_val=0, max_val=T - 1)
                return v

            def edges(n, half, warm):
                if warm:
                    lo = n * HALF - 1
                    _, v = nc.values_load_multi_w_load_instructions(TK[0:1, ds(lo, HALF)], [mybir.EngineType.DVE], min_val=0, max_val=T - 1)
                else:
                    lo = max(n * HALF - 1, 0)
                    _, v = nc.values_load_multi_w_load_instructions(TK[0:1, lo:lo + HALF], [mybir.EngineType.DVE], min_val=0, max_val=T - 1)
                    if n == 0:
                        v = (None, *v[0:HALF - 1])
                onehots(n, half, warm or n > 0, v)
            over_pairs(dve, BODIES // 2, 0, edges)
            _, v = nc.values_load_multi_w_load_instructions(TK[0:1, GROUPS - 1:GROUPS], [mybir.EngineType.DVE], min_val=0, max_val=T - 1)
            add_part(GROUPS - 1, (GROUPS - 1) % 2, v[0])

            dve.wait_ge(part_added, GROUPS)
            nc.vector.tensor_scalar_max(YD[:, :, 2, :], YD[:, :, 2, :], 1.0).then_inc(degmax, 1)
            dve.wait_ge(degsqrt, 1)
            step(nc.vector.reciprocal(YD[:, :, 2, :], YD[:, :, 2, :]))

            def chunk_stats(q, base):
                def f(c, s, warm, n=512):
                    for k in range(KC):
                        bank = PB[2 * s + k]
                        dve.wait_ge(lin_ready, base + KC * c + k + 1)
                        if q:
                            nt = 4 if n == 512 else 1
                            o = bank[:, 0:nt * P if n == 512 else n]
                            if n == 512:
                                o3 = o.rearrange("p (t n) -> p t n", n=P)
                                r = YD[:, ds(c * 4, 4), 2, :]
                            else:
                                o3, r = o, YD[:, T - 1, 2, 0:n]
                            nc.vector.tensor_tensor(o3, o3, r, ALU.mult).then_inc(dve_step, 1)
                            dve.wait_ge(dve_step, step.at + (KC * c + k + 1))
                        nc.vector.bn_stats(BSF[:, k, ds(c, 1), :], bank[:, 0:n]).then_inc(lin_stat, 1)
                return f

            def batchnorm(q, base):
                f = chunk_stats(q, base)
                over_pairs(dve, CHUNKS // 2, 0, f)
                f(CHUNKS, 0, True, LAST)
                if q:
                    step.at += KC * (CHUNKS + 1)
                dve.wait_ge(lin_stat, (q + 1) * KC * (CHUNKS + 1))
                for k in range(KC):
                    step(nc.vector.bn_aggr(MVF[:, k, :], BSF[:, k, :, :]))
                nc.vector.tensor_scalar_add(bns[:, 0, :], MVF[:, :, 1], EPS).then_inc(bn_var, 1)
                dve.wait_ge(bn_sqrt, q + 1)
                step(nc.vector.reciprocal(bns[:, 0, :], bns[:, 0, :]))
                step(nc.vector.tensor_tensor(bns[:, 1, :], bns[:, 0, :], bnp[:, 2 * q, :], ALU.mult))
                step(nc.vector.tensor_tensor(bns[:, 2, :], MVF[:, :, 0], bns[:, 1, :], ALU.mult))
                nc.vector.tensor_tensor(bns[:, 3, :], bnp[:, 2 * q + 1, :], bns[:, 2, :], ALU.subtract).then_inc(bn_ready, 1)
            dve.wait_ge(par_in, 16 * NPAR)
            batchnorm(0, 0)
            batchnorm(1, KC * (CHUNKS + 1))

            dve.wait_ge(h_added, T)

            def residual(t, s, warm):
                dve.wait_ge(r_turned, t + 1)
                nc.vector.tensor_tensor(XH[:, ds(t, 1), :], XH[:, ds(t, 1), :], PB[s][:, 0:D].rearrange("p (a d) -> p a d", a=1), ALU.add).then_inc(x1_ready, 1)
                dve.wait_ge(x1_ready, t + 1)
                nc.vector.bn_stats(BS[:, ds(t, 1), :], XH[:, ds(t, 1), :]).then_inc(dve_step, 1)
            over_pairs(dve, (T - 1) // 2, 1, residual)
            step.at += T
            dve.wait_ge(dve_step, step.at)

            if STAGE >= 2:
                row_stats()
                dve.wait_ge(sqrt_ready, 2)
                step(nc.vector.reciprocal(RS[:, :], RS[:, :]))
                step(nc.vector.scalar_tensor_tensor(nmr[:, :], MV[:, :, 0], -1.0, RS[:, :], ALU.mult, ALU.mult))
                dve.wait_ge(r_turned, T)

                def norm1(t, s, warm):
                    if warm:
                        dve.wait_ge(t1_turned, t - 1)
                    nc.vector.tensor_scalar(HS[:, s:s + 1, :], XH[:, ds(t, 1), :], MV[:, ds(t, 1), 0], RS[:, ds(t, 1)],
                                            ALU.subtract, ALU.mult).then_inc(t1_ready, 1)
                over_pairs(dve, (T - 1) // 2, 1, norm1)

                dve.wait_ge(sums_ready, 1)
                for k in range(KC):
                    step(nc.vector.tensor_copy(ms[:, k:k + 1], PB[2 + k][:, 0:1]))
                for k in range(KC):
                    ins = nc.vector.tensor_scalar(MSB[:, k, :], ones[:, :], ms[:, k:k + 1], 1.0 / N, ALU.mult, ALU.mult)
                    ins.then_inc(msb_ready, 1)
                dve.wait_ge(logits_ready, 1)
                lg, p, eq, p2 = rt[:, 1, :], rt[:, 2, :], rt[:, 3, :], rt[:, 4, :]
                step(nc.vector.tensor_tensor(lg, PB[4][:, 0:NX], rt[:, 0, :], ALU.add))

                def softmax8(nth):
                    step(nc.vector.tensor_reduce(r1[:, 0:1], lg, AX.X, ALU.max))
                    nc.vector.tensor_scalar(lg, lg, r1[:, 0:1], None, ALU.subtract).then_inc(exp_in, 1)
                    dve.wait_ge(exp_out, nth)
                    step(nc.vector.tensor_reduce(r1[:, 1:2], p, AX.X, ALU.add))
                    step(nc.vector.reciprocal(r1[:, 1:2], r1[:, 1:2]))
                    step(nc.vector.tensor_scalar(p, p, r1[:, 1:2], None, ALU.mult))
                softmax8(1)
                step(nc.vector.tensor_scalar_min(lg, p, CAP / N))
                softmax8(2)
                iota8 = iota[:, 0:NX]
                for j in range(TOPK):
                    src_ = p if j == 0 else p2
                    step(nc.vector.tensor_reduce(r1[:, 2 + j:3 + j], src_, AX.X, ALU.max))
                    step(nc.vector.tensor_scalar(eq, src_, r1[:, 2 + j:3 + j], -float(NX), ALU.is_ge, ALU.mult))
                    step(nc.vector.tensor_tensor(eq, eq, iota8, ALU.add))
                    step(nc.vector.tensor_reduce(r1[:, 4 + j:5 + j], eq, AX.X, ALU.min))
                    step(nc.vector.tensor_scalar_add(r1[:, 4 + j:5 + j], r1[:, 4 + j:5 + j], float(NX)))
                    step(nc.vector.tensor_scalar(ohs[:, j, :], iota8, r1[:, 4 + j:5 + j], None, ALU.is_equal))
                    if j == 0:
                        step(nc.vector.scalar_tensor_tensor(p2, ohs[:, 0, :], -2.0, p, ALU.mult, ALU.add))
                for j in range(TOPK):
                    ins = nc.vector.scalar_tensor_tensor(EI[:, j, :], emul[:, :], r1[:, 4 + j:5 + j], ebase[:, :], ALU.mult, ALU.add)
                    step(ins)
                dve.sem_inc(chosen, 1)
                nc.vector.tensor_tensor(r1[:, 6:7], r1[:, 3:4], r1[:, 2:3], ALU.subtract).then_inc(exp_in, 1)
                dve.wait_ge(exp_out, 3)
                step(nc.vector.tensor_scalar_add(r1[:, 8:9], r1[:, 7:8], 1.0))
                step(nc.vector.reciprocal(r1[:, 8:9], r1[:, 8:9]))
                step(nc.vector.tensor_tensor(r1[:, 9:10], r1[:, 7:8], r1[:, 8:9], ALU.mult))
                step(nc.vector.tensor_scalar(ohs[:, 2, :], ohs[:, 0, :], r1[:, 8:9], None, ALU.mult))
                step(nc.vector.scalar_tensor_tensor(ohs[:, 2, :], ohs[:, 1, :], r1[:, 9:10], ohs[:, 2, :], ALU.mult, ALU.add))
                dve.sem_inc(chosen, 1)
                dve.wait_ge(ohs_turned, 1)
                nc.vector.tensor_copy(ohT[:, :, :], PB[6][0:NX, 0:3 * P].rearrange("e (j n) -> e j n", j=3)).then_inc(ohT_ready, 1)
                dve.wait_ge(b_picked, 1)
                step(nc.vector.tensor_copy(b1c[:, :], PB[5][:, 0:TOPK * FQ]))
                nc.vector.tensor_copy(B2M[:, :], PB[7][:, 0:D]).then_inc(b_kept, 1)
                dve.wait_ge(ew_in, 16 * 12)
                for j in range(TOPK):
                    nc.vector.tensor_scalar(EW2[:, j, :, :], EW2[:, j, :, :], r1[:, 8 + j:9 + j], None, ALU.mult).then_inc(ew_ready, 1)

                for k in range(KC):
                    for q in range(2):
                        step(nc.vector.tensor_tensor(MSB[:, :, :].rearrange("p a b -> p (a b)"), WZ[:, k, 0:D], aB[:, q, :], ALU.mult))
                        step(nc.vector.tensor_reduce(WZ[:, k, D + q * GH:D + (q + 1) * GH],
                                                     MSB[:, :, :].rearrange("p a (c o) -> p (a c) o", o=GO), AX.X, ALU.add))

                dve.wait_ge(t1_turned, T)

                def after_moe(t, s, m, warm):
                    V = HS[:, s, :]
                    dve.wait_ge(moe_ready, t + 1)
                    if warm:
                        dve.wait_ge(x2_ready, t - 1)
                    nc.vector.scalar_tensor_tensor(HS[:, s:s + 1, :], XH[:, ds(t, 1), :], RS[:, ds(t, 1)],
                                                   PB[4 + m][:, 0:D].rearrange("p (a d) -> p a d", a=1), ALU.mult, ALU.add).then_inc(moe_kept, 1)
                    dve.wait_ge(moe_kept, t + 1)
                    b = step.at + 3 * t
                    nc.vector.scalar_tensor_tensor(V, B2M[:, :], nmr[:, ds(t, 1)], V, ALU.add, ALU.add).then_inc(dve_step, 1)
                    dve.wait_ge(dve_step, b + 1)
                    nc.vector.bn_stats(vst[:, s, :], V).then_inc(dve_step, 1)
                    wait_apart(dve, dve_step, b + 2, dve_turn)
                    nc.vector.bn_aggr(vmv[:, s, :], vst[:, s, :]).then_inc(dve_step, 1)
                    dve.wait_ge(dve_step, b + 3)
                    nc.vector.tensor_scalar_add(vrs[:, s:s + 1], vmv[:, s, 1:2], EPS).then_inc(var_ready, 1)
                    dve.wait_ge(rs_ready, t + 1)
                    nc.vector.tensor_scalar(V, V, vmv[:, s, 0:1], vrs[:, s:s + 1], ALU.subtract, ALU.mult).then_inc(v_ready, 1)

                def chunk_after(c, s, warm):
                    for m in range(4):
                        after_moe(c * 4 + m, m % 2, m, warm or (isinstance(c, int) and c > 0) or m >= 2)
                over_pairs(dve, CHUNKS // 2, 0, chunk_after)
                after_moe(T - 1, 0, 0, True)
                step.at += 3 * T
                dve.wait_ge(x2_ready, T)

                over_pairs(dve, (T - 1) // 2, 1, stats)
                step.at += T
                dve.wait_ge(dve_step, step.at)
                row_stats()
                dve.wait_ge(sqrt_ready, 3)
                step(nc.vector.reciprocal(RS[:, :], RS[:, :]))

                def norm2(t, s, warm):
                    if warm:
                        dve.wait_ge(t2_turned, t - 1)
                    nc.vector.tensor_scalar(HS[:, s:s + 1, :], XH[:, ds(t, 1), :], MV[:, ds(t, 1), 0], RS[:, ds(t, 1)],
                                            ALU.subtract, ALU.mult).then_inc(t2_ready, 1)
                over_pairs(dve, (T - 1) // 2, 1, norm2)

            if STAGE >= 3:
                dve.wait_ge(z_kept, 2 * T)
                step(nc.vector.tensor_reduce(gm[:, :], EM[:, 0:T - 1, 0:GH].rearrange("p t h -> p h t"), AX.X, ALU.max))
                nc.vector.tensor_tensor(gm[0:LAST, :], gm[0:LAST, :], EM[0:LAST, T - 1, 0:GH], ALU.max).then_inc(gm_step, 1)
                dve.wait_ge(gm_turned, 1)
                step(nc.vector.tensor_reduce(gm4[:, 0:1], PB[4][0:GH, 0:P], AX.X, ALU.max))
                nc.vector.tensor_scalar(gm4[:, 1:1 + GH], ident[0:GH, 0:GH], gm4[:, 0:1], None, ALU.mult).then_inc(gm_step, 1)
                dve.wait_ge(gm_spread, 1)
                step(nc.vector.tensor_copy(gm[:, :], PB[4][:, 0:GH]))
                nc.vector.tensor_copy(EM[:, :, 0:GH], gm[:, :].rearrange("p (a h) -> p a h", a=1).broadcast_to((P, T, GH))).then_inc(em_ready, 1)

                def turned_onehot(gi, half, g):
                    sl = g % 2
                    if not isinstance(gi, int) or gi >= 2:
                        dve.wait_ge(edm_ready, gi - 1)
                    nc.vector.tensor_scalar(ST[:, sl, :], ROWB[:, half, g, :], iotap[:, 0:1], None, ALU.is_equal).then_inc(st_ready, 1)
                dve.wait_ge(rowb_in[0], 16)
                for g in range(HALF):
                    turned_onehot(g, 0, g)
                dve.wait_ge(h2_zero, 1)

                def add_sum(gi, sl, tk):
                    dve.wait_ge(sum_ready, gi + 1)
                    if not isinstance(gi, int) or gi >= 1:
                        dve.wait_ge(sum_added, gi)
                    y = A[:, ds(tk * ROW, ROW)]
                    nc.vector.tensor_tensor(y, y, PB[sl][:, 0:ROW], ALU.add).then_inc(sum_added, 1)

                def attend(n, half, warm):
                    if warm:
                        _, tks = nc.values_load_multi_w_load_instructions(TK[0:1, ds(n * HALF - 1, HALF)], [mybir.EngineType.DVE], min_val=0, max_val=T - 1)
                    else:
                        lo = max(n * HALF - 1, 0)
                        _, tks = nc.values_load_multi_w_load_instructions(TK[0:1, lo:lo + HALF], [mybir.EngineType.DVE], min_val=0, max_val=T - 1)
                        if n == 0:
                            tks = (None, *tks[0:HALF - 1])
                    per = 7
                    b0 = n * per
                    k = [0]

                    def small(ins):
                        ins.then_inc(small_step, 1)
                        k[0] += 1
                        dve.wait_ge(small_step, b0 + k[0])
                    dve.wait_ge(edm_ready, HALF * (n + 1))
                    small(nc.vector.tensor_copy(scn[:, :, :], PB[2 + half][:, 0:NS * 2 * GH].rearrange("p (s v) -> p s v", s=NS)))
                    dve.sem_inc(edm_used, 1)
                    dve.wait_ge(rows2_in[half], 16 * NS * (n // 2 + 1) if isinstance(n, int) else n * (8 * NS) + (16 * NS - half * 8 * NS))
                    v = [sc[:, i, :].rearrange("p (s h) -> p s h", h=GH) for i in range(4)]
                    small(nc.vector.tensor_tensor(v[1], scn[:, :, 0:GH], scn[:, :, GH:2 * GH], ALU.add))
                    small(nc.vector.tensor_tensor(v[0], GR[:, half * NS:(half + 1) * NS, D:ROW], scn[:, :, GH:2 * GH], ALU.add))
                    small(nc.vector.scalar_tensor_tensor(sc[:, 2, :], sc[:, 1, :], 0.01, sc[:, 1, :], ALU.mult, ALU.max))
                    small(nc.vector.scalar_tensor_tensor(sc[:, 3, :], sc[:, 0, :], 0.01, sc[:, 0, :], ALU.mult, ALU.max))
                    small(nc.vector.tensor_tensor(sc[:, 1, :], sc[:, 3, :], sc[:, 2, :], ALU.subtract))
                    if warm or n > 0:
                        dve.wait_ge(expo_out, n)
                    small(nc.vector.tensor_scalar_min(sc[:, 0, :], sc[:, 1, :], 0.0))
                    dve.sem_inc(expo_in, 1)
                    dve.wait_ge(rowb_in[1 - half], (16 * ((n + 1) // 2 + 1)) if isinstance(n, int) else (n + 1) * 8 + (16 - (1 - half) * 8))
                    for g in range(HALF):
                        gi = n * HALF + g
                        sl = g % 2
                        if warm or n > 0 or g >= 2:
                            dve.wait_ge(sum_ready, gi - 1)
                        for b in range(SUB):
                            c = g * SUB + b
                            nc.vector.tensor_scalar(S[:, sl, b, :], iota[:, :], DLS[:, half, c:c + 1], None, ALU.is_equal).then_inc(onehot2_ready, 1)
                        if g == 0:
                            dve.wait_ge(expo_out, n + 1)
                        r0 = half * NS + g * SUB
                        nc.vector.tensor_tensor(US[:, r0:r0 + SUB, 0:D].rearrange("p s (h o) -> p s h o", h=GH),
                                                GR[:, r0:r0 + SUB, 0:D].rearrange("p s (h o) -> p s h o", h=GH),
                                                US[:, r0:r0 + SUB, D:ROW].rearrange("p s (h a) -> p s h a", a=1).broadcast_to((P, SUB, GH, GO)),
                                                ALU.mult).then_inc(us_ready, 1)
                        turned_onehot(gi + HALF, 1 - half, g)
                        if warm or n > 0 or g >= 1:
                            add_sum(gi - 1, (g - 1) % 2, tks[g])
                over_pairs(dve, BODIES // 2, 0, attend)
                _, v = nc.values_load_multi_w_load_instructions(TK[0:1, GROUPS - 1:GROUPS], [mybir.EngineType.DVE], min_val=0, max_val=T - 1)
                add_sum(GROUPS - 1, (GROUPS - 1) % 2, v[0])
                dve.wait_ge(sum_added, GROUPS)

                step(nc.vector.tensor_scalar_max(RD[:, :, :], H2[:, :, D:ROW], 1e-30))
                step(nc.vector.reciprocal(RD[:, :, :], RD[:, :, :]))

                def residual3(t, s, warm):
                    hv = HS[:, s, :].rearrange("p (a h o) -> p a h o", a=1, h=GH)
                    if warm:
                        dve.wait_ge(x3_ready, t - 1)
                    else:
                        dve.wait_ge(t2_turned, T)
                    nc.vector.tensor_tensor(hv, H2[:, ds(t, 1), 0:D].rearrange("p t (h o) -> p t h o", h=GH),
                                            RD[:, ds(t, 1), :].rearrange("p t (h a) -> p t h a", a=1).broadcast_to((P, 1, GH, GO)),
                                            ALU.mult).then_inc(dve_step, 1)
                    dve.wait_ge(dve_step, step.at + t * 2 + 1)
                    nc.vector.tensor_tensor(XH[:, ds(t, 1), :], XH[:, ds(t, 1), :], HS[:, s:s + 1, :], ALU.add).then_inc(x3_ready, 1)
                    dve.wait_ge(x3_ready, t + 1)
                    nc.vector.bn_stats(BS[:, ds(t, 1), :], XH[:, ds(t, 1), :]).then_inc(dve_step, 1)
                over_pairs(dve, (T - 1) // 2, 1, residual3)
                step.at += 2 * T
                dve.wait_ge(dve_step, step.at)

            if STAGE >= 4:
                dve.wait_ge(par2_in, 16 * 16)
                step(nc.vector.tensor_scalar(it[:, :], it[:, :], 0.1, 5.0, ALU.max, ALU.min))
                step(nc.vector.reciprocal(it[:, :], it[:, :]))
                dve.wait_ge(sum_ready, GROUPS)
                for q in range(PAIRS):
                    step(nc.vector.tensor_scalar(bxB[:, q, :], ones[:, :], bxc[:, q:q + 1], None, ALU.mult))
                dve.sem_inc(slp_turn, 1)
                dve.wait_ge(wsl_psum, 1)
                itb = it[:, :].rearrange("p (h a) -> p h a", a=1).broadcast_to((P, SH, SG))
                for k in range(KC):
                    step(nc.vector.tensor_tensor(WSL[:, k, :].rearrange("p (h g) -> p h g", h=SH), PB[4 + k][:, :].rearrange("p (h g) -> p h g", h=SH), itb, ALU.mult))
                bv = BSL.rearrange("p (h g) -> p h g", h=SH)
                step(nc.vector.tensor_tensor(bv, PB[6][:, :].rearrange("p (h g) -> p h g", h=SH), bsB.rearrange("p (a g) -> p a g", a=1).broadcast_to((P, SH, SG)), ALU.add))
                step(nc.vector.tensor_tensor(bv, bv, itb, ALU.mult))
                dve.sem_inc(wsl_ready, 1)
                row_stats()
                dve.wait_ge(sqrt_ready, 4)
                step(nc.vector.reciprocal(RS[:, :], RS[:, :]))

                def norm3(t, s):
                    nc.vector.tensor_scalar(HS[:, s:s + 1, :], XH[:, ds(t, 1), :], MV[:, ds(t, 1), 0], RS[:, ds(t, 1)],
                                            ALU.subtract, ALU.mult).then_inc(t3_ready, 1)
                norm3(0, 0)

                def logits(t, s, warm):
                    first = isinstance(t, int) and t == 0
                    if warm:
                        dve.wait_ge(sw_turned, t - 1)
                        dve.wait_ge(sw_summed, t)
                    dve.wait_ge(l_ready, t + 1)
                    nc.vector.tensor_tensor(SWS[:, s, :], PB[2 + s][:, :], BSL, ALU.add).then_inc(l_kept, 1)
                    dve.wait_ge(l_kept, t + 1)
                    nc.vector.tensor_reduce(ax[:, s, :], SWS[:, s, :].rearrange("p (h g) -> p h g", h=SH), AX.X, ALU.max).then_inc(l_max, 1)
                    if not first:
                        weights(t - 1, 1 - s)
                    if not (isinstance(t, int) and t == T - 1):
                        if warm or not first:
                            dve.wait_ge(sw_turned, t)
                        norm3(t + 1, 1 - s)

                def weights(t, s):
                    dve.wait_ge(l_exp, t + 1)
                    b = step.at + 2 * t
                    lv = SWS[:, s, :].rearrange("p (h g) -> p h g", h=SH)
                    nc.vector.tensor_reduce(ax[:, 2 + s, :], lv, AX.X, ALU.add).then_inc(dve_step, 1)
                    dve.wait_ge(dve_step, b + 1)
                    nc.vector.reciprocal(ax[:, 2 + s, :], ax[:, 2 + s, :]).then_inc(dve_step, 1)
                    dve.wait_ge(dve_step, b + 2)
                    nc.vector.tensor_tensor(lv, lv, ax[:, 2 + s, :].rearrange("p (h a) -> p h a", a=1).broadcast_to((P, SH, SG)), ALU.mult).then_inc(sw_ready, 1)
                over_pairs(dve, (T - 1) // 2, 1, logits)
                weights(T - 1, 0)
                step.at += 2 * T

                dve.wait_ge(tok_pe, 1)
                for k in range(KC):
                    step(nc.vector.tensor_copy(XS[:, k, :], PB[6 + k][:, :]))
                step(nc.vector.tensor_scalar_add(sden[:, :], PB[0][:, 0:PAIRS], 1e-5))
                step(nc.vector.reciprocal(sden[:, :], sden[:, :]))
                step(nc.vector.tensor_copy(nrow, PB[1][0:1, :]))
                dve.sem_inc(tok_dve, 1)

                def q3(ap):
                    return ap.rearrange("p (q n) -> p q n", q=PAIRS)

                def each(m):
                    return m.rearrange("p (a n) -> p a n", a=1).broadcast_to((P, PAIRS, P))

                def per(c):
                    return c.rearrange("p (q a) -> p q a", a=1).broadcast_to((P, PAIRS, P))
                dve.wait_ge(tok_pe, 2)
                step(nc.vector.tensor_tensor(STK, q3(PB[2][:, :]), per(sden[:, :]), ALU.mult))
                step(nc.vector.tensor_tensor(STK, STK, each(bm[:, 0, :]), ALU.mult))
                dve.sem_inc(tok_dve, 1)
                dve.wait_ge(tok_pe, 3)
                step(nc.vector.tensor_copy(STT, q3(PB[3][:, :])))
                dve.sem_inc(tok_dve, 1)
                dve.wait_ge(tok_pe, 4)
                step(nc.vector.tensor_copy(QT, q3(PB[4][:, :])))
                step(nc.vector.tensor_copy(KT, q3(PB[5][:, :])))
                step(nc.vector.tensor_copy(VS, q3(PB[6][:, :])))
                dve.sem_inc(tok_dve, 1)
                dve.wait_ge(tok_pe, 5)
                step(nc.vector.scalar_tensor_tensor(AT, q3(PB[7][:, :]), float(64 ** -0.5), each(bm[:, 1, :]), ALU.mult, ALU.add))
                step(nc.vector.tensor_reduce(sden[:, :], AT, AX.X, ALU.max))
                step(nc.vector.tensor_tensor(AT, AT, per(sden[:, :]), ALU.subtract))
                dve.sem_inc(tok_dve, 1)
                dve.wait_ge(tok_exp, 1)
                step(nc.vector.tensor_reduce(sden[:, :], AT, AX.X, ALU.add))
                step(nc.vector.reciprocal(sden[:, :], sden[:, :]))
                step(nc.vector.tensor_tensor(AT, AT, per(sden[:, :]), ALU.mult))
                dve.sem_inc(tok_dve, 1)
                dve.wait_ge(tok_pe, 6)
                step(nc.vector.tensor_copy(ATT, q3(PB[0][:, :])))
                dve.sem_inc(tok_dve, 1)
                dve.wait_ge(tok_pe, 7)
                step(nc.vector.tensor_copy(OST, q3(PB[1][:, :])))
                dve.sem_inc(tok_dve, 1)
                dve.wait_ge(tok_pe, 8)
                for i in range(2):
                    step(nc.vector.tensor_copy(VV[:, 2 * i:2 * i + 2, :], PB[2 + i][:, :].rearrange("p (q d) -> p q d", q=2)))
                dve.sem_inc(tok_dve, 1)

                def finish(t, s, warm):
                    dve.wait_ge(mix_ready, t + 1)
                    nc.vector.tensor_tensor(XH[:, ds(t, 1), :], XH[:, ds(t, 1), :], PB[4 + s][:, 0:D].rearrange("p (a d) -> p a d", a=1), ALU.add).then_inc(dve_step, 1)
                    dve.wait_ge(dve_step, step.at + t + 1)
                    nc.vector.tensor_tensor(XH[:, ds(t, 1), :], XH[:, ds(t, 1), :], boutB[:, :].rearrange("p (a d) -> p a d", a=1), ALU.add).then_inc(fin_ready, 1)
                over_pairs(dve, (T - 1) // 2, 1, finish)

        @block.scalar
        def _(act):
            for j in range(GC):
                act.wait_ge(tab_turned, j + 1)
                bank = 5 + (j % 2)
                dstc = (DLT, SRCT, WT)
                for a in range(3):
                    pb = PB[bank] if a < 2 else PB[7]
                    o0 = (a % 2) * 256 if a < 2 else (j % 2) * 256
                    nc.scalar.copy(dstc[a][:, j * BLK:(j + 1) * BLK].rearrange("p (k b) -> p b k", b=SUB),
                                   pb[:, o0:o0 + 256].rearrange("p (b k) -> p b k", b=SUB)).then_inc(tab_kept, 1)
            act.wait_ge(veps_ready, 1)
            nc.scalar.sqrt(RS[:, :], RS[:, :]).then_inc(sqrt_ready, 1)
            act.wait_ge(par_in, 16 * NPAR)

            def keep_h(t, s, warm):
                wait_apart(act, h_turned, t + 1, act_turn)
                nc.scalar.mul(YD[:, ds(t, 1), 0:2, :], PB[s][:, 0:D].rearrange("p (a c n) -> p a c n", a=1, c=2), bnp[:, 4, 0:1]).then_inc(h_kept, 1)
            over_pairs(act, (T - 1) // 2, 1, keep_h)

            act.wait_ge(tab_kept, 3 * GC)

            def columns(n, half, warm):
                if warm:
                    wait_apart(act, rows_used, n - 1, act_turn)
                c = ds(n * NS, NS)
                nc.scalar.activation(DLS[:, half, :], DLT[:, c], ACT.Copy).then_inc(act_step, 1)
                nc.scalar.activation(WS[:, half, :], WT[:, c], ACT.Copy).then_inc(act_step, 1)
                nc.scalar.activation(IDX[:, half, :], SRCT[:, c], ACT.Copy).then_inc(act_step, 1)
                act.wait_ge(act_step, (n + 1) * 3)
                act.sem_inc(idx_ready, 1)
            over_pairs(act, BODIES // 2, 0, columns)

            act.wait_ge(degmax, 1)
            nc.scalar.sqrt(YD[:, :, 2, :], YD[:, :, 2, :]).then_inc(degsqrt, 1)

            def keep_lin(q, base):
                def f(c, s, warm, n=512):
                    for k in range(KC):
                        act.wait_ge(lin_stat, base + KC * c + k + 1)
                        wait_apart(act, lin_ready, base + KC * c + KC, act_turn)
                        if n == 512:
                            o = YD[:, ds(c * 4, 4), k, :]
                            i = PB[2 * s + k][:, :].rearrange("p (t n) -> p t n", n=P)
                        else:
                            o, i = YD[:, T - 1, k, 0:n], PB[2 * s + k][:, 0:n]
                        nc.scalar.activation(o, i, ACT.Copy).then_inc(lin_kept, 1)
                return f
            for q in range(2):
                base = q * KC * (CHUNKS + 1)
                if q == 1:
                    act.wait_ge(bn_ready, 1)
                    act.wait_ge(lin_kept, KC * (CHUNKS + 1))

                    def relu(c, n=512):
                        for k in range(KC):
                            y = YD[:, ds(c * 4, 4), k, :] if n == 512 else YD[:, T - 1, k, 0:n]
                            nc.scalar.activation(y, y, ACT.Relu, bias=bns[:, 3, k:k + 1], scale=bns[:, 1, k:k + 1]).then_inc(relu_ready, 1)
                    kl = keep_lin(q, base)
                    relu(0)

                    def both(c, s, warm):
                        if isinstance(c, int) and c + 1 >= CHUNKS:
                            relu(c + 1, LAST)
                        else:
                            relu(c + 1)
                        kl(c, s, warm)
                    over_pairs(act, CHUNKS // 2 - 1, 2, both)
                    kl(CHUNKS, 0, True, LAST)
                else:
                    kl = keep_lin(q, base)
                    over_pairs(act, CHUNKS // 2, 0, kl)
                    kl(CHUNKS, 0, True, LAST)
                act.wait_ge(bn_var, q + 1)
                nc.scalar.sqrt(bns[:, 0, :], bns[:, 0, :]).then_inc(bn_sqrt, 1)
            act.wait_ge(h_added, T)
            act.wait_ge(h_stored[0], 16 * (T // 2 + 1))
            act.wait_ge(h_stored[1], 16 * (T // 2))
            act.wait_ge(bn_ready, 2)
            act.wait_ge(lin_kept, 2 * KC * (CHUNKS + 1))

            def relu2(t, s, warm):
                if warm:
                    wait_apart(act, r_turned, t - 1, act_turn)
                for k in range(KC):
                    nc.scalar.activation(HS[:, s:s + 1, k * P:(k + 1) * P], YD[:, ds(t, 1), k, :], ACT.Relu,
                                         bias=bns[:, 3, k:k + 1], scale=bns[:, 1, k:k + 1]).then_inc(r_ready, 1)
            over_pairs(act, (T - 1) // 2, 1, relu2)

            if STAGE >= 2:
                act.wait_ge(veps_ready, 2)
                nc.scalar.sqrt(RS[:, :], RS[:, :]).then_inc(sqrt_ready, 1)
                act.wait_ge(r_turned, T)

                def keep_t1(t, s, warm):
                    wait_apart(act, t1_turned, t + 1, act_turn)
                    nc.scalar.activation(T1T[:, :, ds(t * P, P)], PB[s][:, 0:D].rearrange("p (k n) -> p k n", k=KC), ACT.Copy).then_inc(t1_kept, 1)
                over_pairs(act, (T - 1) // 2, 1, keep_t1)
                for i in range(2):
                    act.wait_ge(exp_in, i + 1)
                    nc.scalar.activation(rt[:, 2, :], rt[:, 1, :], ACT.Exp).then_inc(exp_out, 1)
                act.wait_ge(exp_in, 3)
                nc.scalar.activation(r1[:, 7:8], r1[:, 6:7], ACT.Exp).then_inc(exp_out, 1)
                act.wait_ge(b_kept, 1)

                def gelu(c, s, warm, n=512):
                    for j in range(TOPK):
                        if warm or s == 1:
                            act.wait_ge(hid_used, TOPK * (c - 1) + j + 1)
                        for q in range(FQ):
                            act.wait_ge(s1_ready, (TOPK * c + j) * FQ + q + 1)
                            nc.scalar.activation(HID[:, j, q, 0:n], PB[q][:, 0:n], ACT.Gelu, bias=b1c[:, j * FQ + q:j * FQ + q + 1]).then_inc(gelu_ready, 1)
                over_pairs(act, CHUNKS // 2, 0, gelu)
                gelu(CHUNKS, 0, True, P)
                act.wait_ge(veps_ready, 3)
                nc.scalar.sqrt(RS[:, :], RS[:, :]).then_inc(sqrt_ready, 1)

                def keep_z(t, s, warm):
                    act.wait_ge(t2_turned, t + 1)
                    if warm:
                        act.wait_ge(z_ready, t - 1)
                    nc.scalar.activation(TT[:, s, :, :], PB[s][:, 0:D].rearrange("p (k n) -> p k n", k=KC), ACT.Copy).then_inc(t2_kept, 1)
                    act.wait_ge(z_ready, t + 1)
                    if warm:
                        wait_apart(act, z_stored[s], (t // 2) * 16 if isinstance(t, int) else t * 8 - 8 * s, act_turn)
                    nc.scalar.activation(zS[:, s, :], PB[2 + s][:, 0:D + 2 * GH], ACT.Copy).then_inc(z_kept, 1)
                    nc.scalar.activation(EM[:, ds(t, 1), :], PB[2 + s][:, D:D + 2 * GH].rearrange("p (a b) -> p a b", a=1), ACT.Copy).then_inc(z_kept, 1)
                over_pairs(act, (T - 1) // 2, 1, keep_z)

            if STAGE >= 3:
                act.wait_ge(z_kept, 2 * T)

                def columns2(n, half):
                    if not isinstance(n, int) or n >= 2:
                        act.wait_ge(onehot2_ready, NS * (n - 1))
                        wait_apart(act, us_ready, HALF * (n - 1), act_turn)
                    c = ds(n * NS, NS)
                    nc.scalar.activation(DLS[:, half, :], DLT[:, c], ACT.Copy).then_inc(act_step, 1)
                    nc.scalar.activation(IDX[:, half, :], SRCT[:, c], ACT.Copy).then_inc(act_step, 1)
                    act.wait_ge(act_step, BODIES * 3 + 2 * n + 2)
                    act.sem_inc(idx2_ready, 1)
                columns2(0, 0)
                columns2(1, 1)

                def expo(n, half, warm):
                    act.wait_ge(expo_in, n + 1)
                    if warm:
                        act.wait_ge(sum_ready, HALF * (n - 1))
                    nc.scalar.activation(US[:, half * NS:(half + 1) * NS, D:ROW], sc[:, 0, :].rearrange("p (s h) -> p s h", h=GH), ACT.Exp).then_inc(expo_out, 1)
                    if not (isinstance(n, int) and n + 2 >= BODIES):
                        columns2(n + 2, half)
                over_pairs(act, BODIES // 2 - 1, 2, expo)

            if STAGE >= 4:
                act.wait_ge(veps_ready, 4)
                nc.scalar.sqrt(RS[:, :], RS[:, :]).then_inc(sqrt_ready, 1)

                def slice_copies(t, s, warm):
                    act.wait_ge(t3_turned, t + 1)
                    if warm:
                        act.wait_ge(l_ready, t - 1)
                    nc.scalar.activation(TT[:, s, :, :], PB[s][:, 0:D].rearrange("p (k n) -> p k n", k=KC), ACT.Copy).then_inc(t3_kept, 1)
                    act.wait_ge(l_less, t + 1)
                    nc.scalar.activation(SWS[:, s, :], SWS[:, s, :], ACT.Exp).then_inc(l_exp, 1)
                    if not (isinstance(t, int) and t == 0):
                        keep_sw(t - 1, 1 - s)

                def keep_sw(t, s):
                    wait_apart(act, sw_turned, t + 1, act_turn)
                    nc.scalar.activation(SWT[:, ds(t, 1), :, :].rearrange("p a q n -> p a (q n)"), PB[4 + s][:, :].rearrange("p (a n) -> p a n", a=1), ACT.Copy).then_inc(sw_kept, 1)
                over_pairs(act, (T - 1) // 2, 1, slice_copies)
                keep_sw(T - 1, 0)
                act.wait_ge(tok_dve, 5)
                nc.scalar.activation(AT, AT, ACT.Exp).then_inc(tok_exp, 1)
                act.wait_ge(tok_dve, 9)
                act.wait_ge(sw_kept, T)

                def stage_sw(t, s, warm):
                    if warm:
                        wait_apart(act, mix_ready, t - 1, act_turn)
                    nc.scalar.activation(SWS[:, s:s + 1, :], SWT[:, ds(t, 1), :, :].rearrange("p a q n -> p a (q n)"), ACT.Copy).then_inc(swt_staged, 1)
                over_pairs(act, (T - 1) // 2, 1, stage_sw)

        @block.tensor
        def _(pe):
            pe.wait_ge(consts_ready, 1)
            pe.wait_ge(lastf_ready, 1)
            h = NBP // 2
            for i in range(2):
                last = nc.tensor.matmul(PB[i][:, 0:h], ones[0:1, :], lastF[0:1, i * h:(i + 1) * h], start=True, stop=True)
            last.then_inc(lastrow_ready, 1)
            pe.wait_ge(tcmp_ready, 1)
            hk = GC * P // 2
            for i in range(2):
                nc.tensor.matmul(PB[2 + i][:, 0:hk], ones[0:T - 1, :], tcmp[:, i * hk:(i + 1) * hk], start=True, stop=True)
            for j in range(GC):
                last = nc.tensor.matmul(PB[4][:, j:j + 1], tcmp[:, j * P:(j + 1) * P], ones[0:T - 1, 0:1], start=True, stop=True)
            last.then_inc(tk_psum, 1)
            for j in range(GC):
                pe.wait_ge(tabf_ready, j + 1)
                if j >= 2:
                    pe.wait_ge(tab_kept, 3 * (j - 1))
                for a in range(3):
                    pb = PB[5 + (j % 2)] if a < 2 else PB[7]
                    o0 = (a % 2) * 256 if a < 2 else (j % 2) * 256
                    if a == 2 and j >= 1:
                        pe.wait_ge(tab_kept, 3 * j)
                    for b in range(SUB):
                        last = nc.tensor.transpose(pb[:, o0 + b * P:o0 + (b + 1) * P], tf[:, j % 2, a, b * P:(b + 1) * P], ident[:, :])
                last.then_inc(tab_turned, 1)

            def turn(src_t, ready, per, kept, turned):
                def f(t, s, warm):
                    pe.wait_ge(ready, (t + 1) * per)
                    if warm:
                        pe.wait_ge(kept, t - 1)
                    for k in range(KC):
                        last = nc.tensor.transpose(PB[s][:, k * P:(k + 1) * P], src_t[:, s, k * P:(k + 1) * P], ident[:, :])
                    last.then_inc(turned, 1)
                return f
            over_pairs(pe, (T - 1) // 2, 1, turn(HS, h_ready, 1, h_kept, h_turned))
            pe.wait_ge(h_kept, T)

            def edge_sum(n, half, warm):
                pe.wait_ge(rows_in[half], (n // 2 + 1) * NS * 16 if isinstance(n, int) else n * (NS * 8) + (NS * 16 - half * NS * 8))
                for g in range(HALF):
                    gi = n * HALF + g
                    sl = g % 2
                    pe.wait_ge(onehot_ready, (gi + 1) * 2 * SUB)
                    if warm or n > 0 or g >= 2:
                        pe.wait_ge(part_added, gi - 1)
                    for k in range(KC):
                        for b in range(SUB):
                            nc.tensor.matmul(PB[sl][:, k * P:(k + 1) * P], GR[:, half * NS + g * SUB + b, k * P:(k + 1) * P],
                                             S[:, sl, b, :], start=(b == 0), stop=(b == SUB - 1))
                    for b in range(SUB):
                        last = nc.tensor.matmul(PB[sl][:, 256:384], onesb[:, :], S1[:, sl, b, :], start=(b == 0), stop=(b == SUB - 1))
                    last.then_inc(part_ready, 1)
                pe.wait_ge(part_ready, (n + 1) * HALF)
                pe.sem_inc(rows_used, 1)
            over_pairs(pe, BODIES // 2, 0, edge_sum)
            pe.wait_ge(part_added, GROUPS)

            pe.wait_ge(par_in, 16 * NPAR)
            for q in range(2):
                base = q * KC * (CHUNKS + 1)

                def lin(c, s, warm, n=512):
                    if q:
                        pe.wait_ge(relu_ready, KC * (c + 1))
                    for f in range(KC):
                        if warm:
                            pe.wait_ge(lin_kept, base + KC * (c - 2) + f + 1)
                            pe.wait_ge(lin_stat, base + KC * (c - 2) + f + 1)
                        for k in range(KC):
                            if n == 512:
                                r = YD[:, ds(c * 4, 4), k, :]
                                o = PB[2 * s + f][:, :].rearrange("p (t n) -> p t n", n=P)
                            else:
                                r, o = YD[:, T - 1, k, 0:n], PB[2 * s + f][:, 0:n]
                            last = nc.tensor.matmul(o, w12[:, q, k, f * P:(f + 1) * P], r, start=(k == 0), stop=(k == KC - 1))
                        last.then_inc(lin_ready, 1)
                if q:
                    pe.wait_ge(lin_kept, base)
                over_pairs(pe, CHUNKS // 2, 0, lin)
                lin(CHUNKS, 0, True, LAST)
            pe.wait_ge(lin_kept, 2 * KC * (CHUNKS + 1))
            over_pairs(pe, (T - 1) // 2, 1, turn(HS, r_ready, 2, x1_ready, r_turned))

            if STAGE >= 2:
                pe.wait_ge(x1_ready, T)
                def turn_sum(t, s, warm):
                    pe.wait_ge(t1_ready, t + 1)
                    if warm:
                        pe.wait_ge(t1_kept, t - 1)
                    for k in range(KC):
                        nc.tensor.transpose(PB[s][:, k * P:(k + 1) * P], HS[:, s, k * P:(k + 1) * P], ident[:, :])
                    end = isinstance(t, int) and t == T - 1
                    for k in range(KC):
                        last = nc.tensor.matmul(PB[2 + k][:, 0:1], HS[:, s, k * P:(k + 1) * P], valid[:, 1:2] if end else valid[:, 0:1],
                                                start=(isinstance(t, int) and t == 0), stop=end)
                    last.then_inc(t1_turned, 1)
                over_pairs(pe, (T - 1) // 2, 1, turn_sum)
                pe.wait_ge(t1_turned, T)
                pe.sem_inc(sums_ready, 1)
                pe.wait_ge(msb_ready, KC)
                for k in range(KC):
                    last = nc.tensor.matmul(PB[4][:, 0:NX], MSB[:, k, :], wr[:, k, :], start=(k == 0), stop=(k == KC - 1))
                last.then_inc(logits_ready, 1)
                pe.wait_ge(chosen, 2)
                for j in range(3):
                    last = nc.tensor.transpose(PB[6][0:NX, j * P:(j + 1) * P], ohs[:, j, :], ident[:, :])
                last.then_inc(ohs_turned, 1)
                pe.wait_ge(ohT_ready, 1)
                for j in range(TOPK):
                    for q in range(FQ):
                        nc.tensor.matmul(PB[5][:, j * FQ + q:j * FQ + q + 1], b1s[:, q * P:(q + 1) * P], ohT[:, j, 0:1], start=True, stop=True)
                nc.tensor.matmul(PB[7][:, 0:D], ohT[:, 2, :], b2s[:, :], start=True, stop=True).then_inc(b_picked, 1)
                pe.wait_ge(b_kept, 1)
                pe.wait_ge(ew_ready, TOPK)
                pe.wait_ge(t1_kept, T)

                def experts(c, s, warm, n=512):
                    warm = warm or s == 1
                    for j in range(TOPK):
                        for q in range(FQ):
                            if warm or j:
                                pe.wait_ge(gelu_ready, (TOPK * c + j - 1) * FQ + q + 1)
                            for k in range(KC):
                                last = nc.tensor.matmul(PB[q][:, 0:n], EW1[:, j, k, q * P:(q + 1) * P], T1T[:, k, ds(c * 512, n)],
                                                        start=(k == 0), stop=(k == KC - 1))
                            last.then_inc(s1_ready, 1)
                    for j in range(TOPK):
                        pe.wait_ge(gelu_ready, (TOPK * c + j + 1) * FQ)
                        for m in range(n // P):
                            if warm and j == 0:
                                pe.wait_ge(moe_kept, 4 * (c - 1) + m + 1)
                            for q in range(FQ):
                                last = nc.tensor.matmul(PB[4 + m][:, 0:D], HID[:, j, q, m * P:(m + 1) * P], EW2[:, j, q, :],
                                                        start=(j == 0 and q == 0), stop=(j == 1 and q == FQ - 1))
                            if j == TOPK - 1:
                                last.then_inc(moe_ready, 1)
                            elif m == n // P - 1:
                                last.then_inc(hid_used, 1)
                    pe.wait_ge(moe_ready, 4 * c + n // P)
                    pe.sem_inc(hid_used, 1)
                over_pairs(pe, CHUNKS // 2, 0, experts)
                experts(CHUNKS, 0, True, P)

                def project(t, s, warm):
                    pe.wait_ge(t2_ready, t + 1)
                    if warm:
                        pe.wait_ge(t2_kept, t - 1)
                    for k in range(KC):
                        last = nc.tensor.transpose(PB[s][:, k * P:(k + 1) * P], HS[:, s, k * P:(k + 1) * P], ident[:, :])
                    last.then_inc(t2_turned, 1)
                    pe.wait_ge(t2_kept, t + 1)
                    if warm:
                        pe.wait_ge(z_kept, 2 * (t - 1))
                    for k in range(KC):
                        last = nc.tensor.matmul(PB[2 + s][:, 0:D + 2 * GH], TT[:, s, k, :], WZ[:, k, :], start=(k == 0), stop=(k == KC - 1))
                    last.then_inc(z_ready, 1)
                pe.wait_ge(gelu_ready, TOPK * FQ * (CHUNKS + 1))
                over_pairs(pe, (T - 1) // 2, 1, project)

            if STAGE >= 3:
                pe.wait_ge(gm_step, 1)
                pe.wait_ge(z_kept, 2 * T)
                nc.tensor.transpose(PB[4][0:GH, 0:P], gm[:, :], ident[:, :]).then_inc(gm_turned, 1)
                pe.wait_ge(gm_step, 2)
                nc.tensor.matmul(PB[4][:, 0:GH], ones[0:GH, :], gm4[:, 1:1 + GH], start=True, stop=True).then_inc(gm_spread, 1)
                pe.wait_ge(em_ready, 1)

                def spread(gi, half, g, tk):
                    pe.wait_ge(st_ready, gi + 1)
                    for b in range(SUB):
                        c = g * SUB + b
                        last = nc.tensor.matmul(PB[2 + half][:, c * 2 * GH:(c + 1) * 2 * GH].rearrange("p (a v) -> p a v", a=1), ST[:, g % 2, b * P:(b + 1) * P],
                                                EM[:, ds(tk, 1), :], start=True, stop=True)
                    last.then_inc(edm_ready, 1)
                _, tks = nc.values_load_multi_w_load_instructions(TK[0:1, 0:HALF], [mybir.EngineType.PE], min_val=0, max_val=T - 1)
                for g in range(HALF):
                    spread(g, 0, g, tks[g])

                def weighted_sum(n, half, warm):
                    _, tks = nc.values_load_multi_w_load_instructions(TK[0:1, ds((n + 1) * HALF, HALF)], [mybir.EngineType.PE], min_val=0, max_val=T - 1)
                    for g in range(HALF):
                        gi = n * HALF + g
                        sl = g % 2
                        pe.wait_ge(us_ready, gi + 1)
                        pe.wait_ge(onehot2_ready, SUB * (gi + 1))
                        if warm or n > 0 or g >= 2:
                            pe.wait_ge(sum_added, gi - 1)
                        for b in range(SUB):
                            last = nc.tensor.matmul(PB[sl][:, 0:ROW], S[:, sl, b, :], US[:, half * NS + g * SUB + b, :], start=(b == 0), stop=(b == SUB - 1))
                        last.then_inc(sum_ready, 1)
                        if g == 0 and (warm or n > 0):
                            pe.wait_ge(edm_used, n)
                        spread(gi + HALF, 1 - half, g, tks[g])
                over_pairs(pe, BODIES // 2, 0, weighted_sum)

            if STAGE >= 4:
                pe.wait_ge(slp_turn, 1)
                for k in range(KC):
                    for q in range(PAIRS):
                        nc.tensor.matmul(PB[4 + k][:, q * P:(q + 1) * P], WXT[:, q, k * P:(k + 1) * P], WBD[:, 0, :], start=True, stop=True)
                for q in range(PAIRS):
                    last = nc.tensor.matmul(PB[6][:, q * P:(q + 1) * P], bxB[:, q, :], WBD[:, 0, :], start=True, stop=True)
                last.then_inc(wsl_psum, 1)
                pe.wait_ge(wsl_ready, 1)

                def slice_logits(t, s, warm):
                    pe.wait_ge(t3_ready, t + 1)
                    if warm:
                        pe.wait_ge(t3_kept, t - 1)
                    for k in range(KC):
                        last = nc.tensor.transpose(PB[s][:, k * P:(k + 1) * P], HS[:, s, k * P:(k + 1) * P], ident[:, :])
                    last.then_inc(t3_turned, 1)
                    pe.wait_ge(t3_kept, t + 1)
                    if warm:
                        pe.wait_ge(l_kept, t - 1)
                    for k in range(KC):
                        last = nc.tensor.matmul(PB[2 + s][:, :], TT[:, s, k, :], WSL[:, k, :], start=(k == 0), stop=(k == KC - 1))
                    last.then_inc(l_ready, 1)
                    if not (isinstance(t, int) and t == 0):
                        tokens(t - 1, 1 - s, warm, P)

                def tokens(t, s, warm, np_):
                    first, end = isinstance(t, int) and t == 0, np_ < P
                    pe.wait_ge(sw_ready, t + 1)
                    for k in range(KC):
                        nc.tensor.matmul(PB[6 + k][:, :], HS[0:np_, s, k * P:(k + 1) * P], SWS[0:np_, s, :], start=first, stop=end)
                    if not isinstance(t, int) or t >= 2:
                        pe.wait_ge(sw_kept, t - 1)
                    for q in range(PAIRS):
                        last = nc.tensor.transpose(PB[4 + s][:, q * P:(q + 1) * P], SWS[:, s, q * P:(q + 1) * P], ident[:, :])
                    last.then_inc(sw_turned, 1)
                over_pairs(pe, (T - 1) // 2, 1, slice_logits)
                tokens(T - 1, 0, True, LAST)

                pe.wait_ge(sw_summed, T + 1)
                pe.wait_ge(t3_kept, T)
                pe.wait_ge(l_kept, T)
                for q in range(PAIRS):
                    nc.tensor.matmul(PB[0][:, q:q + 1], SWsum[:, q * P:(q + 1) * P], ones[:, 0:1], start=True, stop=True)
                nc.tensor.matmul(PB[1][0:1, :], ones[:, 0:1], SWsum, start=True, stop=True).then_inc(tok_pe, 1)
                pe.wait_ge(tok_dve, 1)
                for q in range(PAIRS):
                    c = slice(q * P, (q + 1) * P)
                    for k in range(KC):
                        nc.tensor.matmul(PB[2][:, c], XS[:, k, c], WFX[:, k, c], start=(k == 0), stop=False)
                    last = nc.tensor.matmul(PB[2][:, c], nrow[:, c], bfx[:, c], start=False, stop=True)
                last.then_inc(tok_pe, 1)
                pe.wait_ge(tok_dve, 2)
                for q in range(PAIRS):
                    last = nc.tensor.transpose(PB[3][:, q * P:(q + 1) * P], STK[:, q, :], ident[:, :])
                last.then_inc(tok_pe, 1)
                pe.wait_ge(tok_dve, 3)
                pe.wait_ge(sw_kept, T)
                for i in range(2):
                    nc.tensor.matmul(PB[4 + i][:, :], WBD[:, 1 + i, :], STT.rearrange("p q n -> p (q n)"), start=True, stop=True)
                for q in range(PAIRS):
                    last = nc.tensor.matmul(PB[6][:, q * P:(q + 1) * P], STT[:, q, :], WBD[:, 3, :], start=True, stop=True)
                last.then_inc(tok_pe, 1)
                pe.wait_ge(tok_dve, 4)
                for q in range(PAIRS):
                    last = nc.tensor.matmul(PB[7][:, q * P:(q + 1) * P], QT[:, q, :], KT[:, q, :], start=True, stop=True)
                last.then_inc(tok_pe, 1)
                pe.wait_ge(tok_dve, 6)
                for q in range(PAIRS):
                    last = nc.tensor.transpose(PB[0][:, q * P:(q + 1) * P], AT[:, q, :], ident[:, :])
                last.then_inc(tok_pe, 1)
                pe.wait_ge(tok_dve, 7)
                for q in range(PAIRS):
                    last = nc.tensor.matmul(PB[1][:, q * P:(q + 1) * P], VS[:, q, :], ATT[:, q, :], start=True, stop=True)
                last.then_inc(tok_pe, 1)
                pe.wait_ge(tok_dve, 8)
                for q in range(PAIRS):
                    last = nc.tensor.matmul(PB[2 + q // 2][:, (q % 2) * D:(q % 2 + 1) * D], OST[:, q, :], WOUT[:, q, :], start=True, stop=True)
                last.then_inc(tok_pe, 1)
                pe.wait_ge(tok_dve, 9)

                def mix(t, s, warm):
                    pe.wait_ge(swt_staged, t + 1)
                    if warm:
                        pe.wait_ge(fin_ready, t - 1)
                    for q in range(PAIRS):
                        last = nc.tensor.matmul(PB[4 + s][:, 0:D], SWS[:, s, q * P:(q + 1) * P], VV[:, q, :], start=(q == 0), stop=(q == PAIRS - 1))
                    last.then_inc(mix_ready, 1)
                over_pairs(pe, (T - 1) // 2, 1, mix)


_INS = ["x", "src", "dst", "edge_weight", "L0_gnn_w1", "L0_gnn_w2", "L0_gnn_gamma1", "L0_gnn_beta1", "L0_gnn_eps_weight",
        "L0_gnn_gamma_h", "L0_gnn_beta_h", "L0_ffn_Wr", "L0_ffn_br", "L0_ffn_W1", "L0_ffn_b1", "L0_ffn_W2", "L0_ffn_b2",
        "L0_ffn_gamma", "L0_ffn_beta", "L1_gnn_W", "L1_gnn_a_src", "L1_gnn_a_dst", "L1_ffn_W_fx", "L1_ffn_b_fx",
        "L1_ffn_W_x", "L1_ffn_b_x", "L1_ffn_W_slice", "L1_ffn_b_slice", "L1_ffn_W_q", "L1_ffn_W_k", "L1_ffn_W_v",
        "L1_ffn_W_out", "L1_ffn_b_out", "L1_ffn_temperature"]
_TURNED = ("L0_gnn_w1", "L0_gnn_w2", "L1_ffn_W_x")
STAGE = 4


def kernel(**inputs):
    import numpy as _np
    import concourse.bacc as _bacc
    from concourse import mybir as _mybir
    from concourse.bass_utils import run_bass_kernel_spmd as _run

    nc = _bacc.Bacc("TRN2", target_bir_lowering=False, num_devices=1)
    pad = {"src": (NBP * BLK - E, 0), "dst": (NBP * BLK - E, NODST), "edge_weight": (NBP * BLK - E, 0)}
    arrays, args = {}, []
    for name in _INS:
        a = _np.asarray(inputs[name])
        if name in pad:
            a = _np.concatenate([a, _np.full((pad[name][0],), pad[name][1], a.dtype)])
        if name == "x":
            a = _np.concatenate([a, _np.zeros((T * P - N, D), a.dtype)])
        if name in _TURNED:
            a = a.T
        a = _np.ascontiguousarray(a)
        arrays[f"in_{name}_dram"] = a
        args.append(nc.dram_tensor(f"in_{name}_dram", a.shape, _mybir.dt.from_np(a.dtype), kind="ExternalInput").ap())
    args.append(nc.dram_tensor("out_0_dram", (N, D), _mybir.dt.float32, kind="ExternalOutput").ap())
    build(nc, STAGE, *args)
    r = _run(nc, [arrays], core_ids=[0])
    return r.results[0]["out_0_dram"]
```

```python
import concourse.bass as bass
from concourse import mybir
from contextlib import ExitStack

P = 128
N, D, E = 6250, 256, 200000
KC = D // P
T = -(-N // P)
LAST = N - (T - 1) * P
BLK = 256
SUB = BLK // P
HALF = 4
NB = -(-E // BLK)
GROUPS = -(-(NB + T - 1) // (2 * HALF)) * 2 * HALF
GC = -(-GROUPS // P)
NBP = NB + GROUPS - (NB + T - 1)
NODST = 1 << 20
NS = HALF * SUB
BODIES = GROUPS // HALF
IN_RANGE = "a tile's number counts T - 1 comparisons, so that it lies in 0 ... T - 1 for any edges"
LAG = 2
UG = 2
UNITS = GROUPS // UG
NU = UG * SUB
NPAR = 17
NX = 8
F1 = 512
TOPK = 2
CAP = float(-(-N * 5 // (4 * NX)))
GH, GO = 4, 64
ROW = D + GH
SH, SG = 8, 64
INNER = SH * 64
PAIRS = SH // 2
EPS = 1e-5
CHUNKS = (T - 1) // 4


def over_pairs(eng, pairs, tail, body):
    body(0, 0, False)
    body(1, 1, False)
    with eng.Fori(1, pairs) as i:
        for u in range(2):
            body(i * 2 + u, u, True)
    for t in range(2 * pairs, 2 * pairs + tail):
        body(t, t % 2, True)


def over(eng, total, unroll, body):
    for n in range(unroll):
        body(n, n, 0)
    with eng.Fori(1, total // unroll) as i:
        for j in range(unroll):
            body(i * unroll + j, j, i)
    for n in range(total // unroll * unroll, total):
        body(n, n % unroll, n // unroll)


def past(n, k):
    return not isinstance(n, int) or n >= k


def wait_apart(eng, sem, value, turn):
    eng.wait_ge(sem, value)
    eng.sem_inc(turn, 1)


class Chain:

    def __init__(self, eng, sem):
        self.eng, self.sem, self.at = eng, sem, 0

    def __call__(self, ins):
        ins.then_inc(self.sem, 1)
        self.at = self.at + 1
        self.eng.wait_ge(self.sem, self.at)


def build(nc, x, src, dst, ew, w1T, w2T, gamma1, beta1, epsw, gamma_h, beta_h,
          Wr, br, W1, b1, W2, b2, gamma, beta, gW, ga_src, ga_dst,
          W_fx, b_fx, W_xT, b_x, W_slice, b_slice, W_q, W_k, W_v, W_out, b_out, temperature, out):
    fp32, bf16, i32 = mybir.dt.float32, mybir.dt.bfloat16, mybir.dt.int32
    ALU, ACT, AX = mybir.AluOpType, mybir.ActivationFunctionType, mybir.AxisListType
    ds = bass.ds

    hTab = nc.dram_tensor("hTab", (T * P, D), fp32, kind="Internal").ap()
    zTab = nc.dram_tensor("zTab", (T * P, ROW), fp32, kind="Internal").ap()
    dlTab = nc.dram_tensor("dlTab", (GC * P, BLK), fp32, kind="Internal").ap()

    ctx = ExitStack()
    with ctx:
        ctx.enter_context(nc.allow_non_contiguous_dma("small parameters and strided rows"))

        def sb(name, shape, dt=fp32):
            return ctx.enter_context(nc.sbuf_tensor(name, shape, dt))

        def sem(name):
            return ctx.enter_context(nc.semaphore(name))

        PB = [ctx.enter_context(nc.psum_tensor(f"PB{i}", [P, 512], fp32)) for i in range(8)]

        XH = sb("XH", [P, T, D])
        ARENA = T * 512
        A = sb("A", [P, ARENA])
        YD = A[:, 0:T * 384].rearrange("p (t c n) -> p t c n", c=3, n=P)
        tab = ARENA - 3 * GC * BLK
        WT = A[:, tab:tab + GC * BLK]
        DLT = A[:, tab + GC * BLK:tab + 2 * GC * BLK]
        SRCT = A[:, tab + 2 * GC * BLK:tab + 3 * GC * BLK].bitcast(i32)
        G = sb("G", [P, 2 * NS * ROW])
        GU = G[:, 0:4 * NU * D].rearrange("p (s r) -> p s r", r=D)
        GR = G[:, :].rearrange("p (s r) -> p s r", r=ROW)
        tg = G[:, 0:2 * 3 * BLK].rearrange("p (s a e) -> p s a e", s=2, a=3)
        tf = G[:, 2 * 3 * BLK:4 * 3 * BLK].rearrange("p (s a e) -> p s a e", s=2, a=3)
        TK = sb("TK", [P, GC * P], i32)
        S = sb("S", [P, 2, SUB, P])
        STF = sb("STF", [P, 2 * BLK])
        ST = STF[:, :].bitcast(bf16).rearrange("p (s e) -> p s e", s=HALF)
        iint = STF[:, 0:P].bitcast(i32)
        EM3 = sb("EM3", [P, T, 3, 2 * GH], bf16)
        S1 = A[:, T * 384:T * 384 + SUB * P].bitcast(bf16).rearrange("p (g b n) -> p g b n", g=2, b=SUB)
        IDX = sb("IDX", [P, 3, NS], i32)
        DLS = sb("DLS", [P, 3, NS])
        WS = sb("WS", [P, 4 * NU])
        IDXU, DLU = (b[:, :, :].rearrange("p a b -> p (a b)") for b in (IDX, DLS))
        ident = sb("ident", [P, P])
        iota = sb("iota", [P, P])
        iotap = sb("iotap", [P, 1])
        ipint = sb("ipint", [P, 1], i32)
        ones = sb("ones", [P, P])
        onesb = sb("onesb", [P, P], bf16)
        valid = sb("valid", [P, 2])
        work = A[:, 0:2048]
        lastI = A[0:1, 3072:3072 + NBP].bitcast(i32)
        lastF = A[0:1, 4096:4096 + NBP]
        cmp = work[0:T - 1, 0:NBP]
        kki = work[:, 1024:1024 + GC * P].bitcast(i32)
        kk = A[:, 2048:2048 + GC * P]
        tcmp = work[0:T - 1, 0:GC * P]
        thr = sb("thr", [P, 2])
        cols = sb("cols", [P, 5, GC])
        cidx = sb("cidx", [P, GC], i32)
        kci = sb("kci", [P, GC], i32)
        BS = sb("BS", [P, T, 6])
        MV = sb("MV", [P, T, 2])
        RS = sb("RS", [P, T])
        HS = sb("HS", [P, 2, D])
        w12 = sb("w12", [P, 2, KC, D])
        bnp = sb("bnp", [P, 5, KC])
        BSF = sb("BSF", [P, KC, CHUNKS + 1, 6])
        MVF = sb("MVF", [P, KC, 2])
        bns = sb("bns", [P, 4, KC])

        T1T = A[:, 0:KC * T * P].rearrange("p (k n) -> p k n", k=KC)
        ew0 = KC * T * P
        EW1 = A[:, ew0:ew0 + TOPK * KC * F1].rearrange("p (j k f) -> p j k f", j=TOPK, k=KC)
        FQ = F1 // P
        ew1 = ew0 + TOPK * KC * F1
        EW2 = A[:, ew1:ew1 + TOPK * FQ * D].rearrange("p (j q d) -> p j q d", j=TOPK, q=FQ)
        HID = G[:, 0:TOPK * FQ * 512].rearrange("p (j q n) -> p j q n", j=TOPK, q=FQ)
        ms = sb("ms", [P, KC])
        MSB = sb("MSB", [P, KC, P])
        wr = sb("wr", [P, KC, NX])
        rt = sb("rt", [P, 16, NX])
        r1 = sb("r1", [P, 16])
        ohs = sb("ohs", [P, 3, NX])
        ohT = sb("ohT", [NX, 3, P])
        emul = sb("emul", [P, 6])
        ebase = sb("ebase", [P, 6])
        EI = sb("EI", [P, TOPK, 6], i32)
        b1s = A[0:NX, T * 384 + SUB * P:T * 384 + SUB * P + F1]
        b2s = sb("b2s", [NX, D])
        b1c = sb("b1c", [P, TOPK * FQ])
        B2M = sb("B2M", [P, D])
        rows4 = sb("rows4", [P, 4, D])
        gbB, aB = rows4[:, 0:2, :], rows4[:, 2:4, :]
        nmr = sb("nmr", [P, T])
        vst = sb("vst", [P, 2, 6])
        vmv = sb("vmv", [P, 2, 2])
        vrs = sb("vrs", [P, 2])
        mhalf = sb("mhalf", [P, 1])
        WZ = sb("WZ", [P, KC, D + 2 * GH])
        zS = sb("zS", [P, 2, D + 2 * GH])
        TT = sb("TT", [P, 2, KC, P])
        EM = sb("EM", [P, T, 2 * GH])

        H2 = A[:, 0:T * ROW].rearrange("p (t r) -> p t r", r=ROW)
        us0 = T * ROW
        US = A[:, us0:us0 + 2 * NS * ROW].rearrange("p (s r) -> p s r", r=ROW)
        rb0 = us0 + 2 * NS * ROW
        ROWB = A[:, rb0:rb0 + 2 * HALF * BLK].rearrange("p (s g e) -> p s g e", s=2, g=HALF)
        r20 = rb0 + 2 * HALF * BLK
        GR2 = A[:, r20:r20 + NS * ROW].rearrange("p (s r) -> p s r", r=ROW)
        ROWS2 = [GR[:, 0:NS, :], GR[:, NS:2 * NS, :], GR2]
        SR = [S[:, 0, :, :], S[:, 1, :, :]] + [w12[:, 0, i, :].rearrange("p (b n) -> p b n", b=SUB) for i in range(2)]
        SUMS = [PB[0], PB[1], PB[4], PB[5]]
        sc = sb("sc", [P, 4, NS * GH])
        scn = sb("scn", [P, NS, 2 * GH])
        gm = sb("gm", [P, GH])
        gm4 = sb("gm4", [GH, 1 + GH])
        RD = sb("RD", [P, T, GH])

        SWT = A[:, :].rearrange("p (t q n) -> p t q n", q=PAIRS, n=P)
        WXT = A[:, ARENA - 1024:ARENA].rearrange("p (q k) -> p q k", q=PAIRS)
        WSL = G[:, 0:1024].rearrange("p (k f) -> p k f", k=KC)
        VV = G[:, 0:1024].rearrange("p (q d) -> p q d", q=PAIRS)
        BSL = G[:, 1024:1536]
        SWS = G[:, 1536:2560].rearrange("p (s f) -> p s f", s=2)
        SWsum = G[:, 2560:3072]
        XS = G[:, 3072:4096].rearrange("p (k f) -> p k f", k=KC)
        WFX = w12[:, :, :, :].rearrange("p a k f -> p (a k f)").rearrange("p (k f) -> p k f", k=KC)
        WOUT = rows4
        WBD = sb("WBD", [P, 4, P])
        bm = sb("bm", [P, 2, P])
        it = sb("it", [P, SH])
        bxc = sb("bxc", [P, PAIRS])
        bxB = S[:, :, :, :].rearrange("p a b n -> p (a b) n")
        bsB = MSB[:, 0, 0:SG]
        boutB = B2M
        bfx = EM3[0:1, :, :, :].rearrange("p t a v -> p (t a v)").bitcast(fp32)[:, 0:INNER]
        nrow = zS[0:1, :, :].rearrange("p a b -> p (a b)")[:, 0:INNER]
        sden = sb("sden", [P, PAIRS])
        ax = sb("ax", [P, 4, SH])
        q4 = [b[:, :, :, :].rearrange("p a b n -> p (a b) n") for b in (TT, S)]
        STK = STF[:, :].rearrange("p (b n) -> p b n", n=P)
        STT = HS[:, :, :].rearrange("p a (b n) -> p (a b) n", n=P)
        QT, KT = SWS[:, 0, :].rearrange("p (q n) -> p q n", n=P), SWS[:, 1, :].rearrange("p (q n) -> p q n", n=P)
        VS, AT = XS[:, 0, :].rearrange("p (q n) -> p q n", n=P), XS[:, 1, :].rearrange("p (q n) -> p q n", n=P)
        ATT, OST = q4

        x_in = [sem(f"x_in{i}") for i in range(4)]
        par_in = sem("par_in")
        last_in = sem("last_in")
        consts_ready = sem("consts_ready")
        pool_step = sem("pool_step")
        dve_step = sem("dve_step")
        act_step = sem("act_step")
        lastf_ready = sem("lastf_ready")
        lastrow_ready = sem("lastrow_ready")
        tcmp_ready = sem("tcmp_ready")
        tk_psum = sem("tk_psum")
        cidx_ready = sem("cidx_ready")
        tab_in = [sem(f"tab_in{i}") for i in range(2)]
        tabf_ready = sem("tabf_ready")
        tab_turned = sem("tab_turned")
        tab_kept = sem("tab_kept")
        dl_stored = sem("dl_stored")
        veps_ready = sem("veps_ready")
        sqrt_ready = sem("sqrt_ready")
        h_ready = sem("h_ready")
        h_stored = [sem(f"h_stored{i}") for i in range(2)]
        h_turned = sem("h_turned")
        h_kept = sem("h_kept")
        h_added = sem("h_added")
        idx_ready = sem("idx_ready")
        rows_in = [sem(f"rows_in{i}") for i in range(4)]
        gather_turn = sem("gather_turn")
        act_turn = sem("act_turn")
        onehot_ready = sem("onehot_ready")
        part_ready = sem("part_ready")
        part_added = sem("part_added")
        lin_ready = sem("lin_ready")
        lin_stat = sem("lin_stat")
        lin_kept = sem("lin_kept")
        degmax = sem("degmax")
        degsqrt = sem("degsqrt")
        bn_var = sem("bn_var")
        bn_sqrt = sem("bn_sqrt")
        bn_ready = sem("bn_ready")
        relu_ready = sem("relu_ready")
        r_ready = sem("r_ready")
        r_turned = sem("r_turned")
        x1_ready = sem("x1_ready")
        out_stored = sem("out_stored")
        dve_turn = sem("dve_turn")
        t1_ready = sem("t1_ready")
        t1_turned = sem("t1_turned")
        t1_kept = sem("t1_kept")
        sums_ready = sem("sums_ready")
        msb_ready = sem("msb_ready")
        logits_ready = sem("logits_ready")
        exp_in = sem("exp_in")
        exp_out = sem("exp_out")
        chosen = sem("chosen")
        ohs_turned = sem("ohs_turned")
        ohT_ready = sem("ohT_ready")
        b_picked = sem("b_picked")
        b_kept = sem("b_kept")
        ew_in = sem("ew_in")
        ew_ready = sem("ew_ready")
        s1_ready = sem("s1_ready")
        gelu_ready = sem("gelu_ready")
        hid_used = sem("hid_used")
        moe_ready = sem("moe_ready")
        moe_kept = sem("moe_kept")
        var_ready = sem("var_ready")
        rs_ready = sem("rs_ready")
        v_ready = sem("v_ready")
        x2_ready = sem("x2_ready")
        t2_ready = sem("t2_ready")
        t2_turned = sem("t2_turned")
        t2_kept = sem("t2_kept")
        z_ready = sem("z_ready")
        z_kept = sem("z_kept")
        em_ready = sem("em_ready")
        h2_zero = sem("h2_zero")
        gm_step = sem("gm_step")
        gm_turned = sem("gm_turned")
        gm_spread = sem("gm_spread")
        rowb_in = [sem(f"rowb_in{i}") for i in range(2)]
        idx2_ready = sem("idx2_ready")
        rows2_in = [sem(f"rows2_in{i}") for i in range(3)]
        dls_ready = sem("dls_ready")
        act_scaled = sem("act_scaled")
        st_ready = sem("st_ready")
        edm_ready = sem("edm_ready")
        edm_used = sem("edm_used")
        small_step = sem("small_step")
        expo_in = sem("expo_in")
        expo_out = sem("expo_out")
        us_ready = sem("us_ready")
        sum_ready = sem("sum_ready")
        sum_added = sem("sum_added")
        x3_ready = sem("x3_ready")
        onehot2_ready = sem("onehot2_ready")
        wbd_zero = sem("wbd_zero")
        par2_in = sem("par2_in")
        slp_turn = sem("slp_turn")
        wsl_psum = sem("wsl_psum")
        wsl_ready = sem("wsl_ready")
        t3_ready = sem("t3_ready")
        t3_turned = sem("t3_turned")
        t3_kept = sem("t3_kept")
        l_ready = sem("l_ready")
        l_kept = sem("l_kept")
        l_max = sem("l_max")
        l_less = sem("l_less")
        l_exp = sem("l_exp")
        sw_ready = sem("sw_ready")
        sw_turned = sem("sw_turned")
        sw_kept = sem("sw_kept")
        sw_summed = sem("sw_summed")
        tok_pe = sem("tok_pe")
        tok_dve = sem("tok_dve")
        tok_exp = sem("tok_exp")
        swt_staged = sem("swt_staged")
        mix_ready = sem("mix_ready")
        fin_ready = sem("fin_ready")
        z_stored = [sem(f"z_stored{i}") for i in range(2)]

        block = ctx.enter_context(nc.Block())

        @block.sync
        def _(sp):
            xv = x[0:(T - 1) * P, :].rearrange("(t p) d -> p t d", p=P)
            sp.dma_start(lastI[:, :], dst.rearrange("(a b e) -> a b e", a=1, e=BLK)[:, :, BLK - 1]).then_inc(last_in, 16)
            for i in range(3):
                sp.dma_start(XH[:, 16 * i:16 * (i + 1), :], xv[:, 16 * i:16 * (i + 1), :]).then_inc(x_in[i], 16)
            sp.dma_start(XH[:, T - 1, :], x[(T - 1) * P:T * P, :]).then_inc(x_in[3], 16)
            sp.dma_start(w12[:, 0, :, :], w1T.rearrange("(k p) f -> p k f", p=P)).then_inc(par_in, 16)
            sp.dma_start(w12[:, 1, :, :], w2T.rearrange("(k p) f -> p k f", p=P)).then_inc(par_in, 16)
            for i, v in enumerate((gamma1, beta1, gamma_h, beta_h)):
                sp.dma_start(bnp[:, i, :], v.rearrange("(k p) -> p k", p=P)).then_inc(par_in, 16)
            sp.dma_start(bnp[:, 4, 0:1], epsw.rearrange("(a b) -> a b", a=1).broadcast_to((P, 1))).then_inc(par_in, 16)

            sp.dma_start(wr[:, :, :], Wr.rearrange("(k p) e -> p k e", p=P)).then_inc(par_in, 16)
            sp.dma_start(rt[:, 0, :], br.rearrange("(a b) -> a b", a=1).broadcast_to((P, NX))).then_inc(par_in, 16)
            sp.dma_start(b1s, b1).then_inc(par_in, 16)
            sp.dma_start(b2s[:, :], b2).then_inc(par_in, 16)
            sp.dma_start(gbB[:, 0, :], gamma.rearrange("(a b) -> a b", a=1).broadcast_to((P, D))).then_inc(par_in, 16)
            sp.dma_start(gbB[:, 1, :], beta.rearrange("(a b) -> a b", a=1).broadcast_to((P, D))).then_inc(par_in, 16)
            for k in range(KC):
                sp.dma_start(WZ[:, k, 0:D].rearrange("p (h o) -> p h o", h=GH), gW[:, k * P:(k + 1) * P, :].rearrange("h i o -> i h o")).then_inc(par_in, 16)
            sp.dma_start(aB[:, 0, :], ga_src.rearrange("(a h) o -> a (h o)", a=1).broadcast_to((P, D))).then_inc(par_in, 16)
            sp.dma_start(aB[:, 1, :], ga_dst.rearrange("(a h) o -> a (h o)", a=1).broadcast_to((P, D))).then_inc(par_in, 16)

            sp.wait_ge(wbd_zero, 1)
            for i, v in enumerate((W_slice, W_q, W_k, W_v)):
                for b in range(2):
                    sp.dma_start(WBD[b * SG:(b + 1) * SG, i, b * SG:(b + 1) * SG], v).then_inc(par2_in, 16)
            sp.dma_start(it[:, :], temperature.rearrange("a h b c -> (a b c) h").broadcast_to((P, SH))).then_inc(par2_in, 16)
            sp.dma_start(bxc[:, :], b_x.rearrange("(q p) -> p q", p=P)).then_inc(par2_in, 16)

            for j in range(GC):
                sp.wait_ge(tabf_ready, j + 1)
                sp.dma_start(dlTab[j * P:(j + 1) * P, :], tf[:, j % 2, 0, :]).then_inc(dl_stored, 16)
                sp.wait_ge(dl_stored, 16 * (j + 1))

            def store_h(t, s, warm):
                sp.wait_ge(h_ready, t + 1)
                sp.dma_start(hTab[ds(t * P, P), :], HS[:, s, :]).then_inc(h_stored[s], 16)
            over_pairs(sp, (T - 1) // 2, 1, store_h)

            def store_z(t, s, warm):
                sp.wait_ge(z_kept, 2 * (t + 1))
                sp.dma_start(zTab[ds(t * P, P), :], zS[:, s, 0:ROW]).then_inc(z_stored[s], 16)
            over_pairs(sp, (T - 1) // 2, 1, store_z)

            def load_rows(n, half, warm):
                if warm:
                    sp.wait_ge(st_ready, HALF * (n - 1))
                else:
                    sp.wait_ge(z_kept, 2 * T)
                sp.dma_start(ROWB[:, half, :, :].rearrange("p g e -> p (g e)"),
                             dlTab[ds(n * HALF, HALF), :].rearrange("(a g) e -> a (g e)", a=1).broadcast_to((P, HALF * BLK))).then_inc(rowb_in[half], 16)
            over_pairs(sp, BODIES // 2, 0, load_rows)

            sp.wait_ge(sum_ready, GROUPS)
            sp.dma_start(WXT, W_xT.rearrange("(q p) k -> p q k", p=P)).then_inc(par2_in, 16)
            sp.dma_start(WFX, W_fx.rearrange("(k p) f -> p k f", p=P)).then_inc(par2_in, 16)
            sp.dma_start(WOUT[:, :, :], W_out.rearrange("(q p) d -> p q d", p=P)).then_inc(par2_in, 16)
            sp.dma_start(bfx, b_fx.rearrange("(a b) -> a b", a=1)).then_inc(par2_in, 16)
            sp.dma_start(bsB, b_slice.rearrange("(a b) -> a b", a=1).broadcast_to((P, SG))).then_inc(par2_in, 16)
            sp.dma_start(boutB[:, :], b_out.rearrange("(a b) -> a b", a=1).broadcast_to((P, D))).then_inc(par2_in, 16)

            def store(t, s, warm):
                sp.wait_ge(fin_ready, t + 1)
                if isinstance(t, int) and t == T - 1:
                    sp.dma_start(out[t * P:N, :], XH[0:LAST, t, :]).then_inc(out_stored, 16)
                else:
                    sp.dma_start(out[ds(t * P, P), :], XH[:, ds(t, 1), :].rearrange("p t d -> p (t d)")).then_inc(out_stored, 16)
            over_pairs(sp, (T - 1) // 2, 1, store)
            sp.wait_ge(out_stored, 16 * T)

        @block.gpsimd
        def _(pool):
            step = Chain(pool, pool_step)
            step(nc.gpsimd.memset(ident[:, :], 0.0))
            step(nc.gpsimd.affine_select(out=ident[:, :], in_=ident[:, :], compare_op=ALU.not_equal, fill=1.0,
                                         base=0, pattern=[[-1, P]], channel_multiplier=1))
            step(nc.gpsimd.iota(iint[:, :], [[1, P]], base=0, channel_multiplier=0))
            step(nc.gpsimd.iota(ipint[:, :], [[0, 1]], base=0, channel_multiplier=1))
            step(nc.gpsimd.iota(kki, [[1, GC * P]], base=0, channel_multiplier=0))
            step(nc.gpsimd.iota(kci[:, :], [[P, GC]], base=0, channel_multiplier=1))
            step(nc.gpsimd.tensor_copy(iota[:, :], iint[:, :]))
            step(nc.gpsimd.tensor_copy(iotap[:, :], ipint[:, :]))
            step(nc.gpsimd.tensor_copy(kk[:, :], kki))
            step(nc.gpsimd.tensor_copy(cols[:, 0, :], kci[:, :]))
            step(nc.gpsimd.memset(onesb[:, :], 1.0))
            step(nc.gpsimd.memset(ones[:, :], 1.0))
            step(nc.gpsimd.memset(valid[:, :], 1.0))
            step(nc.gpsimd.tensor_scalar(valid[:, 1:2], iotap[:, :], float(LAST), None, ALU.is_lt))
            step(nc.gpsimd.tensor_scalar(thr[:, 0:1], iotap[:, :], float(P), float(P), ALU.mult, ALU.add))
            step(nc.gpsimd.memset(mhalf[:, :], -0.5))
            step(nc.gpsimd.memset(WBD[:, :, :], 0.0))
            pool.sem_inc(wbd_zero, 1)
            step(nc.gpsimd.tensor_scalar(bm[:, 0, :], iota[:, :], float(SG), None, ALU.is_lt))
            step(nc.gpsimd.tensor_scalar(ms[:, 0:1], iotap[:, :], float(SG), None, ALU.is_lt))
            step(nc.gpsimd.tensor_scalar(bm[:, 0, :], bm[:, 0, :], ms[:, 0:1], None, ALU.is_equal))
            step(nc.gpsimd.tensor_scalar(bm[:, 1, :], bm[:, 0, :], 1.0, 1e30, ALU.subtract, ALU.mult))
            for q in range(6):
                k, m = (q, D) if q < KC else (q - KC, F1)
                step(nc.gpsimd.memset(emul[:, q:q + 1], float(m)))
                step(nc.gpsimd.tensor_scalar(ebase[:, q:q + 1], iotap[:, :], float(k * P), None, ALU.add))
            pool.sem_inc(consts_ready, 1)

            pool.wait_ge(cidx_ready, 1)
            for j in range(GC):
                if j >= 2:
                    pool.wait_ge(tabf_ready, j - 1)
                for a, arr in enumerate((dst, src, ew)):
                    o = tg[:, j % 2, a, :]
                    pool.indirect_dma_start(o if a == 2 else o.bitcast(i32), None,
                                            arr.rearrange("(b e) -> b e", e=BLK),
                                            bass.IndirectOffsetOnAxis(ap=cidx[:, j:j + 1], axis=0)).then_inc(tab_in[j % 2], 16)

            def add_h(t, s, warm):
                pool.wait_ge(h_ready, t + 1)
                nc.gpsimd.tensor_tensor(XH[:, ds(t, 1), :], XH[:, ds(t, 1), :], HS[:, s:s + 1, :], ALU.add).then_inc(h_added, 1)
            over_pairs(pool, (T - 1) // 2, 1, add_h)

            pool.wait_ge(h_stored[0], 16 * (T // 2 + 1))
            pool.wait_ge(h_stored[1], 16 * (T // 2))

            def gather(n, j, i):
                pool.wait_ge(idx_ready, n + 1)
                if past(n, 4):
                    pool.wait_ge(part_ready, UG * (n - 3))
                pool.sem_inc(gather_turn, 1)
                for s in range(NU):
                    pool.indirect_dma_start(GU[:, j * NU + s, :], None, hTab,
                                            bass.IndirectOffsetOnAxis(ap=IDXU[:, j * NU + s:j * NU + s + 1], axis=0)).then_inc(rows_in[j], 16)
            over(pool, UNITS, 4, gather)

            pool.wait_ge(chosen, 1)
            for j in range(TOPK):
                for q in range(6):
                    tab_, o = (W1, EW1[:, j, q, :]) if q < KC else (W2, EW2[:, j, q - KC, :])
                    pool.indirect_dma_start(o, None, tab_.rearrange("e r c -> (e r) c"),
                                            bass.IndirectOffsetOnAxis(ap=EI[:, j, q:q + 1], axis=0)).then_inc(ew_in, 16)

            def finish(t, s):
                pool.wait_ge(var_ready, t + 1)
                nc.gpsimd.tensor_tensor(vrs[:, s:s + 1], vrs[:, s:s + 1], mhalf[:, :], ALU.pow).then_inc(rs_ready, 1)
                pool.wait_ge(v_ready, t + 1)
                v = HS[:, s, :]
                nc.gpsimd.tensor_tensor(v, v, gbB[:, 0, :], ALU.mult).then_inc(pool_step, 1)
                pool.wait_ge(pool_step, step.at + 2 * t + 1)
                nc.gpsimd.tensor_tensor(v, v, gbB[:, 1, :], ALU.add).then_inc(pool_step, 1)
                pool.wait_ge(pool_step, step.at + 2 * t + 2)
                nc.gpsimd.tensor_tensor(XH[:, ds(t, 1), :], XH[:, ds(t, 1), :], HS[:, s:s + 1, :], ALU.add).then_inc(x2_ready, 1)
            over_pairs(pool, (T - 1) // 2, 1, lambda t, s, warm: finish(t, s))

            pool.wait_ge(s1_ready, TOPK * FQ * (CHUNKS + 1))
            nc.gpsimd.memset(A[:, 0:T * ROW], 0.0).then_inc(h2_zero, 1)
            pool.wait_ge(z_stored[0], 16 * (T // 2 + 1))
            pool.wait_ge(z_stored[1], 16 * (T // 2))

            def gather2(n, j, i):
                pool.wait_ge(idx2_ready, n + 1)
                if past(n, 3):
                    pool.wait_ge(us_ready, (HALF - 1) * (n - 2))
                    pool.wait_ge(act_scaled, n - 2)
                else:
                    pool.wait_ge(dls_ready, 1)
                pool.sem_inc(gather_turn, 1)
                for s in range(NS):
                    pool.indirect_dma_start(ROWS2[j % 3][:, s, :], None, zTab,
                                            bass.IndirectOffsetOnAxis(ap=IDX[:, j % 3, s:s + 1], axis=0)).then_inc(rows2_in[j % 3], 16)
            over(pool, BODIES, 6, gather2)

            pool.wait_ge(sum_ready, GROUPS)
            nc.gpsimd.memset(SWsum, 0.0).then_inc(sw_summed, 1)

            def slices(t, s, warm):
                pool.wait_ge(l_max, t + 1)
                lv = SWS[:, s, :].rearrange("p (h g) -> p h g", h=SH)
                nc.gpsimd.tensor_tensor(lv, lv, ax[:, s, :].rearrange("p (h a) -> p h a", a=1).broadcast_to((P, SH, SG)), ALU.subtract).then_inc(l_less, 1)
                if isinstance(t, int) and t == 0:
                    return
                sum_slices(t - 1, 1 - s, P)

            def sum_slices(t, s, np_):
                pool.wait_ge(sw_ready, t + 1)
                pool.wait_ge(sw_summed, t + 1)
                nc.gpsimd.tensor_tensor(SWsum[0:np_, :], SWsum[0:np_, :], SWS[0:np_, s, :], ALU.add).then_inc(sw_summed, 1)
            over_pairs(pool, (T - 1) // 2, 1, slices)
            sum_slices(T - 1, 0, LAST)

        @block.vector
        def _(dve):
            step = Chain(dve, dve_step)
            dve.wait_ge(last_in, 16)
            nc.vector.tensor_copy(lastF[:, :], lastI[:, :]).then_inc(lastf_ready, 1)
            dve.wait_ge(consts_ready, 1)
            dve.wait_ge(lastrow_ready, 1)
            h = NBP // 2
            for i in range(2):
                step(nc.vector.tensor_scalar(cmp[:, i * h:(i + 1) * h], PB[i][0:T - 1, 0:h], thr[0:T - 1, 0:1], None, ALU.is_lt))
            step(nc.vector.tensor_reduce(thr[0:T - 1, 1:2], cmp, AX.X, ALU.add))
            step(nc.vector.tensor_tensor(thr[0:T - 1, 1:2], thr[0:T - 1, 1:2], iotap[0:T - 1, :], ALU.add))
            nc.vector.tensor_scalar(tcmp, kk[0:T - 1, :], thr[0:T - 1, 1:2], None, ALU.is_gt).then_inc(tcmp_ready, 1)
            dve.wait_ge(tk_psum, 1)
            hk = GC * P // 2
            for i in range(2):
                step(nc.vector.tensor_copy(TK[:, i * hk:(i + 1) * hk], PB[2 + i][:, 0:hk]))
            step(nc.vector.tensor_copy(cols[:, 1, :], PB[4][:, 0:GC]))
            step(nc.vector.tensor_tensor(cols[:, 2, :], cols[:, 0, :], cols[:, 1, :], ALU.subtract))
            step(nc.vector.tensor_scalar_min(cols[:, 2, :], cols[:, 2, :], float(NBP - 1)))
            step(nc.vector.tensor_scalar_mul(cols[:, 3, :], cols[:, 1, :], float(P)))
            nc.vector.tensor_copy(cidx[:, :], cols[:, 2, :]).then_inc(cidx_ready, 1)
            for j in range(GC):
                s = j % 2
                dve.wait_ge(tab_in[s], 48 * (j // 2 + 1))
                if j >= 2:
                    dve.wait_ge(tab_turned, j - 1)
                    dve.wait_ge(dl_stored, 16 * (j - 1))
                step(nc.vector.tensor_scalar(tf[:, s, 0, :], tg[:, s, 0, :].bitcast(i32), cols[:, 3, j:j + 1], None, ALU.subtract))
                step(nc.vector.tensor_copy(tf[:, s, 1, :], tg[:, s, 1, :].bitcast(i32)))
                nc.vector.tensor_copy(tf[:, s, 2, :], tg[:, s, 2, :]).then_inc(tabf_ready, 1)

            def stats(t, s, warm):
                nc.vector.bn_stats(BS[:, ds(t, 1), :], XH[:, ds(t, 1), :]).then_inc(dve_step, 1)

            def row_stats():
                me, mo, m, v, rs = BS[:, :, 1], BS[:, :, 4], MV[:, :, 0], MV[:, :, 1], RS[:, :]
                step(nc.vector.tensor_tensor(m, me, mo, ALU.subtract))
                step(nc.vector.tensor_tensor(m, m, m, ALU.mult))
                step(nc.vector.tensor_tensor(v, BS[:, :, 2], BS[:, :, 5], ALU.add))
                step(nc.vector.tensor_scalar_mul(v, v, 1.0 / D))
                step(nc.vector.scalar_tensor_tensor(v, m, 0.25, v, ALU.mult, ALU.add))
                step(nc.vector.tensor_tensor(m, me, mo, ALU.add))
                step(nc.vector.tensor_scalar_mul(m, m, 0.5))
                nc.vector.tensor_scalar_add(rs, v, EPS).then_inc(veps_ready, 1)

            for i in range(4):
                dve.wait_ge(x_in[i], 16)
            over_pairs(dve, (T - 1) // 2, 1, stats)
            step.at += T
            dve.wait_ge(dve_step, step.at)
            row_stats()
            nc.vector.memset(YD[:, :, 2, :], 0.0).then_inc(dve_step, 1)
            step.at += 1
            dve.wait_ge(sqrt_ready, 1)
            step(nc.vector.reciprocal(RS[:, :], RS[:, :]))

            def norm(t, s, warm):
                if warm:
                    dve.wait_ge(h_turned, t - 1)
                    dve.wait_ge(h_added, t - 1)
                    dve.wait_ge(h_stored[s], (t // 2) * 16 if isinstance(t, int) else t * 8 - 8 * s)
                nc.vector.tensor_scalar(HS[:, s:s + 1, :], XH[:, ds(t, 1), :], MV[:, ds(t, 1), 0], RS[:, ds(t, 1)],
                                        ALU.subtract, ALU.mult).then_inc(h_ready, 1)
            over_pairs(dve, (T - 1) // 2, 1, norm)
            dve.wait_ge(h_kept, T)

            tks = []

            def tiles_of(lo, k, engine):
                _, v = nc.values_load_multi_w_load_instructions(TK[0:1, ds(lo, k)], [engine], min_val=0, max_val=T - 1,
                                                                    skip_runtime_bounds_check_because=IN_RANGE)
                return v

            def onehots(n, j, i):
                if j % 2 == 0:
                    first = isinstance(n, int) and n == 0
                    v = tiles_of(0 if first else n * UG - 1, 2 * UG, mybir.EngineType.DVE)
                    tks[:] = (None, *v[0:2 * UG - 1]) if first else v
                dve.wait_ge(idx_ready, n + 1)
                for g in range(UG):
                    gi = n * UG + g
                    if past(n, 1):
                        dve.wait_ge(part_ready, gi - 1)
                    for b in range(SUB):
                        c = j * NU + g * SUB + b
                        nc.vector.tensor_scalar(S[:, g, b, :], iota[:, :], DLU[:, c:c + 1], WS[:, c:c + 1],
                                                ALU.is_equal, ALU.mult).then_inc(onehot_ready, 1)
                        nc.vector.tensor_scalar(S1[:, g, b, :], iota[:, :], DLU[:, c:c + 1], None,
                                                ALU.is_equal).then_inc(onehot_ready, 1)
                    if past(n, 1) or g >= 1:
                        add_part(gi - 1, 1 - g, tks[(j % 2) * UG + g])

            def add_part(gi, sl, tk):
                dve.wait_ge(part_ready, gi + 1)
                if past(gi, 1):
                    dve.wait_ge(part_added, gi)
                y = A[:, ds(tk * 384, 384)]
                nc.vector.tensor_tensor(y, y, PB[sl][:, 0:384], ALU.add).then_inc(part_added, 1)
            over(dve, UNITS, 4, onehots)
            add_part(GROUPS - 1, (GROUPS - 1) % 2, tiles_of(GROUPS - 1, 1, mybir.EngineType.DVE)[0])

            dve.wait_ge(part_added, GROUPS)
            nc.vector.tensor_scalar_max(YD[:, :, 2, :], YD[:, :, 2, :], 1.0).then_inc(degmax, 1)
            dve.wait_ge(degsqrt, 1)
            step(nc.vector.reciprocal(YD[:, :, 2, :], YD[:, :, 2, :]))

            def chunk_stats(q, base):
                def f(c, s, warm, n=512):
                    for k in range(KC):
                        bank = PB[2 * s + k]
                        dve.wait_ge(lin_ready, base + KC * c + k + 1)
                        if q:
                            nt = 4 if n == 512 else 1
                            o = bank[:, 0:nt * P if n == 512 else n]
                            if n == 512:
                                o3 = o.rearrange("p (t n) -> p t n", n=P)
                                r = YD[:, ds(c * 4, 4), 2, :]
                            else:
                                o3, r = o, YD[:, T - 1, 2, 0:n]
                            nc.vector.tensor_tensor(o3, o3, r, ALU.mult).then_inc(dve_step, 1)
                            dve.wait_ge(dve_step, step.at + (KC * c + k + 1))
                        nc.vector.bn_stats(BSF[:, k, ds(c, 1), :], bank[:, 0:n]).then_inc(lin_stat, 1)
                return f

            def batchnorm(q, base):
                f = chunk_stats(q, base)
                over_pairs(dve, CHUNKS // 2, 0, f)
                f(CHUNKS, 0, True, LAST)
                if q:
                    step.at += KC * (CHUNKS + 1)
                dve.wait_ge(lin_stat, (q + 1) * KC * (CHUNKS + 1))
                for k in range(KC):
                    step(nc.vector.bn_aggr(MVF[:, k, :], BSF[:, k, :, :]))
                nc.vector.tensor_scalar_add(bns[:, 0, :], MVF[:, :, 1], EPS).then_inc(bn_var, 1)
                dve.wait_ge(bn_sqrt, q + 1)
                step(nc.vector.reciprocal(bns[:, 0, :], bns[:, 0, :]))
                step(nc.vector.tensor_tensor(bns[:, 1, :], bns[:, 0, :], bnp[:, 2 * q, :], ALU.mult))
                step(nc.vector.tensor_tensor(bns[:, 2, :], MVF[:, :, 0], bns[:, 1, :], ALU.mult))
                nc.vector.tensor_tensor(bns[:, 3, :], bnp[:, 2 * q + 1, :], bns[:, 2, :], ALU.subtract).then_inc(bn_ready, 1)
            dve.wait_ge(par_in, 16 * NPAR)
            batchnorm(0, 0)
            batchnorm(1, KC * (CHUNKS + 1))

            dve.wait_ge(h_added, T)

            def residual(t, s, warm):
                dve.wait_ge(r_turned, t + 1)
                nc.vector.tensor_tensor(XH[:, ds(t, 1), :], XH[:, ds(t, 1), :], PB[s][:, 0:D].rearrange("p (a d) -> p a d", a=1), ALU.add).then_inc(x1_ready, 1)
                dve.wait_ge(x1_ready, t + 1)
                nc.vector.bn_stats(BS[:, ds(t, 1), :], XH[:, ds(t, 1), :]).then_inc(dve_step, 1)
            over_pairs(dve, (T - 1) // 2, 1, residual)
            step.at += T
            dve.wait_ge(dve_step, step.at)

            row_stats()
            dve.wait_ge(sqrt_ready, 2)
            step(nc.vector.reciprocal(RS[:, :], RS[:, :]))
            step(nc.vector.scalar_tensor_tensor(nmr[:, :], MV[:, :, 0], -1.0, RS[:, :], ALU.mult, ALU.mult))
            dve.wait_ge(r_turned, T)

            def norm1(t, s, warm):
                if warm:
                    dve.wait_ge(t1_turned, t - 1)
                nc.vector.tensor_scalar(HS[:, s:s + 1, :], XH[:, ds(t, 1), :], MV[:, ds(t, 1), 0], RS[:, ds(t, 1)],
                                        ALU.subtract, ALU.mult).then_inc(t1_ready, 1)
            over_pairs(dve, (T - 1) // 2, 1, norm1)

            dve.wait_ge(sums_ready, 1)
            for k in range(KC):
                step(nc.vector.tensor_copy(ms[:, k:k + 1], PB[2 + k][:, 0:1]))
            for k in range(KC):
                ins = nc.vector.tensor_scalar(MSB[:, k, :], ones[:, :], ms[:, k:k + 1], 1.0 / N, ALU.mult, ALU.mult)
                ins.then_inc(msb_ready, 1)
            dve.wait_ge(logits_ready, 1)
            lg, p, eq, p2 = rt[:, 1, :], rt[:, 2, :], rt[:, 3, :], rt[:, 4, :]
            step(nc.vector.tensor_tensor(lg, PB[4][:, 0:NX], rt[:, 0, :], ALU.add))

            def softmax8(nth):
                step(nc.vector.tensor_reduce(r1[:, 0:1], lg, AX.X, ALU.max))
                nc.vector.tensor_scalar(lg, lg, r1[:, 0:1], None, ALU.subtract).then_inc(exp_in, 1)
                dve.wait_ge(exp_out, nth)
                step(nc.vector.tensor_reduce(r1[:, 1:2], p, AX.X, ALU.add))
                step(nc.vector.reciprocal(r1[:, 1:2], r1[:, 1:2]))
                step(nc.vector.tensor_scalar(p, p, r1[:, 1:2], None, ALU.mult))
            softmax8(1)
            step(nc.vector.tensor_scalar_min(lg, p, CAP / N))
            softmax8(2)
            iota8 = iota[:, 0:NX]
            for j in range(TOPK):
                src_ = p if j == 0 else p2
                step(nc.vector.tensor_reduce(r1[:, 2 + j:3 + j], src_, AX.X, ALU.max))
                step(nc.vector.tensor_scalar(eq, src_, r1[:, 2 + j:3 + j], -float(NX), ALU.is_ge, ALU.mult))
                step(nc.vector.tensor_tensor(eq, eq, iota8, ALU.add))
                step(nc.vector.tensor_reduce(r1[:, 4 + j:5 + j], eq, AX.X, ALU.min))
                step(nc.vector.tensor_scalar_add(r1[:, 4 + j:5 + j], r1[:, 4 + j:5 + j], float(NX)))
                step(nc.vector.tensor_scalar(ohs[:, j, :], iota8, r1[:, 4 + j:5 + j], None, ALU.is_equal))
                if j == 0:
                    step(nc.vector.scalar_tensor_tensor(p2, ohs[:, 0, :], -2.0, p, ALU.mult, ALU.add))
            for j in range(TOPK):
                ins = nc.vector.scalar_tensor_tensor(EI[:, j, :], emul[:, :], r1[:, 4 + j:5 + j], ebase[:, :], ALU.mult, ALU.add)
                step(ins)
            dve.sem_inc(chosen, 1)
            nc.vector.tensor_tensor(r1[:, 6:7], r1[:, 3:4], r1[:, 2:3], ALU.subtract).then_inc(exp_in, 1)
            dve.wait_ge(exp_out, 3)
            step(nc.vector.tensor_scalar_add(r1[:, 8:9], r1[:, 7:8], 1.0))
            step(nc.vector.reciprocal(r1[:, 8:9], r1[:, 8:9]))
            step(nc.vector.tensor_tensor(r1[:, 9:10], r1[:, 7:8], r1[:, 8:9], ALU.mult))
            step(nc.vector.tensor_scalar(ohs[:, 2, :], ohs[:, 0, :], r1[:, 8:9], None, ALU.mult))
            step(nc.vector.scalar_tensor_tensor(ohs[:, 2, :], ohs[:, 1, :], r1[:, 9:10], ohs[:, 2, :], ALU.mult, ALU.add))
            dve.sem_inc(chosen, 1)
            dve.wait_ge(ohs_turned, 1)
            nc.vector.tensor_copy(ohT[:, :, :], PB[6][0:NX, 0:3 * P].rearrange("e (j n) -> e j n", j=3)).then_inc(ohT_ready, 1)
            dve.wait_ge(b_picked, 1)
            step(nc.vector.tensor_copy(b1c[:, :], PB[5][:, 0:TOPK * FQ]))
            nc.vector.tensor_copy(B2M[:, :], PB[7][:, 0:D]).then_inc(b_kept, 1)
            dve.wait_ge(ew_in, 16 * 12)
            for j in range(TOPK):
                nc.vector.tensor_scalar(EW2[:, j, :, :], EW2[:, j, :, :], r1[:, 8 + j:9 + j], None, ALU.mult).then_inc(ew_ready, 1)

            for k in range(KC):
                for q in range(2):
                    step(nc.vector.tensor_tensor(MSB[:, :, :].rearrange("p a b -> p (a b)"), WZ[:, k, 0:D], aB[:, q, :], ALU.mult))
                    step(nc.vector.tensor_reduce(WZ[:, k, D + q * GH:D + (q + 1) * GH],
                                                 MSB[:, :, :].rearrange("p a (c o) -> p (a c) o", o=GO), AX.X, ALU.add))

            dve.wait_ge(t1_turned, T)

            def after_moe(t, s, m, warm):
                V = HS[:, s, :]
                dve.wait_ge(moe_ready, t + 1)
                if warm:
                    dve.wait_ge(x2_ready, t - 1)
                nc.vector.scalar_tensor_tensor(HS[:, s:s + 1, :], XH[:, ds(t, 1), :], RS[:, ds(t, 1)],
                                               PB[4 + m][:, 0:D].rearrange("p (a d) -> p a d", a=1), ALU.mult, ALU.add).then_inc(moe_kept, 1)
                dve.wait_ge(moe_kept, t + 1)
                b = step.at + 3 * t
                nc.vector.scalar_tensor_tensor(V, B2M[:, :], nmr[:, ds(t, 1)], V, ALU.add, ALU.add).then_inc(dve_step, 1)
                dve.wait_ge(dve_step, b + 1)
                nc.vector.bn_stats(vst[:, s, :], V).then_inc(dve_step, 1)
                wait_apart(dve, dve_step, b + 2, dve_turn)
                nc.vector.bn_aggr(vmv[:, s, :], vst[:, s, :]).then_inc(dve_step, 1)
                dve.wait_ge(dve_step, b + 3)
                nc.vector.tensor_scalar_add(vrs[:, s:s + 1], vmv[:, s, 1:2], EPS).then_inc(var_ready, 1)
                dve.wait_ge(rs_ready, t + 1)
                nc.vector.tensor_scalar(V, V, vmv[:, s, 0:1], vrs[:, s:s + 1], ALU.subtract, ALU.mult).then_inc(v_ready, 1)

            def chunk_after(c, s, warm):
                for m in range(4):
                    after_moe(c * 4 + m, m % 2, m, warm or (isinstance(c, int) and c > 0) or m >= 2)
            over_pairs(dve, CHUNKS // 2, 0, chunk_after)
            after_moe(T - 1, 0, 0, True)
            step.at += 3 * T
            dve.wait_ge(x2_ready, T)

            over_pairs(dve, (T - 1) // 2, 1, stats)
            step.at += T
            dve.wait_ge(dve_step, step.at)
            row_stats()
            dve.wait_ge(sqrt_ready, 3)
            step(nc.vector.reciprocal(RS[:, :], RS[:, :]))

            def norm2(t, s, warm):
                if warm:
                    dve.wait_ge(t2_turned, t - 1)
                nc.vector.tensor_scalar(HS[:, s:s + 1, :], XH[:, ds(t, 1), :], MV[:, ds(t, 1), 0], RS[:, ds(t, 1)],
                                        ALU.subtract, ALU.mult).then_inc(t2_ready, 1)
            over_pairs(dve, (T - 1) // 2, 1, norm2)

            dve.wait_ge(z_kept, 2 * T)
            step(nc.vector.tensor_reduce(gm[:, :], EM[:, 0:T - 1, 0:GH].rearrange("p t h -> p h t"), AX.X, ALU.max))
            nc.vector.tensor_tensor(gm[0:LAST, :], gm[0:LAST, :], EM[0:LAST, T - 1, 0:GH], ALU.max).then_inc(gm_step, 1)
            dve.wait_ge(gm_turned, 1)
            step(nc.vector.tensor_reduce(gm4[:, 0:1], PB[4][0:GH, 0:P], AX.X, ALU.max))
            nc.vector.tensor_scalar(gm4[:, 1:1 + GH], ident[0:GH, 0:GH], gm4[:, 0:1], None, ALU.mult).then_inc(gm_step, 1)
            dve.wait_ge(gm_spread, 1)
            step(nc.vector.tensor_copy(gm[:, :], PB[4][:, 0:GH]))
            step(nc.vector.tensor_copy(EM[:, :, 0:GH], gm[:, :].rearrange("p (a h) -> p a h", a=1).broadcast_to((P, T, GH))))
            for i in range(3):
                step(nc.vector.tensor_copy(EM3[:, :, i, :], EM[:, :, :]))
                if i < 2:
                    step(nc.vector.tensor_tensor(EM[:, :, :], EM[:, :, :], EM3[:, :, i, :], ALU.subtract))
            dve.sem_inc(em_ready, 1)

            def turned_onehot(gi, half, g):
                if past(gi, HALF):
                    dve.wait_ge(edm_ready, gi - HALF + 1)
                nc.vector.tensor_scalar(ST[:, g, :], ROWB[:, half, g, :], iotap[:, 0:1], None, ALU.is_equal).then_inc(st_ready, 1)

            def scores(n, j, i, between=()):
                k = [0]
                between = list(between)

                def small(ins):
                    ins.then_inc(small_step, 1)
                    k[0] += 1
                    if between:
                        turned_onehot(*between.pop(0))
                    dve.wait_ge(small_step, n * 6 + k[0])
                dve.wait_ge(edm_ready, HALF * (n + 1))
                small(nc.vector.tensor_copy(scn[:, :, :], PB[2 + j % 2][:, 0:NS * 2 * GH].rearrange("p (s v) -> p s v", s=NS)))
                dve.sem_inc(edm_used, 1)
                dve.wait_ge(rows2_in[j % 3], 16 * NS * (2 * i + j // 3 + 1))
                v = [sc[:, i_, :].rearrange("p (s h) -> p s h", h=GH) for i_ in range(4)]
                small(nc.vector.tensor_tensor(v[1], scn[:, :, 0:GH], scn[:, :, GH:2 * GH], ALU.add))
                small(nc.vector.tensor_tensor(v[2], ROWS2[j % 3][:, :, D:ROW], scn[:, :, GH:2 * GH], ALU.add))
                small(nc.vector.scalar_tensor_tensor(sc[:, 1:3, :], sc[:, 1:3, :], 0.01, sc[:, 1:3, :], ALU.mult, ALU.max))
                small(nc.vector.tensor_tensor(sc[:, 3, :], sc[:, 2, :], sc[:, 1, :], ALU.subtract))
                if past(n, 1):
                    dve.wait_ge(expo_out, n)
                small(nc.vector.tensor_scalar_min(sc[:, 0, :], sc[:, 3, :], 0.0))
                dve.sem_inc(expo_in, 1)

            dve.wait_ge(rowb_in[0], 16)
            for g in range(HALF):
                turned_onehot(g, 0, g)
            dve.wait_ge(rowb_in[1], 16)
            scores(0, 0, 0, [(HALF + g, 1, g) for g in range(HALF)])
            dve.wait_ge(h2_zero, 1)

            def add_sum(gi, sl, tk):
                dve.wait_ge(sum_ready, gi + 1)
                if past(gi, 1):
                    dve.wait_ge(sum_added, gi)
                y = A[:, ds(tk * ROW, ROW)]
                nc.vector.tensor_tensor(y, y, SUMS[sl][:, 0:ROW], ALU.add).then_inc(sum_added, 1)

            def attend(n, j, i):
                half, b3 = j % 2, j % 3
                first, end = isinstance(n, int) and n == 0, isinstance(n, int) and n == BODIES - 1
                v = tiles_of(0 if first else n * HALF - LAG, HALF, mybir.EngineType.DVE)
                if first:
                    v = (*(None,) * LAG, *v[0:HALF - LAG])
                dve.wait_ge(dls_ready, n + 1)
                more = not (isinstance(n, int) and n + 2 >= BODIES)
                if more:
                    dve.wait_ge(rowb_in[half], 16 * (3 * i + (j + 2) // 2 + 1))
                for g in range(HALF):
                    gi = n * HALF + g
                    if past(n, 1):
                        dve.wait_ge(sum_ready, gi - HALF + 1)
                    for b in range(SUB):
                        c = g * SUB + b
                        nc.vector.tensor_scalar(SR[g][:, b, :], iota[:, :], DLS[:, b3, c:c + 1], None, ALU.is_equal).then_inc(onehot2_ready, 1)
                    if g == 0:
                        dve.wait_ge(expo_out, n + 1)
                    if g < HALF - 1:
                        u0 = half * NS + g * SUB
                        nc.vector.tensor_tensor(US[:, u0:u0 + SUB, 0:D].rearrange("p s (h o) -> p s h o", h=GH),
                                                ROWS2[b3][:, g * SUB:(g + 1) * SUB, 0:D].rearrange("p s (h o) -> p s h o", h=GH),
                                                US[:, u0:u0 + SUB, D:ROW].rearrange("p s (h a) -> p s h a", a=1).broadcast_to((P, SUB, GH, GO)),
                                                ALU.mult).then_inc(us_ready, 1)
                    if g == 2 and not end:
                        scores(n + 1, j + 1, i, [((n + 2) * HALF + m, half, m) for m in range(HALF)] if more else ())
                    if past(n, 1) or g >= LAG:
                        add_sum(gi - LAG, (g - LAG) % HALF, v[g])
            over(dve, BODIES, 6, attend)
            v = tiles_of(GROUPS - LAG, LAG, mybir.EngineType.DVE)
            for g in range(LAG):
                add_sum(GROUPS - LAG + g, HALF - LAG + g, v[g])
            dve.wait_ge(sum_added, GROUPS)

            step(nc.vector.tensor_scalar_max(RD[:, :, :], H2[:, :, D:ROW], 1e-30))
            step(nc.vector.reciprocal(RD[:, :, :], RD[:, :, :]))

            def residual3(t, s, warm):
                hv = HS[:, s, :].rearrange("p (a h o) -> p a h o", a=1, h=GH)
                if warm:
                    dve.wait_ge(x3_ready, t - 1)
                else:
                    dve.wait_ge(t2_turned, T)
                nc.vector.tensor_tensor(hv, H2[:, ds(t, 1), 0:D].rearrange("p t (h o) -> p t h o", h=GH),
                                        RD[:, ds(t, 1), :].rearrange("p t (h a) -> p t h a", a=1).broadcast_to((P, 1, GH, GO)),
                                        ALU.mult).then_inc(dve_step, 1)
                dve.wait_ge(dve_step, step.at + t * 2 + 1)
                nc.vector.tensor_tensor(XH[:, ds(t, 1), :], XH[:, ds(t, 1), :], HS[:, s:s + 1, :], ALU.add).then_inc(x3_ready, 1)
                dve.wait_ge(x3_ready, t + 1)
                nc.vector.bn_stats(BS[:, ds(t, 1), :], XH[:, ds(t, 1), :]).then_inc(dve_step, 1)
            over_pairs(dve, (T - 1) // 2, 1, residual3)
            step.at += 2 * T
            dve.wait_ge(dve_step, step.at)

            dve.wait_ge(par2_in, 16 * 16)
            step(nc.vector.tensor_scalar(it[:, :], it[:, :], 0.1, 5.0, ALU.max, ALU.min))
            step(nc.vector.reciprocal(it[:, :], it[:, :]))
            dve.wait_ge(sum_ready, GROUPS)
            for q in range(PAIRS):
                step(nc.vector.tensor_scalar(bxB[:, q, :], ones[:, :], bxc[:, q:q + 1], None, ALU.mult))
            dve.sem_inc(slp_turn, 1)
            dve.wait_ge(wsl_psum, 1)
            itb = it[:, :].rearrange("p (h a) -> p h a", a=1).broadcast_to((P, SH, SG))
            for k in range(KC):
                step(nc.vector.tensor_tensor(WSL[:, k, :].rearrange("p (h g) -> p h g", h=SH), PB[4 + k][:, :].rearrange("p (h g) -> p h g", h=SH), itb, ALU.mult))
            bv = BSL.rearrange("p (h g) -> p h g", h=SH)
            step(nc.vector.tensor_tensor(bv, PB[6][:, :].rearrange("p (h g) -> p h g", h=SH), bsB.rearrange("p (a g) -> p a g", a=1).broadcast_to((P, SH, SG)), ALU.add))
            step(nc.vector.tensor_tensor(bv, bv, itb, ALU.mult))
            dve.sem_inc(wsl_ready, 1)
            row_stats()
            dve.wait_ge(sqrt_ready, 4)
            step(nc.vector.reciprocal(RS[:, :], RS[:, :]))

            def norm3(t, s):
                nc.vector.tensor_scalar(HS[:, s:s + 1, :], XH[:, ds(t, 1), :], MV[:, ds(t, 1), 0], RS[:, ds(t, 1)],
                                        ALU.subtract, ALU.mult).then_inc(t3_ready, 1)
            norm3(0, 0)

            def logits(t, s, warm):
                first = isinstance(t, int) and t == 0
                if warm:
                    dve.wait_ge(sw_turned, t - 1)
                    dve.wait_ge(sw_summed, t)
                dve.wait_ge(l_ready, t + 1)
                nc.vector.tensor_tensor(SWS[:, s, :], PB[2 + s][:, :], BSL, ALU.add).then_inc(l_kept, 1)
                dve.wait_ge(l_kept, t + 1)
                nc.vector.tensor_reduce(ax[:, s, :], SWS[:, s, :].rearrange("p (h g) -> p h g", h=SH), AX.X, ALU.max).then_inc(l_max, 1)
                if not first:
                    weights(t - 1, 1 - s)
                if not (isinstance(t, int) and t == T - 1):
                    if warm or not first:
                        dve.wait_ge(sw_turned, t)
                    norm3(t + 1, 1 - s)

            def weights(t, s):
                dve.wait_ge(l_exp, t + 1)
                b = step.at + 2 * t
                lv = SWS[:, s, :].rearrange("p (h g) -> p h g", h=SH)
                nc.vector.tensor_reduce(ax[:, 2 + s, :], lv, AX.X, ALU.add).then_inc(dve_step, 1)
                dve.wait_ge(dve_step, b + 1)
                nc.vector.reciprocal(ax[:, 2 + s, :], ax[:, 2 + s, :]).then_inc(dve_step, 1)
                dve.wait_ge(dve_step, b + 2)
                nc.vector.tensor_tensor(lv, lv, ax[:, 2 + s, :].rearrange("p (h a) -> p h a", a=1).broadcast_to((P, SH, SG)), ALU.mult).then_inc(sw_ready, 1)
            over_pairs(dve, (T - 1) // 2, 1, logits)
            weights(T - 1, 0)
            step.at += 2 * T

            dve.wait_ge(tok_pe, 1)
            for k in range(KC):
                step(nc.vector.tensor_copy(XS[:, k, :], PB[6 + k][:, :]))
            step(nc.vector.tensor_scalar_add(sden[:, :], PB[0][:, 0:PAIRS], 1e-5))
            step(nc.vector.reciprocal(sden[:, :], sden[:, :]))
            step(nc.vector.tensor_copy(nrow, PB[1][0:1, :]))
            dve.sem_inc(tok_dve, 1)

            def q3(ap):
                return ap.rearrange("p (q n) -> p q n", q=PAIRS)

            def each(m):
                return m.rearrange("p (a n) -> p a n", a=1).broadcast_to((P, PAIRS, P))

            def per(c):
                return c.rearrange("p (q a) -> p q a", a=1).broadcast_to((P, PAIRS, P))
            dve.wait_ge(tok_pe, 2)
            step(nc.vector.tensor_tensor(STK, q3(PB[2][:, :]), per(sden[:, :]), ALU.mult))
            step(nc.vector.tensor_tensor(STK, STK, each(bm[:, 0, :]), ALU.mult))
            dve.sem_inc(tok_dve, 1)
            dve.wait_ge(tok_pe, 3)
            step(nc.vector.tensor_copy(STT, q3(PB[3][:, :])))
            dve.sem_inc(tok_dve, 1)
            dve.wait_ge(tok_pe, 4)
            step(nc.vector.tensor_copy(QT, q3(PB[4][:, :])))
            step(nc.vector.tensor_copy(KT, q3(PB[5][:, :])))
            step(nc.vector.tensor_copy(VS, q3(PB[6][:, :])))
            dve.sem_inc(tok_dve, 1)
            dve.wait_ge(tok_pe, 5)
            step(nc.vector.scalar_tensor_tensor(AT, q3(PB[7][:, :]), float(64 ** -0.5), each(bm[:, 1, :]), ALU.mult, ALU.add))
            step(nc.vector.tensor_reduce(sden[:, :], AT, AX.X, ALU.max))
            step(nc.vector.tensor_tensor(AT, AT, per(sden[:, :]), ALU.subtract))
            dve.sem_inc(tok_dve, 1)
            dve.wait_ge(tok_exp, 1)
            step(nc.vector.tensor_reduce(sden[:, :], AT, AX.X, ALU.add))
            step(nc.vector.reciprocal(sden[:, :], sden[:, :]))
            step(nc.vector.tensor_tensor(AT, AT, per(sden[:, :]), ALU.mult))
            dve.sem_inc(tok_dve, 1)
            dve.wait_ge(tok_pe, 6)
            step(nc.vector.tensor_copy(ATT, q3(PB[0][:, :])))
            dve.sem_inc(tok_dve, 1)
            dve.wait_ge(tok_pe, 7)
            step(nc.vector.tensor_copy(OST, q3(PB[1][:, :])))
            dve.sem_inc(tok_dve, 1)
            dve.wait_ge(tok_pe, 8)
            for i in range(2):
                step(nc.vector.tensor_copy(VV[:, 2 * i:2 * i + 2, :], PB[2 + i][:, :].rearrange("p (q d) -> p q d", q=2)))
            dve.sem_inc(tok_dve, 1)

            def finish(t, s, warm):
                dve.wait_ge(mix_ready, t + 1)
                nc.vector.tensor_tensor(XH[:, ds(t, 1), :], XH[:, ds(t, 1), :], PB[4 + s][:, 0:D].rearrange("p (a d) -> p a d", a=1), ALU.add).then_inc(dve_step, 1)
                dve.wait_ge(dve_step, step.at + t + 1)
                nc.vector.tensor_tensor(XH[:, ds(t, 1), :], XH[:, ds(t, 1), :], boutB[:, :].rearrange("p (a d) -> p a d", a=1), ALU.add).then_inc(fin_ready, 1)
            over_pairs(dve, (T - 1) // 2, 1, finish)

        @block.scalar
        def _(act):
            for j in range(GC):
                act.wait_ge(tab_turned, j + 1)
                bank = 5 + (j % 2)
                dstc = (DLT, SRCT, WT)
                for a in range(3):
                    pb = PB[bank] if a < 2 else PB[7]
                    o0 = (a % 2) * 256 if a < 2 else (j % 2) * 256
                    nc.scalar.copy(dstc[a][:, j * BLK:(j + 1) * BLK].rearrange("p (k b) -> p b k", b=SUB),
                                   pb[:, o0:o0 + 256].rearrange("p (b k) -> p b k", b=SUB)).then_inc(tab_kept, 1)
            act.wait_ge(veps_ready, 1)
            nc.scalar.sqrt(RS[:, :], RS[:, :]).then_inc(sqrt_ready, 1)
            act.wait_ge(par_in, 16 * NPAR)

            def keep_h(t, s, warm):
                wait_apart(act, h_turned, t + 1, act_turn)
                nc.scalar.mul(YD[:, ds(t, 1), 0:2, :], PB[s][:, 0:D].rearrange("p (a c n) -> p a c n", a=1, c=2), bnp[:, 4, 0:1]).then_inc(h_kept, 1)
            over_pairs(act, (T - 1) // 2, 1, keep_h)

            act.wait_ge(tab_kept, 3 * GC)

            def columns(n, j, i):
                if past(n, 4):
                    wait_apart(act, part_ready, UG * (n - 3), act_turn)
                c, o = ds(n * NU, NU), slice(j * NU, (j + 1) * NU)
                nc.scalar.activation(DLU[:, o], DLT[:, c], ACT.Copy).then_inc(act_step, 1)
                nc.scalar.activation(WS[:, o], WT[:, c], ACT.Copy).then_inc(act_step, 1)
                nc.scalar.activation(IDXU[:, o], SRCT[:, c], ACT.Copy).then_inc(act_step, 1)
                act.wait_ge(act_step, (n + 1) * 3)
                act.sem_inc(idx_ready, 1)
            over(act, UNITS, 4, columns)

            act.wait_ge(degmax, 1)
            nc.scalar.sqrt(YD[:, :, 2, :], YD[:, :, 2, :]).then_inc(degsqrt, 1)

            def keep_lin(q, base):
                def f(c, s, warm, n=512):
                    for k in range(KC):
                        act.wait_ge(lin_stat, base + KC * c + k + 1)
                        wait_apart(act, lin_ready, base + KC * c + KC, act_turn)
                        if n == 512:
                            o = YD[:, ds(c * 4, 4), k, :]
                            i = PB[2 * s + k][:, :].rearrange("p (t n) -> p t n", n=P)
                        else:
                            o, i = YD[:, T - 1, k, 0:n], PB[2 * s + k][:, 0:n]
                        nc.scalar.activation(o, i, ACT.Copy).then_inc(lin_kept, 1)
                return f
            for q in range(2):
                base = q * KC * (CHUNKS + 1)
                if q == 1:
                    act.wait_ge(bn_ready, 1)
                    act.wait_ge(lin_kept, KC * (CHUNKS + 1))

                    def relu(c, n=512):
                        for k in range(KC):
                            y = YD[:, ds(c * 4, 4), k, :] if n == 512 else YD[:, T - 1, k, 0:n]
                            nc.scalar.activation(y, y, ACT.Relu, bias=bns[:, 3, k:k + 1], scale=bns[:, 1, k:k + 1]).then_inc(relu_ready, 1)
                    kl = keep_lin(q, base)
                    relu(0)

                    def both(c, s, warm):
                        if isinstance(c, int) and c + 1 >= CHUNKS:
                            relu(c + 1, LAST)
                        else:
                            relu(c + 1)
                        kl(c, s, warm)
                    over_pairs(act, CHUNKS // 2 - 1, 2, both)
                    kl(CHUNKS, 0, True, LAST)
                else:
                    kl = keep_lin(q, base)
                    over_pairs(act, CHUNKS // 2, 0, kl)
                    kl(CHUNKS, 0, True, LAST)
                act.wait_ge(bn_var, q + 1)
                nc.scalar.sqrt(bns[:, 0, :], bns[:, 0, :]).then_inc(bn_sqrt, 1)
            act.wait_ge(h_added, T)
            act.wait_ge(h_stored[0], 16 * (T // 2 + 1))
            act.wait_ge(h_stored[1], 16 * (T // 2))
            act.wait_ge(bn_ready, 2)
            act.wait_ge(lin_kept, 2 * KC * (CHUNKS + 1))

            def relu2(t, s, warm):
                if warm:
                    wait_apart(act, r_turned, t - 1, act_turn)
                for k in range(KC):
                    nc.scalar.activation(HS[:, s:s + 1, k * P:(k + 1) * P], YD[:, ds(t, 1), k, :], ACT.Relu,
                                         bias=bns[:, 3, k:k + 1], scale=bns[:, 1, k:k + 1]).then_inc(r_ready, 1)
            over_pairs(act, (T - 1) // 2, 1, relu2)

            act.wait_ge(veps_ready, 2)
            nc.scalar.sqrt(RS[:, :], RS[:, :]).then_inc(sqrt_ready, 1)
            act.wait_ge(r_turned, T)

            def keep_t1(t, s, warm):
                wait_apart(act, t1_turned, t + 1, act_turn)
                nc.scalar.activation(T1T[:, :, ds(t * P, P)], PB[s][:, 0:D].rearrange("p (k n) -> p k n", k=KC), ACT.Copy).then_inc(t1_kept, 1)
            over_pairs(act, (T - 1) // 2, 1, keep_t1)
            for i in range(2):
                act.wait_ge(exp_in, i + 1)
                nc.scalar.activation(rt[:, 2, :], rt[:, 1, :], ACT.Exp).then_inc(exp_out, 1)
            act.wait_ge(exp_in, 3)
            nc.scalar.activation(r1[:, 7:8], r1[:, 6:7], ACT.Exp).then_inc(exp_out, 1)
            act.wait_ge(b_kept, 1)

            def gelu(c, s, warm, n=512):
                for j in range(TOPK):
                    if warm or s == 1:
                        act.wait_ge(hid_used, TOPK * (c - 1) + j + 1)
                    for q in range(FQ):
                        act.wait_ge(s1_ready, (TOPK * c + j) * FQ + q + 1)
                        nc.scalar.activation(HID[:, j, q, 0:n], PB[q][:, 0:n], ACT.Gelu, bias=b1c[:, j * FQ + q:j * FQ + q + 1]).then_inc(gelu_ready, 1)
            over_pairs(act, CHUNKS // 2, 0, gelu)
            gelu(CHUNKS, 0, True, P)
            act.wait_ge(veps_ready, 3)
            nc.scalar.sqrt(RS[:, :], RS[:, :]).then_inc(sqrt_ready, 1)

            def keep_z(t, s, warm):
                act.wait_ge(t2_turned, t + 1)
                if warm:
                    act.wait_ge(z_ready, t - 1)
                nc.scalar.activation(TT[:, s, :, :], PB[s][:, 0:D].rearrange("p (k n) -> p k n", k=KC), ACT.Copy).then_inc(t2_kept, 1)
                act.wait_ge(z_ready, t + 1)
                if warm:
                    wait_apart(act, z_stored[s], (t // 2) * 16 if isinstance(t, int) else t * 8 - 8 * s, act_turn)
                nc.scalar.activation(zS[:, s, :], PB[2 + s][:, 0:D + 2 * GH], ACT.Copy).then_inc(z_kept, 1)
                nc.scalar.activation(EM[:, ds(t, 1), :], PB[2 + s][:, D:D + 2 * GH].rearrange("p (a b) -> p a b", a=1), ACT.Copy).then_inc(z_kept, 1)
            over_pairs(act, (T - 1) // 2, 1, keep_z)

            act.wait_ge(z_kept, 2 * T)

            def index_columns(n, b3):
                nc.scalar.activation(IDX[:, b3, :], SRCT[:, ds(n * NS, NS)], ACT.Copy).then_inc(idx2_ready, 1)

            def dst_columns(n, b3):
                nc.scalar.activation(DLS[:, b3, :], DLT[:, ds(n * NS, NS)], ACT.Copy).then_inc(dls_ready, 1)
            for n in range(3):
                index_columns(n, n)
            for n in range(2):
                dst_columns(n, n)

            def expo(n, j, i):
                half, b3 = j % 2, j % 3
                act.wait_ge(expo_in, n + 1)
                if past(n, 2):
                    act.wait_ge(sum_ready, HALF * (n - 1))
                nc.scalar.activation(US[:, half * NS:(half + 1) * NS, D:ROW], sc[:, 0, :].rearrange("p (s h) -> p s h", h=GH), ACT.Exp).then_inc(expo_out, 1)
                wait_apart(act, rows2_in[b3], 16 * NS * (2 * i + j // 3 + 1), act_turn)
                if not (isinstance(n, int) and n + 3 >= BODIES):
                    index_columns(n + 3, b3)
                act.wait_ge(expo_out, n + 1)
                for s in range(NS - SUB, NS):
                    for h in range(GH):
                        c = slice(h * GO, (h + 1) * GO)
                        last = nc.scalar.activation(US[:, half * NS + s, c], ROWS2[b3][:, s, c], ACT.Copy, scale=US[:, half * NS + s, D + h:D + h + 1])
                last.then_inc(act_scaled, 1)
                if not (isinstance(n, int) and n + 2 >= BODIES):
                    if past(n, 1):
                        wait_apart(act, onehot2_ready, NS * n, act_turn)
                    dst_columns(n + 2, (b3 + 2) % 3)
            over(act, BODIES, 6, expo)

            act.wait_ge(veps_ready, 4)
            nc.scalar.sqrt(RS[:, :], RS[:, :]).then_inc(sqrt_ready, 1)

            def slice_copies(t, s, warm):
                act.wait_ge(t3_turned, t + 1)
                if warm:
                    act.wait_ge(l_ready, t - 1)
                nc.scalar.activation(TT[:, s, :, :], PB[s][:, 0:D].rearrange("p (k n) -> p k n", k=KC), ACT.Copy).then_inc(t3_kept, 1)
                act.wait_ge(l_less, t + 1)
                nc.scalar.activation(SWS[:, s, :], SWS[:, s, :], ACT.Exp).then_inc(l_exp, 1)
                if not (isinstance(t, int) and t == 0):
                    keep_sw(t - 1, 1 - s)

            def keep_sw(t, s):
                wait_apart(act, sw_turned, t + 1, act_turn)
                nc.scalar.activation(SWT[:, ds(t, 1), :, :].rearrange("p a q n -> p a (q n)"), PB[4 + s][:, :].rearrange("p (a n) -> p a n", a=1), ACT.Copy).then_inc(sw_kept, 1)
            over_pairs(act, (T - 1) // 2, 1, slice_copies)
            keep_sw(T - 1, 0)
            act.wait_ge(tok_dve, 5)
            nc.scalar.activation(AT, AT, ACT.Exp).then_inc(tok_exp, 1)
            act.wait_ge(tok_dve, 9)
            act.wait_ge(sw_kept, T)

            def stage_sw(t, s, warm):
                if warm:
                    wait_apart(act, mix_ready, t - 1, act_turn)
                nc.scalar.activation(SWS[:, s:s + 1, :], SWT[:, ds(t, 1), :, :].rearrange("p a q n -> p a (q n)"), ACT.Copy).then_inc(swt_staged, 1)
            over_pairs(act, (T - 1) // 2, 1, stage_sw)

        @block.tensor
        def _(pe):
            pe.wait_ge(consts_ready, 1)
            pe.wait_ge(lastf_ready, 1)
            h = NBP // 2
            for i in range(2):
                last = nc.tensor.matmul(PB[i][:, 0:h], ones[0:1, :], lastF[0:1, i * h:(i + 1) * h], start=True, stop=True)
            last.then_inc(lastrow_ready, 1)
            pe.wait_ge(tcmp_ready, 1)
            hk = GC * P // 2
            for i in range(2):
                nc.tensor.matmul(PB[2 + i][:, 0:hk], ones[0:T - 1, :], tcmp[:, i * hk:(i + 1) * hk], start=True, stop=True)
            for j in range(GC):
                last = nc.tensor.matmul(PB[4][:, j:j + 1], tcmp[:, j * P:(j + 1) * P], ones[0:T - 1, 0:1], start=True, stop=True)
            last.then_inc(tk_psum, 1)
            for j in range(GC):
                pe.wait_ge(tabf_ready, j + 1)
                if j >= 2:
                    pe.wait_ge(tab_kept, 3 * (j - 1))
                for a in range(3):
                    pb = PB[5 + (j % 2)] if a < 2 else PB[7]
                    o0 = (a % 2) * 256 if a < 2 else (j % 2) * 256
                    if a == 2 and j >= 1:
                        pe.wait_ge(tab_kept, 3 * j)
                    for b in range(SUB):
                        last = nc.tensor.transpose(pb[:, o0 + b * P:o0 + (b + 1) * P], tf[:, j % 2, a, b * P:(b + 1) * P], ident[:, :])
                last.then_inc(tab_turned, 1)

            def turn(src_t, ready, per, kept, turned):
                def f(t, s, warm):
                    pe.wait_ge(ready, (t + 1) * per)
                    if warm:
                        pe.wait_ge(kept, t - 1)
                    for k in range(KC):
                        last = nc.tensor.transpose(PB[s][:, k * P:(k + 1) * P], src_t[:, s, k * P:(k + 1) * P], ident[:, :])
                    last.then_inc(turned, 1)
                return f
            over_pairs(pe, (T - 1) // 2, 1, turn(HS, h_ready, 1, h_kept, h_turned))
            pe.wait_ge(h_kept, T)

            def edge_sum(n, j, i):
                pe.wait_ge(rows_in[j], (i + 1) * NU * 16)
                for g in range(UG):
                    gi = n * UG + g
                    pe.wait_ge(onehot_ready, (gi + 1) * 2 * SUB)
                    if past(n, 1):
                        pe.wait_ge(part_added, gi - 1)
                    for k in range(KC):
                        for b in range(SUB):
                            nc.tensor.matmul(PB[g][:, k * P:(k + 1) * P], GU[:, j * NU + g * SUB + b, k * P:(k + 1) * P],
                                             S[:, g, b, :], start=(b == 0), stop=(b == SUB - 1))
                    for b in range(SUB):
                        last = nc.tensor.matmul(PB[g][:, 256:384], onesb[:, :], S1[:, g, b, :], start=(b == 0), stop=(b == SUB - 1))
                    last.then_inc(part_ready, 1)
            over(pe, UNITS, 4, edge_sum)
            pe.wait_ge(part_added, GROUPS)

            pe.wait_ge(par_in, 16 * NPAR)
            for q in range(2):
                base = q * KC * (CHUNKS + 1)

                def lin(c, s, warm, n=512):
                    if q:
                        pe.wait_ge(relu_ready, KC * (c + 1))
                    for f in range(KC):
                        if warm:
                            pe.wait_ge(lin_kept, base + KC * (c - 2) + f + 1)
                            pe.wait_ge(lin_stat, base + KC * (c - 2) + f + 1)
                        for k in range(KC):
                            if n == 512:
                                r = YD[:, ds(c * 4, 4), k, :]
                                o = PB[2 * s + f][:, :].rearrange("p (t n) -> p t n", n=P)
                            else:
                                r, o = YD[:, T - 1, k, 0:n], PB[2 * s + f][:, 0:n]
                            last = nc.tensor.matmul(o, w12[:, q, k, f * P:(f + 1) * P], r, start=(k == 0), stop=(k == KC - 1))
                        last.then_inc(lin_ready, 1)
                if q:
                    pe.wait_ge(lin_kept, base)
                over_pairs(pe, CHUNKS // 2, 0, lin)
                lin(CHUNKS, 0, True, LAST)
            pe.wait_ge(lin_kept, 2 * KC * (CHUNKS + 1))
            over_pairs(pe, (T - 1) // 2, 1, turn(HS, r_ready, 2, x1_ready, r_turned))

            pe.wait_ge(x1_ready, T)
            def turn_sum(t, s, warm):
                pe.wait_ge(t1_ready, t + 1)
                if warm:
                    pe.wait_ge(t1_kept, t - 1)
                for k in range(KC):
                    nc.tensor.transpose(PB[s][:, k * P:(k + 1) * P], HS[:, s, k * P:(k + 1) * P], ident[:, :])
                end = isinstance(t, int) and t == T - 1
                for k in range(KC):
                    last = nc.tensor.matmul(PB[2 + k][:, 0:1], HS[:, s, k * P:(k + 1) * P], valid[:, 1:2] if end else valid[:, 0:1],
                                            start=(isinstance(t, int) and t == 0), stop=end)
                last.then_inc(t1_turned, 1)
            over_pairs(pe, (T - 1) // 2, 1, turn_sum)
            pe.wait_ge(t1_turned, T)
            pe.sem_inc(sums_ready, 1)
            pe.wait_ge(msb_ready, KC)
            for k in range(KC):
                last = nc.tensor.matmul(PB[4][:, 0:NX], MSB[:, k, :], wr[:, k, :], start=(k == 0), stop=(k == KC - 1))
            last.then_inc(logits_ready, 1)
            pe.wait_ge(chosen, 2)
            for j in range(3):
                last = nc.tensor.transpose(PB[6][0:NX, j * P:(j + 1) * P], ohs[:, j, :], ident[:, :])
            last.then_inc(ohs_turned, 1)
            pe.wait_ge(ohT_ready, 1)
            for j in range(TOPK):
                for q in range(FQ):
                    nc.tensor.matmul(PB[5][:, j * FQ + q:j * FQ + q + 1], b1s[:, q * P:(q + 1) * P], ohT[:, j, 0:1], start=True, stop=True)
            nc.tensor.matmul(PB[7][:, 0:D], ohT[:, 2, :], b2s[:, :], start=True, stop=True).then_inc(b_picked, 1)
            pe.wait_ge(b_kept, 1)
            pe.wait_ge(ew_ready, TOPK)
            pe.wait_ge(t1_kept, T)

            def experts(c, s, warm, n=512):
                warm = warm or s == 1
                for j in range(TOPK):
                    for q in range(FQ):
                        if warm or j:
                            pe.wait_ge(gelu_ready, (TOPK * c + j - 1) * FQ + q + 1)
                        for k in range(KC):
                            last = nc.tensor.matmul(PB[q][:, 0:n], EW1[:, j, k, q * P:(q + 1) * P], T1T[:, k, ds(c * 512, n)],
                                                    start=(k == 0), stop=(k == KC - 1))
                        last.then_inc(s1_ready, 1)
                for j in range(TOPK):
                    pe.wait_ge(gelu_ready, (TOPK * c + j + 1) * FQ)
                    for m in range(n // P):
                        if warm and j == 0:
                            pe.wait_ge(moe_kept, 4 * (c - 1) + m + 1)
                        for q in range(FQ):
                            last = nc.tensor.matmul(PB[4 + m][:, 0:D], HID[:, j, q, m * P:(m + 1) * P], EW2[:, j, q, :],
                                                    start=(j == 0 and q == 0), stop=(j == 1 and q == FQ - 1))
                        if j == TOPK - 1:
                            last.then_inc(moe_ready, 1)
                        elif m == n // P - 1:
                            last.then_inc(hid_used, 1)
                pe.wait_ge(moe_ready, 4 * c + n // P)
                pe.sem_inc(hid_used, 1)
            over_pairs(pe, CHUNKS // 2, 0, experts)
            experts(CHUNKS, 0, True, P)

            def project(t, s, warm):
                pe.wait_ge(t2_ready, t + 1)
                if warm:
                    pe.wait_ge(t2_kept, t - 1)
                for k in range(KC):
                    last = nc.tensor.transpose(PB[s][:, k * P:(k + 1) * P], HS[:, s, k * P:(k + 1) * P], ident[:, :])
                last.then_inc(t2_turned, 1)
                pe.wait_ge(t2_kept, t + 1)
                if warm:
                    pe.wait_ge(z_kept, 2 * (t - 1))
                for k in range(KC):
                    last = nc.tensor.matmul(PB[2 + s][:, 0:D + 2 * GH], TT[:, s, k, :], WZ[:, k, :], start=(k == 0), stop=(k == KC - 1))
                last.then_inc(z_ready, 1)
            pe.wait_ge(gelu_ready, TOPK * FQ * (CHUNKS + 1))
            over_pairs(pe, (T - 1) // 2, 1, project)

            pe.wait_ge(gm_step, 1)
            pe.wait_ge(z_kept, 2 * T)
            nc.tensor.transpose(PB[4][0:GH, 0:P], gm[:, :], ident[:, :]).then_inc(gm_turned, 1)
            pe.wait_ge(gm_step, 2)
            nc.tensor.matmul(PB[4][:, 0:GH], ones[0:GH, :], gm4[:, 1:1 + GH], start=True, stop=True).then_inc(gm_spread, 1)
            pe.wait_ge(em_ready, 1)

            def spread(gi, half, g, tk):
                pe.wait_ge(st_ready, gi + 1)
                for b in range(SUB):
                    c = g * SUB + b
                    for i in range(3):
                        last = nc.tensor.matmul(PB[2 + half][:, c * 2 * GH:(c + 1) * 2 * GH].rearrange("p (a v) -> p a v", a=1), ST[:, g, b * P:(b + 1) * P],
                                                EM3[:, ds(tk, 1), i, :], start=(i == 0), stop=(i == 2))
                last.then_inc(edm_ready, 1)

            def tiles_of(lo, k, engine):
                _, v = nc.values_load_multi_w_load_instructions(TK[0:1, ds(lo, k)], [engine], min_val=0, max_val=T - 1,
                                                                    skip_runtime_bounds_check_because=IN_RANGE)
                return v
            v = tiles_of(0, HALF, mybir.EngineType.PE)
            for g in range(HALF):
                spread(g, 0, g, v[g])
            v = tiles_of(HALF, HALF, mybir.EngineType.PE)
            for g in range(HALF):
                spread(HALF + g, 1, g, v[g])

            def weighted_sum(n, j, i):
                half = j % 2
                more = not (isinstance(n, int) and n + 2 >= BODIES)
                if more:
                    v = tiles_of((n + 2) * HALF, HALF, mybir.EngineType.PE)
                for g in range(HALF):
                    gi = n * HALF + g
                    pe.wait_ge(onehot2_ready, SUB * (gi + 1))
                    if g < HALF - 1:
                        pe.wait_ge(us_ready, (HALF - 1) * n + g + 1)
                    else:
                        pe.wait_ge(act_scaled, n + 1)
                    if past(n, 1):
                        pe.wait_ge(sum_added, gi - HALF + 1)
                    for b in range(SUB):
                        last = nc.tensor.matmul(SUMS[g][:, 0:ROW], SR[g][:, b, :], US[:, half * NS + g * SUB + b, :], start=(b == 0), stop=(b == SUB - 1))
                    last.then_inc(sum_ready, 1)
                    if g >= 2 and more:
                        if g == 2:
                            pe.wait_ge(edm_used, n + 1)
                        for m in range(2 * g - 4, 2 * g - 2):
                            spread((n + 2) * HALF + m, half, m, v[m])
            over(pe, BODIES, 6, weighted_sum)

            pe.wait_ge(slp_turn, 1)
            for k in range(KC):
                for q in range(PAIRS):
                    nc.tensor.matmul(PB[4 + k][:, q * P:(q + 1) * P], WXT[:, q, k * P:(k + 1) * P], WBD[:, 0, :], start=True, stop=True)
            for q in range(PAIRS):
                last = nc.tensor.matmul(PB[6][:, q * P:(q + 1) * P], bxB[:, q, :], WBD[:, 0, :], start=True, stop=True)
            last.then_inc(wsl_psum, 1)
            pe.wait_ge(wsl_ready, 1)

            def slice_logits(t, s, warm):
                pe.wait_ge(t3_ready, t + 1)
                if warm:
                    pe.wait_ge(t3_kept, t - 1)
                for k in range(KC):
                    last = nc.tensor.transpose(PB[s][:, k * P:(k + 1) * P], HS[:, s, k * P:(k + 1) * P], ident[:, :])
                last.then_inc(t3_turned, 1)
                pe.wait_ge(t3_kept, t + 1)
                if warm:
                    pe.wait_ge(l_kept, t - 1)
                for k in range(KC):
                    last = nc.tensor.matmul(PB[2 + s][:, :], TT[:, s, k, :], WSL[:, k, :], start=(k == 0), stop=(k == KC - 1))
                last.then_inc(l_ready, 1)
                if not (isinstance(t, int) and t == 0):
                    tokens(t - 1, 1 - s, warm, P)

            def tokens(t, s, warm, np_):
                first, end = isinstance(t, int) and t == 0, np_ < P
                pe.wait_ge(sw_ready, t + 1)
                for k in range(KC):
                    nc.tensor.matmul(PB[6 + k][:, :], HS[0:np_, s, k * P:(k + 1) * P], SWS[0:np_, s, :], start=first, stop=end)
                if not isinstance(t, int) or t >= 2:
                    pe.wait_ge(sw_kept, t - 1)
                for q in range(PAIRS):
                    last = nc.tensor.transpose(PB[4 + s][:, q * P:(q + 1) * P], SWS[:, s, q * P:(q + 1) * P], ident[:, :])
                last.then_inc(sw_turned, 1)
            over_pairs(pe, (T - 1) // 2, 1, slice_logits)
            tokens(T - 1, 0, True, LAST)

            pe.wait_ge(sw_summed, T + 1)
            pe.wait_ge(t3_kept, T)
            pe.wait_ge(l_kept, T)
            for q in range(PAIRS):
                nc.tensor.matmul(PB[0][:, q:q + 1], SWsum[:, q * P:(q + 1) * P], ones[:, 0:1], start=True, stop=True)
            nc.tensor.matmul(PB[1][0:1, :], ones[:, 0:1], SWsum, start=True, stop=True).then_inc(tok_pe, 1)
            pe.wait_ge(tok_dve, 1)
            for q in range(PAIRS):
                c = slice(q * P, (q + 1) * P)
                for k in range(KC):
                    nc.tensor.matmul(PB[2][:, c], XS[:, k, c], WFX[:, k, c], start=(k == 0), stop=False)
                last = nc.tensor.matmul(PB[2][:, c], nrow[:, c], bfx[:, c], start=False, stop=True)
            last.then_inc(tok_pe, 1)
            pe.wait_ge(tok_dve, 2)
            for q in range(PAIRS):
                last = nc.tensor.transpose(PB[3][:, q * P:(q + 1) * P], STK[:, q, :], ident[:, :])
            last.then_inc(tok_pe, 1)
            pe.wait_ge(tok_dve, 3)
            pe.wait_ge(sw_kept, T)
            for i in range(2):
                nc.tensor.matmul(PB[4 + i][:, :], WBD[:, 1 + i, :], STT.rearrange("p q n -> p (q n)"), start=True, stop=True)
            for q in range(PAIRS):
                last = nc.tensor.matmul(PB[6][:, q * P:(q + 1) * P], STT[:, q, :], WBD[:, 3, :], start=True, stop=True)
            last.then_inc(tok_pe, 1)
            pe.wait_ge(tok_dve, 4)
            for q in range(PAIRS):
                last = nc.tensor.matmul(PB[7][:, q * P:(q + 1) * P], QT[:, q, :], KT[:, q, :], start=True, stop=True)
            last.then_inc(tok_pe, 1)
            pe.wait_ge(tok_dve, 6)
            for q in range(PAIRS):
                last = nc.tensor.transpose(PB[0][:, q * P:(q + 1) * P], AT[:, q, :], ident[:, :])
            last.then_inc(tok_pe, 1)
            pe.wait_ge(tok_dve, 7)
            for q in range(PAIRS):
                last = nc.tensor.matmul(PB[1][:, q * P:(q + 1) * P], VS[:, q, :], ATT[:, q, :], start=True, stop=True)
            last.then_inc(tok_pe, 1)
            pe.wait_ge(tok_dve, 8)
            for q in range(PAIRS):
                last = nc.tensor.matmul(PB[2 + q // 2][:, (q % 2) * D:(q % 2 + 1) * D], OST[:, q, :], WOUT[:, q, :], start=True, stop=True)
            last.then_inc(tok_pe, 1)
            pe.wait_ge(tok_dve, 9)

            def mix(t, s, warm):
                pe.wait_ge(swt_staged, t + 1)
                if warm:
                    pe.wait_ge(fin_ready, t - 1)
                for q in range(PAIRS):
                    last = nc.tensor.matmul(PB[4 + s][:, 0:D], SWS[:, s, q * P:(q + 1) * P], VV[:, q, :], start=(q == 0), stop=(q == PAIRS - 1))
                last.then_inc(mix_ready, 1)
            over_pairs(pe, (T - 1) // 2, 1, mix)


_INS = ["x", "src", "dst", "edge_weight", "L0_gnn_w1", "L0_gnn_w2", "L0_gnn_gamma1", "L0_gnn_beta1", "L0_gnn_eps_weight",
        "L0_gnn_gamma_h", "L0_gnn_beta_h", "L0_ffn_Wr", "L0_ffn_br", "L0_ffn_W1", "L0_ffn_b1", "L0_ffn_W2", "L0_ffn_b2",
        "L0_ffn_gamma", "L0_ffn_beta", "L1_gnn_W", "L1_gnn_a_src", "L1_gnn_a_dst", "L1_ffn_W_fx", "L1_ffn_b_fx",
        "L1_ffn_W_x", "L1_ffn_b_x", "L1_ffn_W_slice", "L1_ffn_b_slice", "L1_ffn_W_q", "L1_ffn_W_k", "L1_ffn_W_v",
        "L1_ffn_W_out", "L1_ffn_b_out", "L1_ffn_temperature"]
_TURNED = ("L0_gnn_w1", "L0_gnn_w2", "L1_ffn_W_x")


def kernel(**inputs):
    import numpy as _np
    import concourse.bacc as _bacc
    from concourse import mybir as _mybir
    from concourse.bass_utils import run_bass_kernel_spmd as _run

    nc = _bacc.Bacc("TRN2", target_bir_lowering=False, num_devices=1)
    pad = {"src": (NBP * BLK - E, 0), "dst": (NBP * BLK - E, NODST), "edge_weight": (NBP * BLK - E, 0)}
    arrays, args = {}, []
    for name in _INS:
        a = _np.asarray(inputs[name])
        if name in pad:
            a = _np.concatenate([a, _np.full((pad[name][0],), pad[name][1], a.dtype)])
        if name == "x":
            a = _np.concatenate([a, _np.zeros((T * P - N, D), a.dtype)])
        if name in _TURNED:
            a = a.T
        a = _np.ascontiguousarray(a)
        arrays[f"in_{name}_dram"] = a
        args.append(nc.dram_tensor(f"in_{name}_dram", a.shape, _mybir.dt.from_np(a.dtype), kind="ExternalInput").ap())
    args.append(nc.dram_tensor("out_0_dram", (N, D), _mybir.dt.float32, kind="ExternalOutput").ap())
    build(nc, *args)
    r = _run(nc, [arrays], core_ids=[0])
    return r.results[0]["out_0_dram"]
```

```python
import concourse.bass as bass
from concourse import mybir
from contextlib import ExitStack

P = 128
N, D, E = 6250, 256, 200000
KC = D // P
T = -(-N // P)
LAST = N - (T - 1) * P
BLK = 256
SUB = BLK // P
HALF = 4
NB = -(-E // BLK)
GROUPS = -(-(NB + T - 1) // (2 * HALF)) * 2 * HALF
GC = -(-GROUPS // P)
NBP = NB + GROUPS - (NB + T - 1)
NODST = 1 << 20
NS = HALF * SUB
BODIES = GROUPS // HALF
IN_RANGE = "a tile's number counts T - 1 comparisons, so that it lies in 0 ... T - 1 for any edges"
SPREAD = 40.0
MSTEPS = 6
LAG = 2
UG = 2
UNITS = GROUPS // UG
NU = UG * SUB
NPAR = 17
NX = 8
F1 = 512
TOPK = 2
CAP = float(-(-N * 5 // (4 * NX)))
GH, GO = 4, 64
ROW = D + GH
SH, SG = 8, 64
INNER = SH * 64
PAIRS = SH // 2
EPS = 1e-5
CHUNKS = (T - 1) // 4


def over_pairs(eng, pairs, tail, body):
    body(0, 0, False)
    body(1, 1, False)
    with eng.Fori(1, pairs) as i:
        for u in range(2):
            body(i * 2 + u, u, True)
    for t in range(2 * pairs, 2 * pairs + tail):
        body(t, t % 2, True)


def over(eng, total, unroll, body, peel=0):
    for n in range(unroll):
        body(n, n, 0)
    with eng.Fori(1, total // unroll - peel) as i:
        for j in range(unroll):
            body(i * unroll + j, j, i)
    for n in range((total // unroll - peel) * unroll, total):
        body(n, n % unroll, n // unroll)


def of_slot(j, slots):
    return (T - 1 - j) // slots + 1


def past(n, k):
    return not isinstance(n, int) or n >= k


def before(n, k):
    return not isinstance(n, int) or n < k


def wait_apart(eng, sem, value, turn):
    eng.wait_ge(sem, value)
    eng.sem_inc(turn, 1)


class Chain:

    def __init__(self, eng, sem):
        self.eng, self.sem, self.at = eng, sem, 0

    def __call__(self, ins):
        ins.then_inc(self.sem, 1)
        self.at = self.at + 1
        self.eng.wait_ge(self.sem, self.at)


def build(nc, x, src, dst, ew, w1T, w2T, gamma1, beta1, epsw, gamma_h, beta_h,
          Wr, br, W1, b1, W2, b2, gamma, beta, gW, ga_src, ga_dst,
          W_fx, b_fx, W_xT, b_x, W_slice, b_slice, W_q, W_k, W_v, W_out, b_out, temperature, out):
    fp32, bf16, i32 = mybir.dt.float32, mybir.dt.bfloat16, mybir.dt.int32
    ALU, ACT, AX = mybir.AluOpType, mybir.ActivationFunctionType, mybir.AxisListType
    ds = bass.ds

    hTab = nc.dram_tensor("hTab", (T * P, D), fp32, kind="Internal").ap()
    zTab = nc.dram_tensor("zTab", (T * P, ROW), fp32, kind="Internal").ap()
    dlTab = nc.dram_tensor("dlTab", (GC * P, BLK), fp32, kind="Internal").ap()

    ctx = ExitStack()
    with ctx:
        ctx.enter_context(nc.allow_non_contiguous_dma("small parameters and strided rows"))

        def sb(name, shape, dt=fp32):
            return ctx.enter_context(nc.sbuf_tensor(name, shape, dt))

        def sem(name):
            return ctx.enter_context(nc.semaphore(name))

        PB = [ctx.enter_context(nc.psum_tensor(f"PB{i}", [P, 512], fp32)) for i in range(8)]

        XH = sb("XH", [P, T, D])
        ARENA = T * 512
        A = sb("A", [P, ARENA])
        YD = A[:, 0:T * 384].rearrange("p (t c n) -> p t c n", c=3, n=P)
        tab = ARENA - 3 * GC * BLK
        WT = A[:, tab:tab + GC * BLK]
        DLT = A[:, tab + GC * BLK:tab + 2 * GC * BLK]
        SRCT = A[:, tab + 2 * GC * BLK:tab + 3 * GC * BLK].bitcast(i32)
        G = sb("G", [P, 2 * NS * ROW])
        GU = G[:, 0:4 * NU * D].rearrange("p (s r) -> p s r", r=D)
        GR = G[:, :].rearrange("p (s r) -> p s r", r=ROW)
        tg = G[:, 0:2 * 3 * BLK].rearrange("p (s a e) -> p s a e", s=2, a=3)
        tf = G[:, 2 * 3 * BLK:4 * 3 * BLK].rearrange("p (s a e) -> p s a e", s=2, a=3)
        TK = sb("TK", [P, GC * P], i32)
        S = sb("S", [P, 2, SUB, P])
        STF = sb("STF", [P, 2 * BLK])
        ST = STF[:, :].bitcast(bf16).rearrange("p (s e) -> p s e", s=HALF)
        iint = STF[:, 0:P].bitcast(i32)
        EM3 = sb("EM3", [P, T, 3, 2 * GH], bf16)
        S1 = A[:, T * 384:T * 384 + SUB * P].bitcast(bf16).rearrange("p (g b n) -> p g b n", g=2, b=SUB)
        IDX = sb("IDX", [P, 3, NS], i32)
        DLS = sb("DLS", [P, 3, NS])
        WS = sb("WS", [P, 4 * NU])
        IDXU, DLU = (b[:, :, :].rearrange("p a b -> p (a b)") for b in (IDX, DLS))
        ident = sb("ident", [P, P])
        iota = sb("iota", [P, P])
        iotap = sb("iotap", [P, 1])
        ipint = sb("ipint", [P, 1], i32)
        ones = sb("ones", [P, P])
        onesb = sb("onesb", [P, P], bf16)
        work = A[:, 0:2048]
        lastI = A[0:1, 3072:3072 + NBP].bitcast(i32)
        lastF = A[0:1, 4096:4096 + NBP]
        cmp = work[0:T - 1, 0:NBP]
        kki = work[:, 1024:1024 + GC * P].bitcast(i32)
        kk = A[:, 2048:2048 + GC * P]
        tcmp = work[0:T - 1, 0:GC * P]
        thr = sb("thr", [P, 2])
        cols = sb("cols", [P, 5, GC])
        cidx = sb("cidx", [P, GC], i32)
        kci = sb("kci", [P, GC], i32)
        BS = sb("BS", [P, T, 6])
        MV = sb("MV", [P, T, 2])
        RS = sb("RS", [P, T])
        HS = sb("HS", [P, 2, D])
        HT = G[:, 2048:4096].rearrange("p (s d) -> p s d", d=D)
        R8 = G[:, 0:2048].rearrange("p (s k t n) -> p s k t n", s=2, k=KC, t=4)
        R4 = G[:, 0:1024].rearrange("p (s d) -> p s d", d=D)
        w12 = sb("w12", [P, 2, KC, D])
        bnp = sb("bnp", [P, 5, KC])
        BSF = sb("BSF", [P, KC, CHUNKS + 1, 6])
        MVF = sb("MVF", [P, KC, 2])
        bns = sb("bns", [P, 4, KC])

        T1T = A[:, 0:KC * T * P].rearrange("p (k n) -> p k n", k=KC)
        ew0 = KC * T * P
        EW1 = A[:, ew0:ew0 + TOPK * KC * F1].rearrange("p (j k f) -> p j k f", j=TOPK, k=KC)
        FQ = F1 // P
        ew1 = ew0 + TOPK * KC * F1
        EW2 = A[:, ew1:ew1 + TOPK * FQ * D].rearrange("p (j q d) -> p j q d", j=TOPK, q=FQ)
        HID = G[:, 0:TOPK * FQ * 512].rearrange("p (j q n) -> p j q n", j=TOPK, q=FQ)
        ms = sb("ms", [P, KC])
        MSB = sb("MSB", [P, KC, P])
        wr = sb("wr", [P, KC, NX])
        rt = sb("rt", [P, 16, NX])
        r1 = sb("r1", [P, 16])
        ohs = sb("ohs", [P, 3, NX])
        ohT = sb("ohT", [NX, 3, P])
        emul = sb("emul", [P, 6])
        ebase = sb("ebase", [P, 6])
        EI = sb("EI", [P, TOPK, 6], i32)
        b1s = A[0:NX, T * 384 + SUB * P:T * 384 + SUB * P + F1]
        b2s = sb("b2s", [NX, D])
        b1c = sb("b1c", [P, TOPK * FQ])
        B2M = sb("B2M", [P, D])
        rows4 = sb("rows4", [P, 4, D])
        gbB, aB = rows4[:, 0:2, :], rows4[:, 2:4, :]
        nmr = sb("nmr", [P, T])
        rs1 = sb("rs1", [P, T])
        vst = sb("vst", [P, 2, 6])
        vmv = sb("vmv", [P, 2, 2])
        vrs = sb("vrs", [P, 2])
        mhalf = sb("mhalf", [P, 1])
        WZ = sb("WZ", [P, KC, D + 2 * GH])
        zS = sb("zS", [P, 2, D + 2 * GH])
        Z4 = G[:, 1024:1024 + 4 * (D + 2 * GH)].rearrange("p (s r) -> p s r", s=4)
        TT = sb("TT", [P, 2, KC, P])
        EM = sb("EM", [P, T, 2 * GH])

        H2 = A[:, 0:T * ROW].rearrange("p (t r) -> p t r", r=ROW)
        us0 = T * ROW
        US = A[:, us0:us0 + 2 * NS * ROW].rearrange("p (s r) -> p s r", r=ROW)
        rb0 = us0 + 2 * NS * ROW
        ROWB = A[:, rb0:rb0 + 2 * HALF * BLK].rearrange("p (s g e) -> p s g e", s=2, g=HALF)
        r20 = rb0 + 2 * HALF * BLK
        GR2 = A[:, r20:r20 + NS * ROW].rearrange("p (s r) -> p s r", r=ROW)
        ROWS2 = [GR[:, 0:NS, :], GR[:, NS:2 * NS, :], GR2]
        SR = [S[:, 0, :, :], S[:, 1, :, :]] + [w12[:, 0, i, :].rearrange("p (b n) -> p b n", b=SUB) for i in range(2)]
        SUMS = [PB[0], PB[1], PB[4], PB[5]]
        sc = sb("sc", [P, 4, NS * GH])
        scn = sb("scn", [P, NS, 2 * GH])
        gm = sb("gm", [P, 2 * GH])
        gm4 = sb("gm4", [2 * GH, 1 + 2 * GH])
        wide = sb("wide", [P, 1], i32)
        mrow, moh, mout = G[:, 0:ROW], G[:, 512:512 + P], G[:, 640:640 + P]
        msc = G[:, 1024:1024 + GH * P].rearrange("p (h n) -> p h n", h=GH)
        mmax = G[:, 1536:1536 + GH]
        RD = sb("RD", [P, T, GH])

        SWT = A[:, :].rearrange("p (t q n) -> p t q n", q=PAIRS, n=P)
        WXT = A[:, ARENA - 1024:ARENA].rearrange("p (q k) -> p q k", q=PAIRS)
        WSL = G[:, 0:1024].rearrange("p (k f) -> p k f", k=KC)
        VV = G[:, 0:1024].rearrange("p (q d) -> p q d", q=PAIRS)
        BSL = G[:, 1024:1536]
        SWS = G[:, 1536:2560].rearrange("p (s f) -> p s f", s=2)
        SWsum = G[:, 2560:3072]
        T3 = ([G[:, 3072 + i * D:3072 + (i + 1) * D] for i in range(4)]
              + [HS[:, i, :] for i in range(2)] + [STF[:, i * D:(i + 1) * D] for i in range(2)])
        SW = [SWS[:, 0, :], SWS[:, 1, :], S[:, :, :, :].rearrange("p a b n -> p (a b n)"),
              zS[:, :, :].rearrange("p a b -> p (a b)")[:, 0:INNER]]
        XS = G[:, 3072:4096].rearrange("p (k f) -> p k f", k=KC)
        WFX = w12[:, :, :, :].rearrange("p a k f -> p (a k f)").rearrange("p (k f) -> p k f", k=KC)
        WOUT = rows4
        WBD = sb("WBD", [P, 4, P])
        bm = sb("bm", [P, 2, P])
        it = sb("it", [P, SH])
        bxc = sb("bxc", [P, PAIRS])
        bxB = S[:, :, :, :].rearrange("p a b n -> p (a b) n")
        bsB = MSB[:, 0, 0:SG]
        boutB = B2M
        bfx = EM3[0:1, :, :, :].rearrange("p t a v -> p (t a v)").bitcast(fp32)[:, 0:INNER]
        nrow = zS[0:1, :, :].rearrange("p a b -> p (a b)")[:, 0:INNER]
        sden = sb("sden", [P, PAIRS])
        ax = sb("ax", [P, 4, SH])
        q4 = [b[:, :, :, :].rearrange("p a b n -> p (a b) n") for b in (TT, S)]
        STK = STF[:, :].rearrange("p (b n) -> p b n", n=P)
        STT = HS[:, :, :].rearrange("p a (b n) -> p (a b) n", n=P)
        QT, KT = SWS[:, 0, :].rearrange("p (q n) -> p q n", n=P), SWS[:, 1, :].rearrange("p (q n) -> p q n", n=P)
        VS, AT = XS[:, 0, :].rearrange("p (q n) -> p q n", n=P), XS[:, 1, :].rearrange("p (q n) -> p q n", n=P)
        ATT, OST = q4

        x_in = [sem(f"x_in{i}") for i in range(4)]
        par_in = sem("par_in")
        last_in = sem("last_in")
        consts_ready = sem("consts_ready")
        pool_step = sem("pool_step")
        dve_step = sem("dve_step")
        act_step = sem("act_step")
        lastf_ready = sem("lastf_ready")
        lastrow_ready = sem("lastrow_ready")
        tcmp_ready = sem("tcmp_ready")
        tk_psum = sem("tk_psum")
        cidx_ready = sem("cidx_ready")
        tab_in = [sem(f"tab_in{i}") for i in range(2)]
        tabf_ready = sem("tabf_ready")
        tab_turned = sem("tab_turned")
        tab_kept = sem("tab_kept")
        dl_stored = sem("dl_stored")
        veps_ready = sem("veps_ready")
        sqrt_ready = sem("sqrt_ready")
        h_ready = sem("h_ready")
        h_stored = [sem(f"h_stored{i}") for i in range(8)]
        h_turned = sem("h_turned")
        h_kept = sem("h_kept")
        h_added = sem("h_added")
        rs1_ready = sem("rs1_ready")
        idx_ready = sem("idx_ready")
        rows_in = [sem(f"rows_in{i}") for i in range(4)]
        gather_turn = sem("gather_turn")
        act_turn = sem("act_turn")
        onehot_ready = sem("onehot_ready")
        part_ready = sem("part_ready")
        part_added = sem("part_added")
        lin_ready = sem("lin_ready")
        lin_stat = sem("lin_stat")
        lin_kept = sem("lin_kept")
        degmax = sem("degmax")
        degsqrt = sem("degsqrt")
        deg_ready = sem("deg_ready")
        deg_zero = sem("deg_zero")
        bn_var = sem("bn_var")
        bn_sqrt = sem("bn_sqrt")
        bn_ready = sem("bn_ready")
        relu_ready = sem("relu_ready")
        r_ready = sem("r_ready")
        r_turned = sem("r_turned")
        x1_ready = sem("x1_ready")
        out_stored = sem("out_stored")
        dve_turn = sem("dve_turn")
        t1_ready = sem("t1_ready")
        t1_turned = sem("t1_turned")
        t1_kept = sem("t1_kept")
        sums_ready = sem("sums_ready")
        msb_ready = sem("msb_ready")
        logits_ready = sem("logits_ready")
        exp_in = sem("exp_in")
        exp_out = sem("exp_out")
        chosen = sem("chosen")
        ohs_turned = sem("ohs_turned")
        ohT_ready = sem("ohT_ready")
        b_picked = sem("b_picked")
        b_kept = sem("b_kept")
        ew1_in = [sem(f"ew1_in{j}") for j in range(TOPK)]
        ew2_in = sem("ew2_in")
        ew_ready = sem("ew_ready")
        s1_ready = sem("s1_ready")
        gelu_ready = sem("gelu_ready")
        hid_used = sem("hid_used")
        moe_ready = sem("moe_ready")
        moe_kept = sem("moe_kept")
        var_ready = sem("var_ready")
        rs_ready = sem("rs_ready")
        v_ready = sem("v_ready")
        x2_ready = sem("x2_ready")
        x2_stat = sem("x2_stat")
        t2_ready = sem("t2_ready")
        t2_turned = sem("t2_turned")
        t2_kept = sem("t2_kept")
        z_ready = sem("z_ready")
        z_kept = sem("z_kept")
        em_ready = sem("em_ready")
        h2_zero = sem("h2_zero")
        gm_step = sem("gm_step")
        gm_turned = sem("gm_turned")
        gm_spread = sem("gm_spread")
        wide_ready = sem("wide_ready")
        mcol_ready = sem("mcol_ready")
        mrow_in = sem("mrow_in")
        msc_ready = sem("msc_ready")
        msc_turned = sem("msc_turned")
        mmax_step = sem("mmax_step")
        rowb_in = [sem(f"rowb_in{i}") for i in range(2)]
        idx2_ready = sem("idx2_ready")
        rows2_in = [sem(f"rows2_in{i}") for i in range(3)]
        dls_ready = sem("dls_ready")
        act_scaled = sem("act_scaled")
        st_ready = sem("st_ready")
        edm_ready = sem("edm_ready")
        edm_used = sem("edm_used")
        small_step = sem("small_step")
        expo_in = sem("expo_in")
        expo_out = sem("expo_out")
        us_ready = sem("us_ready")
        sum_ready = sem("sum_ready")
        sum_added = sem("sum_added")
        rd_ready = sem("rd_ready")
        h3_ready = sem("h3_ready")
        x3_ready = sem("x3_ready")
        onehot2_ready = sem("onehot2_ready")
        wbd_zero = sem("wbd_zero")
        par2_in = sem("par2_in")
        slp_turn = sem("slp_turn")
        wsl_psum = sem("wsl_psum")
        wsl_ready = sem("wsl_ready")
        t3_ready = sem("t3_ready")
        t3_turned = sem("t3_turned")
        t3_kept = sem("t3_kept")
        l_ready = sem("l_ready")
        l_kept = sem("l_kept")
        l_max = sem("l_max")
        l_less = sem("l_less")
        l_exp = sem("l_exp")
        sw_ready = sem("sw_ready")
        sw_turned = sem("sw_turned")
        sw_kept = sem("sw_kept")
        sw_summed = sem("sw_summed")
        tok_pe = sem("tok_pe")
        tok_dve = sem("tok_dve")
        tok_exp = sem("tok_exp")
        swt_staged = sem("swt_staged")
        mix_ready = sem("mix_ready")
        fin_ready = sem("fin_ready")
        z_stored = [sem(f"z_stored{i}") for i in range(4)]

        def tiles_of(lo, k, engine):
            _, v = nc.values_load_multi_w_load_instructions(TK[0:1, ds(lo, k)], [engine], min_val=0, max_val=T - 1,
                                                                skip_runtime_bounds_check_because=IN_RANGE)
            return v

        def load_wide(engine):
            _, v = nc.values_load_multi_w_load_instructions(wide[0:1, 0:1], [engine], min_val=0, max_val=1,
                                                            skip_runtime_bounds_check_because="a comparison gives 0 or 1")
            return v[0]

        block = ctx.enter_context(nc.Block())

        @block.sync
        def _(sp):
            xv = x[0:(T - 1) * P, :].rearrange("(t p) d -> p t d", p=P)
            sp.dma_start(lastI[:, :], dst.rearrange("(a b e) -> a b e", a=1, e=BLK)[:, :, BLK - 1]).then_inc(last_in, 16)
            for i in range(3):
                sp.dma_start(XH[:, 16 * i:16 * (i + 1), :], xv[:, 16 * i:16 * (i + 1), :]).then_inc(x_in[i], 16)
            sp.dma_start(XH[:, T - 1, :], x[(T - 1) * P:T * P, :]).then_inc(x_in[3], 16)
            sp.dma_start(w12[:, 0, :, :], w1T.rearrange("(k p) f -> p k f", p=P)).then_inc(par_in, 16)
            sp.dma_start(w12[:, 1, :, :], w2T.rearrange("(k p) f -> p k f", p=P)).then_inc(par_in, 16)
            for i, v in enumerate((gamma1, beta1, gamma_h, beta_h)):
                sp.dma_start(bnp[:, i, :], v.rearrange("(k p) -> p k", p=P)).then_inc(par_in, 16)
            sp.dma_start(bnp[:, 4, 0:1], epsw.rearrange("(a b) -> a b", a=1).broadcast_to((P, 1))).then_inc(par_in, 16)

            sp.dma_start(wr[:, :, :], Wr.rearrange("(k p) e -> p k e", p=P)).then_inc(par_in, 16)
            sp.dma_start(rt[:, 0, :], br.rearrange("(a b) -> a b", a=1).broadcast_to((P, NX))).then_inc(par_in, 16)
            sp.dma_start(b1s, b1).then_inc(par_in, 16)
            sp.dma_start(b2s[:, :], b2).then_inc(par_in, 16)
            sp.dma_start(gbB[:, 0, :], gamma.rearrange("(a b) -> a b", a=1).broadcast_to((P, D))).then_inc(par_in, 16)
            sp.dma_start(gbB[:, 1, :], beta.rearrange("(a b) -> a b", a=1).broadcast_to((P, D))).then_inc(par_in, 16)
            for k in range(KC):
                sp.dma_start(WZ[:, k, 0:D].rearrange("p (h o) -> p h o", h=GH), gW[:, k * P:(k + 1) * P, :].rearrange("h i o -> i h o")).then_inc(par_in, 16)
            sp.dma_start(aB[:, 0, :], ga_src.rearrange("(a h) o -> a (h o)", a=1).broadcast_to((P, D))).then_inc(par_in, 16)
            sp.dma_start(aB[:, 1, :], ga_dst.rearrange("(a h) o -> a (h o)", a=1).broadcast_to((P, D))).then_inc(par_in, 16)

            sp.wait_ge(wbd_zero, 1)
            for i, v in enumerate((W_slice, W_q, W_k, W_v)):
                for b in range(2):
                    sp.dma_start(WBD[b * SG:(b + 1) * SG, i, b * SG:(b + 1) * SG], v).then_inc(par2_in, 16)
            sp.dma_start(it[:, :], temperature.rearrange("a h b c -> (a b c) h").broadcast_to((P, SH))).then_inc(par2_in, 16)
            sp.dma_start(bxc[:, :], b_x.rearrange("(q p) -> p q", p=P)).then_inc(par2_in, 16)

            for j in range(GC):
                sp.wait_ge(tabf_ready, j + 1)
                sp.dma_start(dlTab[j * P:(j + 1) * P, :], tf[:, j % 2, 0, :]).then_inc(dl_stored, 16)
                sp.wait_ge(dl_stored, 16 * (j + 1))

            def store_h(t, j, i):
                sp.wait_ge(h_ready, t + 1)
                sp.dma_start(hTab[ds(t * P, P), :], HT[:, j, :]).then_inc(h_stored[j], 16)
            over(sp, T, 8, store_h)

            def store_z(t, j, i):
                sp.wait_ge(z_kept, 2 * (t + 1))
                sp.dma_start(zTab[ds(t * P, P), :], Z4[:, j, 0:ROW]).then_inc(z_stored[j], 16)
            over(sp, T, 4, store_z)

            def load_rows(n, half, warm):
                if warm:
                    sp.wait_ge(st_ready, HALF * (n - 1))
                else:
                    sp.wait_ge(z_kept, 2 * T)
                sp.dma_start(ROWB[:, half, :, :].rearrange("p g e -> p (g e)"),
                             dlTab[ds(n * HALF, HALF), :].rearrange("(a g) e -> a (g e)", a=1).broadcast_to((P, HALF * BLK))).then_inc(rowb_in[half], 16)
            over_pairs(sp, BODIES // 2, 0, load_rows)

            sp.wait_ge(sum_ready, GROUPS)
            sp.dma_start(WXT, W_xT.rearrange("(q p) k -> p q k", p=P)).then_inc(par2_in, 16)
            sp.dma_start(WFX, W_fx.rearrange("(k p) f -> p k f", p=P)).then_inc(par2_in, 16)
            sp.dma_start(WOUT[:, :, :], W_out.rearrange("(q p) d -> p q d", p=P)).then_inc(par2_in, 16)
            sp.dma_start(bfx, b_fx.rearrange("(a b) -> a b", a=1)).then_inc(par2_in, 16)
            sp.dma_start(bsB, b_slice.rearrange("(a b) -> a b", a=1).broadcast_to((P, SG))).then_inc(par2_in, 16)
            sp.dma_start(boutB[:, :], b_out.rearrange("(a b) -> a b", a=1).broadcast_to((P, D))).then_inc(par2_in, 16)

            def store(t, s, warm):
                sp.wait_ge(fin_ready, t + 1)
                if isinstance(t, int) and t == T - 1:
                    sp.dma_start(out[t * P:N, :], XH[0:LAST, t, :]).then_inc(out_stored, 16)
                else:
                    sp.dma_start(out[ds(t * P, P), :], XH[:, ds(t, 1), :].rearrange("p t d -> p (t d)")).then_inc(out_stored, 16)
            over_pairs(sp, (T - 1) // 2, 1, store)
            sp.wait_ge(out_stored, 16 * T)

        @block.gpsimd
        def _(pool):
            step = Chain(pool, pool_step)
            step(nc.gpsimd.memset(ident[:, :], 0.0))
            step(nc.gpsimd.affine_select(out=ident[:, :], in_=ident[:, :], compare_op=ALU.not_equal, fill=1.0,
                                         base=0, pattern=[[-1, P]], channel_multiplier=1))
            step(nc.gpsimd.iota(iint[:, :], [[1, P]], base=0, channel_multiplier=0))
            step(nc.gpsimd.iota(ipint[:, :], [[0, 1]], base=0, channel_multiplier=1))
            step(nc.gpsimd.iota(kki, [[1, GC * P]], base=0, channel_multiplier=0))
            step(nc.gpsimd.iota(kci[:, :], [[P, GC]], base=0, channel_multiplier=1))
            step(nc.gpsimd.tensor_copy(iota[:, :], iint[:, :]))
            step(nc.gpsimd.tensor_copy(iotap[:, :], ipint[:, :]))
            step(nc.gpsimd.tensor_copy(kk[:, :], kki))
            step(nc.gpsimd.tensor_copy(cols[:, 0, :], kci[:, :]))
            step(nc.gpsimd.memset(onesb[:, :], 1.0))
            step(nc.gpsimd.memset(ones[:, :], 1.0))
            step(nc.gpsimd.tensor_scalar(thr[:, 0:1], iotap[:, :], float(P), float(P), ALU.mult, ALU.add))
            pool.sem_inc(consts_ready, 1)
            step(nc.gpsimd.memset(mhalf[:, :], -0.5))
            step(nc.gpsimd.memset(WBD[:, :, :], 0.0))
            pool.sem_inc(wbd_zero, 1)
            step(nc.gpsimd.tensor_scalar(bm[:, 0, :], iota[:, :], float(SG), None, ALU.is_lt))
            step(nc.gpsimd.tensor_scalar(ms[:, 0:1], iotap[:, :], float(SG), None, ALU.is_lt))
            step(nc.gpsimd.tensor_scalar(bm[:, 0, :], bm[:, 0, :], ms[:, 0:1], None, ALU.is_equal))
            step(nc.gpsimd.tensor_scalar(bm[:, 1, :], bm[:, 0, :], 1.0, 1e30, ALU.subtract, ALU.mult))
            for q in range(6):
                k, m = (q, D) if q < KC else (q - KC, F1)
                step(nc.gpsimd.memset(emul[:, q:q + 1], float(m)))
                step(nc.gpsimd.tensor_scalar(ebase[:, q:q + 1], iotap[:, :], float(k * P), None, ALU.add))
            pool.sem_inc(consts_ready, 1)

            pool.wait_ge(cidx_ready, 1)
            for j in range(GC):
                if j >= 2:
                    pool.wait_ge(tabf_ready, j - 1)
                for a, arr in enumerate((dst, src, ew)):
                    o = tg[:, j % 2, a, :]
                    pool.indirect_dma_start(o if a == 2 else o.bitcast(i32), None,
                                            arr.rearrange("(b e) -> b e", e=BLK),
                                            bass.IndirectOffsetOnAxis(ap=cidx[:, j:j + 1], axis=0)).then_inc(tab_in[j % 2], 16)

            nc.gpsimd.memset(YD[:, :, 2, :], 0.0).then_inc(deg_zero, 1)

            for j in range(8):
                pool.wait_ge(h_stored[j], 16 * of_slot(j, 8))
            pool.wait_ge(h_turned, T)

            def gather(n, j, i):
                pool.wait_ge(idx_ready, n + 1)
                if past(n, 4):
                    pool.wait_ge(part_ready, UG * (n - 3))
                pool.sem_inc(gather_turn, 1)
                for s in range(NU):
                    pool.indirect_dma_start(GU[:, j * NU + s, :], None, hTab,
                                            bass.IndirectOffsetOnAxis(ap=IDXU[:, j * NU + s:j * NU + s + 1], axis=0)).then_inc(rows_in[j], 16)
            over(pool, UNITS, 4, gather)

            pool.wait_ge(rs1_ready, 1)

            for op, c in ((ALU.mult, rs1), (ALU.add, nmr)):
                step(nc.gpsimd.tensor_tensor(XH[:, :, :], XH[:, :, :], c[:, :].rearrange("p (t a) -> p t a", a=1).broadcast_to((P, T, D)), op))
            pool.sem_inc(h_added, 1)

            pool.wait_ge(chosen, 1)
            for j in range(TOPK):
                for q in range(KC):
                    pool.indirect_dma_start(EW1[:, j, q, :], None, W1.rearrange("e r c -> (e r) c"),
                                            bass.IndirectOffsetOnAxis(ap=EI[:, j, q:q + 1], axis=0)).then_inc(ew1_in[j], 16)
            for j in range(TOPK):
                for q in range(FQ):
                    pool.indirect_dma_start(EW2[:, j, q, :], None, W2.rearrange("e r c -> (e r) c"),
                                            bass.IndirectOffsetOnAxis(ap=EI[:, j, KC + q:KC + q + 1], axis=0)).then_inc(ew2_in, 16)

            def finish(t, s):
                pool.wait_ge(var_ready, t + 1)
                nc.gpsimd.tensor_tensor(vrs[:, s:s + 1], vrs[:, s:s + 1], mhalf[:, :], ALU.pow).then_inc(rs_ready, 1)
                pool.wait_ge(v_ready, t + 1)
                v = HS[:, s, :]
                nc.gpsimd.tensor_tensor(v, v, gbB[:, 0, :], ALU.mult).then_inc(pool_step, 1)
                pool.wait_ge(pool_step, step.at + 2 * t + 1)
                nc.gpsimd.tensor_tensor(v, v, gbB[:, 1, :], ALU.add).then_inc(pool_step, 1)
                pool.wait_ge(pool_step, step.at + 2 * t + 2)
                nc.gpsimd.tensor_tensor(XH[:, ds(t, 1), :], XH[:, ds(t, 1), :], HS[:, s:s + 1, :], ALU.add).then_inc(x2_ready, 1)
            over_pairs(pool, (T - 1) // 2, 1, lambda t, s, warm: finish(t, s))

            pool.wait_ge(s1_ready, TOPK * FQ * (CHUNKS + 1))
            nc.gpsimd.memset(A[:, 0:T * ROW], 0.0).then_inc(h2_zero, 1)
            for j in range(4):
                pool.wait_ge(z_stored[j], 16 * of_slot(j, 4))

            pool.wait_ge(wide_ready, 1)
            is_wide = load_wide(mybir.EngineType.Pool)
            with pool.If(is_wide > 0):
                with pool.Fori(0, SUB * GROUPS) as c:
                    pool.wait_ge(mcol_ready, c + 1)
                    pool.sem_inc(gather_turn, 1)
                    pool.indirect_dma_start(mrow, None, zTab, bass.IndirectOffsetOnAxis(ap=cidx[:, 0:1], axis=0)).then_inc(mrow_in, 16)
                pool.wait_ge(mrow_in, SUB * GROUPS * 16)
                pool.wait_ge(mmax_step, MSTEPS * SUB * GROUPS + 1)

            def gather2(n, j, i):
                pool.wait_ge(idx2_ready, n + 1)
                if past(n, 3):
                    pool.wait_ge(us_ready, (HALF - 1) * (n - 2))
                    pool.wait_ge(act_scaled, n - 2)
                else:
                    pool.wait_ge(dls_ready, 1)
                pool.sem_inc(gather_turn, 1)
                for s in range(NS):
                    pool.indirect_dma_start(ROWS2[j % 3][:, s, :], None, zTab,
                                            bass.IndirectOffsetOnAxis(ap=IDX[:, j % 3, s:s + 1], axis=0)).then_inc(rows2_in[j % 3], 16)
            over(pool, BODIES, 6, gather2)

            pool.wait_ge(rd_ready, 1)

            def divide(t, s, warm):
                if warm:
                    pool.wait_ge(x3_ready, t - 1)
                nc.gpsimd.tensor_tensor(HS[:, s, :].rearrange("p (a h o) -> p a h o", a=1, h=GH),
                                        H2[:, ds(t, 1), 0:D].rearrange("p t (h o) -> p t h o", h=GH),
                                        RD[:, ds(t, 1), :].rearrange("p t (h a) -> p t h a", a=1).broadcast_to((P, 1, GH, GO)),
                                        ALU.mult).then_inc(h3_ready, 1)
            over_pairs(pool, (T - 1) // 2, 1, divide)

            pool.wait_ge(sum_ready, GROUPS)
            nc.gpsimd.memset(SWsum, 0.0).then_inc(sw_summed, 1)

            def slices(t, j, i):
                if past(t, 2):
                    sum_slices(t - 2, (j - 2) % 4, P)
                pool.wait_ge(l_max, t + 1)
                lv = SW[j % 4].rearrange("p (h g) -> p h g", h=SH)
                nc.gpsimd.tensor_tensor(lv, lv, ax[:, j % 2, :].rearrange("p (h a) -> p h a", a=1).broadcast_to((P, SH, SG)), ALU.subtract).then_inc(l_less, 1)

            def sum_slices(t, s, np_):
                pool.wait_ge(sw_ready, t + 1)
                pool.wait_ge(sw_summed, t + 1)
                nc.gpsimd.tensor_tensor(SWsum[0:np_, :], SWsum[0:np_, :], SW[s][0:np_, :], ALU.add).then_inc(sw_summed, 1)
            over(pool, T, 8, slices, 1)
            sum_slices(T - 2, (T - 2) % 4, P)
            sum_slices(T - 1, (T - 1) % 4, LAST)

        @block.vector
        def _(dve):
            step = Chain(dve, dve_step)
            dve.wait_ge(last_in, 16)
            nc.vector.tensor_copy(lastF[:, :], lastI[:, :]).then_inc(lastf_ready, 1)
            dve.wait_ge(consts_ready, 1)
            dve.wait_ge(lastrow_ready, 1)
            h = NBP // 2
            for i in range(2):
                step(nc.vector.tensor_scalar(cmp[:, i * h:(i + 1) * h], PB[i][0:T - 1, 0:h], thr[0:T - 1, 0:1], None, ALU.is_lt))
            step(nc.vector.tensor_reduce(thr[0:T - 1, 1:2], cmp, AX.X, ALU.add))
            step(nc.vector.tensor_tensor(thr[0:T - 1, 1:2], thr[0:T - 1, 1:2], iotap[0:T - 1, :], ALU.add))
            nc.vector.tensor_scalar(tcmp, kk[0:T - 1, :], thr[0:T - 1, 1:2], None, ALU.is_gt).then_inc(tcmp_ready, 1)
            dve.wait_ge(tk_psum, 1)
            hk = GC * P // 2
            for i in range(2):
                step(nc.vector.tensor_copy(TK[:, i * hk:(i + 1) * hk], PB[2 + i][:, 0:hk]))
            step(nc.vector.tensor_copy(cols[:, 1, :], PB[4][:, 0:GC]))
            step(nc.vector.tensor_tensor(cols[:, 2, :], cols[:, 0, :], cols[:, 1, :], ALU.subtract))
            step(nc.vector.tensor_scalar_min(cols[:, 2, :], cols[:, 2, :], float(NBP - 1)))
            step(nc.vector.tensor_scalar_mul(cols[:, 3, :], cols[:, 1, :], float(P)))
            nc.vector.tensor_copy(cidx[:, :], cols[:, 2, :]).then_inc(cidx_ready, 1)
            def stats(t, s, warm):
                nc.vector.bn_stats(BS[:, ds(t, 1), :], XH[:, ds(t, 1), :]).then_inc(dve_step, 1)

            for j in range(GC):
                s = j % 2
                dve.wait_ge(tab_in[s], 48 * (j // 2 + 1))
                if j >= 2:
                    dve.wait_ge(tab_turned, j - 1)
                    dve.wait_ge(dl_stored, 16 * (j - 1))
                step(nc.vector.tensor_scalar(tf[:, s, 0, :], tg[:, s, 0, :].bitcast(i32), cols[:, 3, j:j + 1], None, ALU.subtract))
                step(nc.vector.tensor_copy(tf[:, s, 1, :], tg[:, s, 1, :].bitcast(i32)))
                nc.vector.tensor_copy(tf[:, s, 2, :], tg[:, s, 2, :]).then_inc(tabf_ready, 1)
                lo, hi = T * j // GC, T * (j + 1) // GC
                for i in range(lo // 16, (hi - 1) // 16 + 1):
                    dve.wait_ge(x_in[i], 16)
                for t in range(lo, hi):
                    stats(t, 0, True)
                step.at += hi - lo
                dve.wait_ge(dve_step, step.at)

            def row_stats():
                me, mo, m, v, rs = BS[:, :, 1], BS[:, :, 4], MV[:, :, 0], MV[:, :, 1], RS[:, :]
                step(nc.vector.tensor_tensor(m, me, mo, ALU.subtract))
                step(nc.vector.tensor_tensor(m, m, m, ALU.mult))
                step(nc.vector.tensor_tensor(v, BS[:, :, 2], BS[:, :, 5], ALU.add))
                step(nc.vector.tensor_scalar_mul(v, v, 1.0 / D))
                step(nc.vector.scalar_tensor_tensor(v, m, 0.25, v, ALU.mult, ALU.add))
                step(nc.vector.tensor_tensor(m, me, mo, ALU.add))
                step(nc.vector.tensor_scalar_mul(m, m, 0.5))
                nc.vector.tensor_scalar_add(rs, v, EPS).then_inc(veps_ready, 1)

            dve.wait_ge(consts_ready, 2)
            row_stats()
            dve.wait_ge(sqrt_ready, 1)
            step(nc.vector.reciprocal(RS[:, :], RS[:, :]))
            step(nc.vector.scalar_tensor_tensor(nmr[:, :], MV[:, :, 0], -1.0, RS[:, :], ALU.mult, ALU.mult))
            step(nc.vector.tensor_scalar_add(rs1[:, :], RS[:, :], 1.0))

            def norm(t, j, i):
                if past(t, 8):
                    dve.wait_ge(h_turned, t - 7)
                    dve.wait_ge(h_stored[j], i * 16)
                nc.vector.tensor_scalar(HT[:, j:j + 1, :], XH[:, ds(t, 1), :], MV[:, ds(t, 1), 0], RS[:, ds(t, 1)],
                                        ALU.subtract, ALU.mult).then_inc(h_ready, 1)
            dve.wait_ge(tab_turned, GC)
            dve.wait_ge(dl_stored, 16 * GC)
            over(dve, T, 8, norm)
            dve.wait_ge(h_ready, T)
            dve.sem_inc(rs1_ready, 1)
            dve.wait_ge(h_kept, T)
            dve.wait_ge(deg_zero, 1)

            tks = []


            def onehots(n, j, i):
                if j % 2 == 0:
                    first = isinstance(n, int) and n == 0
                    v = tiles_of(0 if first else n * UG - 1, 2 * UG, mybir.EngineType.DVE)
                    tks[:] = (None, *v[0:2 * UG - 1]) if first else v
                dve.wait_ge(idx_ready, n + 1)
                for g in range(UG):
                    gi = n * UG + g
                    if past(n, 1):
                        dve.wait_ge(part_ready, gi - 1)
                    for b in range(SUB):
                        c = j * NU + g * SUB + b
                        nc.vector.tensor_scalar(S[:, g, b, :], iota[:, :], DLU[:, c:c + 1], WS[:, c:c + 1],
                                                ALU.is_equal, ALU.mult).then_inc(onehot_ready, 1)
                        nc.vector.tensor_scalar(S1[:, g, b, :], iota[:, :], DLU[:, c:c + 1], None,
                                                ALU.is_equal).then_inc(onehot_ready, 1)
                    if past(n, 1) or g >= 1:
                        add_part(gi - 1, 1 - g, tks[(j % 2) * UG + g])

            def add_part(gi, sl, tk):
                dve.wait_ge(part_ready, gi + 1)
                if past(gi, 1):
                    dve.wait_ge(part_added, gi)
                y = A[:, ds(tk * 384, 384)]
                nc.vector.tensor_tensor(y, y, PB[sl][:, 0:384], ALU.add).then_inc(part_added, 1)
            over(dve, UNITS, 4, onehots)
            add_part(GROUPS - 1, (GROUPS - 1) % 2, tiles_of(GROUPS - 1, 1, mybir.EngineType.DVE)[0])

            dve.wait_ge(part_added, GROUPS)
            nc.vector.tensor_scalar_max(YD[:, :, 2, :], YD[:, :, 2, :], 1.0).then_inc(degmax, 1)
            dve.wait_ge(degsqrt, 1)

            def invert(lo, n):
                r = YD[:, ds(lo, n), 2, :]
                nc.vector.reciprocal(r, r).then_inc(deg_ready, 1)

            def chunk_stats(q, base):
                def f(c, s, warm, n=512):
                    if q and n == 512:
                        invert(c + (T - CHUNKS), 1)
                    for k in range(KC):
                        bank = PB[2 * s + k]
                        dve.wait_ge(lin_ready, base + KC * c + k + 1)
                        if q:
                            nt = 4 if n == 512 else 1
                            o = bank[:, 0:nt * P if n == 512 else n]
                            if n == 512:
                                o3 = o.rearrange("p (t n) -> p t n", n=P)
                                r = YD[:, ds(c * 4, 4), 2, :]
                            else:
                                o3, r = o, YD[:, T - 1, 2, 0:n]
                            if k == 0:
                                dve.wait_ge(deg_ready, CHUNKS + 1 + (c + 1 if n == 512 else CHUNKS))
                            nc.vector.tensor_tensor(o3, o3, r, ALU.mult).then_inc(dve_step, 1)
                            dve.wait_ge(dve_step, step.at + (KC * c + k + 1))
                        nc.vector.bn_stats(BSF[:, k, ds(c, 1), :], bank[:, 0:n]).then_inc(lin_stat, 1)
                    if not q:
                        invert(3 * c, 3 if n == 512 else 1)
                return f

            def batchnorm(q, base):
                f = chunk_stats(q, base)
                over_pairs(dve, CHUNKS // 2, 0, f)
                f(CHUNKS, 0, True, LAST)
                if q:
                    step.at += KC * (CHUNKS + 1)
                dve.wait_ge(lin_stat, (q + 1) * KC * (CHUNKS + 1))
                for k in range(KC):
                    step(nc.vector.bn_aggr(MVF[:, k, :], BSF[:, k, :, :]))
                nc.vector.tensor_scalar_add(bns[:, 0, :], MVF[:, :, 1], EPS).then_inc(bn_var, 1)
                dve.wait_ge(bn_sqrt, q + 1)
                step(nc.vector.reciprocal(bns[:, 0, :], bns[:, 0, :]))
                step(nc.vector.tensor_tensor(bns[:, 1, :], bns[:, 0, :], bnp[:, 2 * q, :], ALU.mult))
                step(nc.vector.tensor_tensor(bns[:, 2, :], MVF[:, :, 0], bns[:, 1, :], ALU.mult))
                nc.vector.tensor_tensor(bns[:, 3, :], bnp[:, 2 * q + 1, :], bns[:, 2, :], ALU.subtract).then_inc(bn_ready, 1)
            dve.wait_ge(par_in, 16 * NPAR)
            batchnorm(0, 0)
            batchnorm(1, KC * (CHUNKS + 1))

            dve.wait_ge(h_added, 1)

            def residual(t, j, i):
                dve.wait_ge(r_turned, t + 1)
                nc.vector.tensor_tensor(XH[:, ds(t, 1), :], XH[:, ds(t, 1), :], PB[j][:, 0:D].rearrange("p (a d) -> p a d", a=1), ALU.add).then_inc(x1_ready, 1)
                if past(t, 1):
                    dve.wait_ge(x1_ready, t)
                    stats(t - 1, j, True)
            over(dve, T, 4, residual)
            dve.wait_ge(x1_ready, T)
            stats(T - 1, 0, True)
            step.at += T
            dve.wait_ge(dve_step, step.at)

            row_stats()
            dve.wait_ge(sqrt_ready, 2)
            step(nc.vector.reciprocal(RS[:, :], RS[:, :]))
            step(nc.vector.scalar_tensor_tensor(nmr[:, :], MV[:, :, 0], -1.0, RS[:, :], ALU.mult, ALU.mult))
            dve.wait_ge(r_turned, T)

            def sum_t1(c, n=512):
                nc.vector.tensor_reduce(BSF[:, :, ds(c, 1), 0], T1T[:, :, ds(c * 512, n)], AX.X, ALU.add).then_inc(sums_ready, 1)

            def norm1(t, j, i):
                if past(t, 4):
                    dve.wait_ge(t1_turned, t - 3)
                nc.vector.tensor_scalar(R4[:, j:j + 1, :], XH[:, ds(t, 1), :], MV[:, ds(t, 1), 0], RS[:, ds(t, 1)],
                                        ALU.subtract, ALU.mult).then_inc(t1_ready, 1)
                if j == 3 and past(t, 4):
                    dve.wait_ge(t1_kept, t - 3)
                    sum_t1(i - 1)
            over(dve, T, 4, norm1)

            dve.wait_ge(t1_kept, T)
            sum_t1(CHUNKS - 1)
            sum_t1(CHUNKS, LAST)
            dve.wait_ge(sums_ready, CHUNKS + 1)
            step(nc.vector.tensor_reduce(ms[:, :], BSF[:, :, :, 0], AX.X, ALU.add))
            for k in range(KC):
                ins = nc.vector.tensor_scalar(MSB[:, k, :], ones[:, :], ms[:, k:k + 1], 1.0 / N, ALU.mult, ALU.mult)
                ins.then_inc(msb_ready, 1)
            dve.wait_ge(logits_ready, 1)
            lg, p, eq, p2 = rt[:, 1, :], rt[:, 2, :], rt[:, 3, :], rt[:, 4, :]
            step(nc.vector.tensor_tensor(lg, PB[4][:, 0:NX], rt[:, 0, :], ALU.add))

            def softmax8(nth):
                step(nc.vector.tensor_reduce(r1[:, 0:1], lg, AX.X, ALU.max))
                nc.vector.tensor_scalar(lg, lg, r1[:, 0:1], None, ALU.subtract).then_inc(exp_in, 1)
                dve.wait_ge(exp_out, nth)
                step(nc.vector.tensor_reduce(r1[:, 1:2], p, AX.X, ALU.add))
                step(nc.vector.reciprocal(r1[:, 1:2], r1[:, 1:2]))
                step(nc.vector.tensor_scalar(p, p, r1[:, 1:2], None, ALU.mult))
            softmax8(1)
            step(nc.vector.tensor_scalar_min(lg, p, CAP / N))
            softmax8(2)
            iota8 = iota[:, 0:NX]
            for j in range(TOPK):
                src_ = p if j == 0 else p2
                step(nc.vector.tensor_reduce(r1[:, 2 + j:3 + j], src_, AX.X, ALU.max))
                step(nc.vector.tensor_scalar(eq, src_, r1[:, 2 + j:3 + j], -float(NX), ALU.is_ge, ALU.mult))
                step(nc.vector.tensor_tensor(eq, eq, iota8, ALU.add))
                step(nc.vector.tensor_reduce(r1[:, 4 + j:5 + j], eq, AX.X, ALU.min))
                step(nc.vector.tensor_scalar_add(r1[:, 4 + j:5 + j], r1[:, 4 + j:5 + j], float(NX)))
                step(nc.vector.tensor_scalar(ohs[:, j, :], iota8, r1[:, 4 + j:5 + j], None, ALU.is_equal))
                if j == 0:
                    step(nc.vector.scalar_tensor_tensor(p2, ohs[:, 0, :], -2.0, p, ALU.mult, ALU.add))
            for j in range(TOPK):
                ins = nc.vector.scalar_tensor_tensor(EI[:, j, :], emul[:, :], r1[:, 4 + j:5 + j], ebase[:, :], ALU.mult, ALU.add)
                step(ins)
            dve.sem_inc(chosen, 1)
            nc.vector.tensor_tensor(r1[:, 6:7], r1[:, 3:4], r1[:, 2:3], ALU.subtract).then_inc(exp_in, 1)
            dve.wait_ge(exp_out, 3)
            step(nc.vector.tensor_scalar_add(r1[:, 8:9], r1[:, 7:8], 1.0))
            step(nc.vector.reciprocal(r1[:, 8:9], r1[:, 8:9]))
            step(nc.vector.tensor_tensor(r1[:, 9:10], r1[:, 7:8], r1[:, 8:9], ALU.mult))
            step(nc.vector.tensor_scalar(ohs[:, 2, :], ohs[:, 0, :], r1[:, 8:9], None, ALU.mult))
            step(nc.vector.scalar_tensor_tensor(ohs[:, 2, :], ohs[:, 1, :], r1[:, 9:10], ohs[:, 2, :], ALU.mult, ALU.add))
            dve.sem_inc(chosen, 1)
            dve.wait_ge(ohs_turned, 1)
            nc.vector.tensor_copy(ohT[:, :, :], PB[6][0:NX, 0:3 * P].rearrange("e (j n) -> e j n", j=3)).then_inc(ohT_ready, 1)
            dve.wait_ge(b_picked, 1)
            step(nc.vector.tensor_copy(b1c[:, :], PB[5][:, 0:TOPK * FQ]))
            nc.vector.tensor_copy(B2M[:, :], PB[7][:, 0:D]).then_inc(b_kept, 1)
            dve.wait_ge(ew2_in, 16 * TOPK * FQ)
            for j in range(TOPK):
                nc.vector.tensor_scalar(EW2[:, j, :, :], EW2[:, j, :, :], r1[:, 8 + j:9 + j], None, ALU.mult).then_inc(ew_ready, 1)

            for k in range(KC):
                for q in range(2):
                    step(nc.vector.tensor_tensor(MSB[:, :, :].rearrange("p a b -> p (a b)"), WZ[:, k, 0:D], aB[:, q, :], ALU.mult))
                    step(nc.vector.tensor_reduce(WZ[:, k, D + q * GH:D + (q + 1) * GH],
                                                 MSB[:, :, :].rearrange("p a (c o) -> p (a c) o", o=GO), AX.X, ALU.add))

            dve.wait_ge(t1_turned, T)

            def after_moe(t, s, m, warm):
                V = HS[:, s, :]
                if warm:
                    dve.wait_ge(x2_ready, t - 1)
                    nc.vector.bn_stats(BS[:, ds(t - 2, 1), :], XH[:, ds(t - 2, 1), :]).then_inc(x2_stat, 1)
                dve.wait_ge(moe_ready, t + 1)
                nc.vector.scalar_tensor_tensor(HS[:, s:s + 1, :], XH[:, ds(t, 1), :], RS[:, ds(t, 1)],
                                               PB[4 + m][:, 0:D].rearrange("p (a d) -> p a d", a=1), ALU.mult, ALU.add).then_inc(moe_kept, 1)
                dve.wait_ge(moe_kept, t + 1)
                b = step.at + 3 * t
                nc.vector.scalar_tensor_tensor(V, B2M[:, :], nmr[:, ds(t, 1)], V, ALU.add, ALU.add).then_inc(dve_step, 1)
                dve.wait_ge(dve_step, b + 1)
                nc.vector.bn_stats(vst[:, s, :], V).then_inc(dve_step, 1)
                wait_apart(dve, dve_step, b + 2, dve_turn)
                nc.vector.bn_aggr(vmv[:, s, :], vst[:, s, :]).then_inc(dve_step, 1)
                dve.wait_ge(dve_step, b + 3)
                nc.vector.tensor_scalar_add(vrs[:, s:s + 1], vmv[:, s, 1:2], EPS).then_inc(var_ready, 1)
                dve.wait_ge(rs_ready, t + 1)
                nc.vector.tensor_scalar(V, V, vmv[:, s, 0:1], vrs[:, s:s + 1], ALU.subtract, ALU.mult).then_inc(v_ready, 1)

            def chunk_after(c, s, warm):
                for m in range(4):
                    after_moe(c * 4 + m, m % 2, m, warm or (isinstance(c, int) and c > 0) or m >= 2)
            over_pairs(dve, CHUNKS // 2, 0, chunk_after)
            after_moe(T - 1, 0, 0, True)
            step.at += 3 * T
            dve.wait_ge(x2_ready, T)
            for t in (T - 2, T - 1):
                nc.vector.bn_stats(BS[:, t, :], XH[:, t, :]).then_inc(x2_stat, 1)
            dve.wait_ge(x2_stat, T)
            row_stats()
            dve.wait_ge(sqrt_ready, 3)
            step(nc.vector.reciprocal(RS[:, :], RS[:, :]))

            def norm2(t, j, i):
                if past(t, 4):
                    dve.wait_ge(t2_turned, t - 3)
                nc.vector.tensor_scalar(R4[:, j:j + 1, :], XH[:, ds(t, 1), :], MV[:, ds(t, 1), 0], RS[:, ds(t, 1)],
                                        ALU.subtract, ALU.mult).then_inc(t2_ready, 1)
            over(dve, T, 4, norm2)

            dve.wait_ge(z_kept, 2 * T)
            lo = gm[:, GH:2 * GH]
            step(nc.vector.tensor_reduce(gm[:, 0:GH], EM[:, 0:T - 1, 0:GH].rearrange("p t h -> p h t"), AX.X, ALU.max))
            step(nc.vector.tensor_reduce(lo, EM[:, 0:T - 1, 0:GH].rearrange("p t h -> p h t"), AX.X, ALU.min))
            step(nc.vector.tensor_tensor(gm[0:LAST, 0:GH], gm[0:LAST, 0:GH], EM[0:LAST, T - 1, 0:GH], ALU.max))
            step(nc.vector.tensor_tensor(lo[0:LAST, :], lo[0:LAST, :], EM[0:LAST, T - 1, 0:GH], ALU.min))
            nc.vector.tensor_scalar_mul(lo, lo, -1.0).then_inc(gm_step, 1)
            dve.wait_ge(gm_turned, 1)
            step(nc.vector.tensor_reduce(gm4[:, 0:1], PB[4][0:2 * GH, 0:P], AX.X, ALU.max))
            nc.vector.tensor_scalar(gm4[:, 1:1 + 2 * GH], ident[0:2 * GH, 0:2 * GH], gm4[:, 0:1], None, ALU.mult).then_inc(gm_step, 1)
            dve.wait_ge(gm_spread, 1)
            step(nc.vector.tensor_copy(gm[:, :], PB[4][:, 0:2 * GH]))
            step(nc.vector.tensor_copy(EM[:, :, 0:GH], gm[:, 0:GH].rearrange("p (a h) -> p a h", a=1).broadcast_to((P, T, GH))))
            step(nc.vector.tensor_tensor(sc[:, 0, 0:GH], gm[:, 0:GH], lo, ALU.add))
            step(nc.vector.tensor_reduce(sc[:, 1, 0:1], sc[:, 0, 0:GH], AX.X, ALU.max))
            step(nc.vector.tensor_scalar(wide[:, :], sc[:, 1, 0:1], SPREAD, None, ALU.is_gt))
            dve.sem_inc(wide_ready, 1)

            is_wide = load_wide(mybir.EngineType.DVE)
            with dve.If(is_wide > 0):
                nc.vector.memset(EM[:, :, 0:GH], -1e30).then_inc(mmax_step, 1)
                with dve.Fori(0, GROUPS) as k:
                    for b in range(SUB):
                        c = k * SUB + b
                        at = [c * MSTEPS + 1]

                        def small(ins):
                            ins.then_inc(mmax_step, 1)
                            at[0] = at[0] + 1
                            dve.wait_ge(mmax_step, at[0])
                        dve.wait_ge(mmax_step, at[0])
                        small(nc.vector.tensor_scalar(cidx[:, 0:1], SRCT[:, ds(c, 1)], 0.0, None, ALU.add))
                        small(nc.vector.tensor_scalar(cols[:, 0, 0:1], DLT[:, ds(c, 1)], 0.0, None, ALU.add))
                        dve.sem_inc(mcol_ready, 1)
                        small(nc.vector.tensor_scalar(moh, iota[:, :], cols[:, 0, 0:1], None, ALU.is_equal))
                        nc.vector.tensor_scalar(mout, moh, 1.0, 1e30, ALU.subtract, ALU.mult).then_inc(mmax_step, 1)
                        dve.wait_ge(mmax_step, at[0] + 1)
                        dve.wait_ge(mrow_in, (c + 1) * 16)
                        for h in range(GH):
                            nc.vector.scalar_tensor_tensor(msc[:, h, :], moh, mrow[:, D + h:D + h + 1], mout, ALU.mult, ALU.add).then_inc(msc_ready, 1)
                        dve.wait_ge(msc_turned, c + 1)
                        nc.vector.tensor_reduce(mmax, PB[4][:, :].rearrange("p (h e) -> p h e", h=GH), AX.X, ALU.max).then_inc(mmax_step, 1)
                        at[0] = at[0] + 2
                        dve.wait_ge(mmax_step, at[0])
                        if b == 0:
                            tk = tiles_of(k, 1, mybir.EngineType.DVE)[0]
                        e = EM[:, ds(tk, 1), 0:GH]
                        nc.vector.tensor_tensor(e, e, mmax.rearrange("p (a h) -> p a h", a=1), ALU.max).then_inc(mmax_step, 1)
                dve.wait_ge(mmax_step, MSTEPS * SUB * GROUPS + 1)
            for i in range(3):
                step(nc.vector.tensor_copy(EM3[:, :, i, :], EM[:, :, :]))
                if i < 2:
                    step(nc.vector.tensor_tensor(EM[:, :, :], EM[:, :, :], EM3[:, :, i, :], ALU.subtract))
            dve.sem_inc(em_ready, 1)

            def turned_onehot(gi, half, g):
                if past(gi, HALF):
                    dve.wait_ge(edm_ready, gi - HALF + 1)
                nc.vector.tensor_scalar(ST[:, g, :], ROWB[:, half, g, :], iotap[:, 0:1], None, ALU.is_equal).then_inc(st_ready, 1)

            def scores(n, j, i, between=()):
                k = [0]
                between = list(between)

                def small(ins):
                    ins.then_inc(small_step, 1)
                    k[0] += 1
                    if between:
                        turned_onehot(*between.pop(0))
                    dve.wait_ge(small_step, n * 6 + k[0])
                dve.wait_ge(edm_ready, HALF * (n + 1))
                small(nc.vector.tensor_copy(scn[:, :, :], PB[2 + j % 2][:, 0:NS * 2 * GH].rearrange("p (s v) -> p s v", s=NS)))
                dve.sem_inc(edm_used, 1)
                dve.wait_ge(rows2_in[j % 3], 16 * NS * (2 * i + j // 3 + 1))
                v = [sc[:, i_, :].rearrange("p (s h) -> p s h", h=GH) for i_ in range(4)]
                small(nc.vector.tensor_tensor(v[1], scn[:, :, 0:GH], scn[:, :, GH:2 * GH], ALU.add))
                small(nc.vector.tensor_tensor(v[2], ROWS2[j % 3][:, :, D:ROW], scn[:, :, GH:2 * GH], ALU.add))
                small(nc.vector.scalar_tensor_tensor(sc[:, 1:3, :], sc[:, 1:3, :], 0.01, sc[:, 1:3, :], ALU.mult, ALU.max))
                small(nc.vector.tensor_tensor(sc[:, 3, :], sc[:, 2, :], sc[:, 1, :], ALU.subtract))
                if past(n, 1):
                    dve.wait_ge(expo_out, n)
                small(nc.vector.tensor_scalar_min(sc[:, 0, :], sc[:, 3, :], 0.0))
                dve.sem_inc(expo_in, 1)

            dve.wait_ge(rowb_in[0], 16)
            for g in range(HALF):
                turned_onehot(g, 0, g)
            dve.wait_ge(rowb_in[1], 16)
            scores(0, 0, 0, [(HALF + g, 1, g) for g in range(HALF)])
            dve.wait_ge(h2_zero, 1)

            def add_sum(gi, sl, tk):
                dve.wait_ge(sum_ready, gi + 1)
                if past(gi, 1):
                    dve.wait_ge(sum_added, gi)
                y = A[:, ds(tk * ROW, ROW)]
                nc.vector.tensor_tensor(y, y, SUMS[sl][:, 0:ROW], ALU.add).then_inc(sum_added, 1)

            def attend(n, j, i):
                half, b3 = j % 2, j % 3
                first, end = isinstance(n, int) and n == 0, isinstance(n, int) and n == BODIES - 1
                v = tiles_of(0 if first else n * HALF - LAG, HALF, mybir.EngineType.DVE)
                if first:
                    v = (*(None,) * LAG, *v[0:HALF - LAG])
                dve.wait_ge(dls_ready, n + 1)
                more = not (isinstance(n, int) and n + 2 >= BODIES)
                if more:
                    dve.wait_ge(rowb_in[half], 16 * (3 * i + (j + 2) // 2 + 1))
                for g in range(HALF):
                    gi = n * HALF + g
                    if past(n, 1):
                        dve.wait_ge(sum_ready, gi - HALF + 1)
                    for b in range(SUB):
                        c = g * SUB + b
                        nc.vector.tensor_scalar(SR[g][:, b, :], iota[:, :], DLS[:, b3, c:c + 1], None, ALU.is_equal).then_inc(onehot2_ready, 1)
                    if g == 0:
                        dve.wait_ge(expo_out, n + 1)
                    if g < HALF - 1:
                        u0 = half * NS + g * SUB
                        nc.vector.tensor_tensor(US[:, u0:u0 + SUB, 0:D].rearrange("p s (h o) -> p s h o", h=GH),
                                                ROWS2[b3][:, g * SUB:(g + 1) * SUB, 0:D].rearrange("p s (h o) -> p s h o", h=GH),
                                                US[:, u0:u0 + SUB, D:ROW].rearrange("p s (h a) -> p s h a", a=1).broadcast_to((P, SUB, GH, GO)),
                                                ALU.mult).then_inc(us_ready, 1)
                    if g == 2 and not end:
                        scores(n + 1, j + 1, i, [((n + 2) * HALF + m, half, m) for m in range(HALF)] if more else ())
                    if past(n, 1) or g >= LAG:
                        add_sum(gi - LAG, (g - LAG) % HALF, v[g])
            over(dve, BODIES, 6, attend)
            v = tiles_of(GROUPS - LAG, LAG, mybir.EngineType.DVE)
            for g in range(LAG):
                add_sum(GROUPS - LAG + g, HALF - LAG + g, v[g])
            dve.wait_ge(sum_added, GROUPS)

            step(nc.vector.tensor_scalar_max(RD[:, :, :], H2[:, :, D:ROW], 1e-30))
            step(nc.vector.reciprocal(RD[:, :, :], RD[:, :, :]))
            dve.sem_inc(rd_ready, 1)

            def residual3(t, s, warm):
                dve.wait_ge(h3_ready, t + 1)
                nc.vector.tensor_tensor(XH[:, ds(t, 1), :], XH[:, ds(t, 1), :], HS[:, s:s + 1, :], ALU.add).then_inc(x3_ready, 1)
                if past(t, 1):
                    dve.wait_ge(x3_ready, t)
                    stats(t - 1, s, warm)
            over_pairs(dve, (T - 1) // 2, 1, residual3)
            dve.wait_ge(x3_ready, T)
            stats(T - 1, 0, True)
            step.at += T
            dve.wait_ge(dve_step, step.at)

            dve.wait_ge(par2_in, 16 * 16)
            step(nc.vector.tensor_scalar(it[:, :], it[:, :], 0.1, 5.0, ALU.max, ALU.min))
            step(nc.vector.reciprocal(it[:, :], it[:, :]))
            dve.wait_ge(sum_ready, GROUPS)
            for q in range(PAIRS):
                step(nc.vector.tensor_scalar(bxB[:, q, :], ones[:, :], bxc[:, q:q + 1], None, ALU.mult))
            dve.sem_inc(slp_turn, 1)
            dve.wait_ge(wsl_psum, 1)
            itb = it[:, :].rearrange("p (h a) -> p h a", a=1).broadcast_to((P, SH, SG))
            for k in range(KC):
                step(nc.vector.tensor_tensor(WSL[:, k, :].rearrange("p (h g) -> p h g", h=SH), PB[4 + k][:, :].rearrange("p (h g) -> p h g", h=SH), itb, ALU.mult))
            bv = BSL.rearrange("p (h g) -> p h g", h=SH)
            step(nc.vector.tensor_tensor(bv, PB[6][:, :].rearrange("p (h g) -> p h g", h=SH), bsB.rearrange("p (a g) -> p a g", a=1).broadcast_to((P, SH, SG)), ALU.add))
            step(nc.vector.tensor_tensor(bv, bv, itb, ALU.mult))
            dve.sem_inc(wsl_ready, 1)
            row_stats()
            dve.wait_ge(sqrt_ready, 4)
            step(nc.vector.reciprocal(RS[:, :], RS[:, :]))

            def norm3(t, j):
                if past(t, 8):
                    dve.wait_ge(sw_turned, t - 7)
                nc.vector.tensor_scalar(T3[j].rearrange("p (a d) -> p a d", a=1), XH[:, ds(t, 1), :], MV[:, ds(t, 1), 0], RS[:, ds(t, 1)],
                                        ALU.subtract, ALU.mult).then_inc(t3_ready, 1)
            for t in range(4):
                norm3(t, t)

            def logits(t, j, i):
                if past(t, 2):
                    weights(t - 2, (j - 2) % 4)
                if past(t, 4):
                    dve.wait_ge(sw_turned, t - 3)
                    dve.wait_ge(sw_summed, t - 2)
                dve.wait_ge(l_ready, t + 1)
                nc.vector.tensor_tensor(SW[j % 4], PB[2 + j % 2][:, :], BSL, ALU.add).then_inc(l_kept, 1)
                if past(t, 2):
                    dve.wait_ge(l_less, t - 1)
                dve.wait_ge(l_kept, t + 1)
                nc.vector.tensor_reduce(ax[:, j % 2, :], SW[j % 4].rearrange("p (h g) -> p h g", h=SH), AX.X, ALU.max).then_inc(l_max, 1)
                if before(t, T - 4):
                    norm3(t + 4, (j + 4) % 8)

            def weights(t, j):
                dve.wait_ge(l_exp, t + 1)
                b = step.at + 2 * t
                s = 2 + j % 2
                lv = SW[j].rearrange("p (h g) -> p h g", h=SH)
                nc.vector.tensor_reduce(ax[:, s, :], lv, AX.X, ALU.add).then_inc(dve_step, 1)
                dve.wait_ge(dve_step, b + 1)
                nc.vector.reciprocal(ax[:, s, :], ax[:, s, :]).then_inc(dve_step, 1)
                dve.wait_ge(dve_step, b + 2)
                nc.vector.tensor_tensor(lv, lv, ax[:, s, :].rearrange("p (h a) -> p h a", a=1).broadcast_to((P, SH, SG)), ALU.mult).then_inc(sw_ready, 1)
            over(dve, T, 8, logits, 1)
            for t in (T - 2, T - 1):
                weights(t, t % 4)
            step.at += 2 * T

            dve.wait_ge(tok_pe, 1)
            for k in range(KC):
                step(nc.vector.tensor_copy(XS[:, k, :], PB[6 + k][:, :]))
            step(nc.vector.tensor_scalar_add(sden[:, :], PB[0][:, 0:PAIRS], 1e-5))
            step(nc.vector.reciprocal(sden[:, :], sden[:, :]))
            step(nc.vector.tensor_copy(nrow, PB[1][0:1, :]))
            dve.sem_inc(tok_dve, 1)

            def q3(ap):
                return ap.rearrange("p (q n) -> p q n", q=PAIRS)

            def each(m):
                return m.rearrange("p (a n) -> p a n", a=1).broadcast_to((P, PAIRS, P))

            def per(c):
                return c.rearrange("p (q a) -> p q a", a=1).broadcast_to((P, PAIRS, P))
            dve.wait_ge(tok_pe, 2)
            step(nc.vector.tensor_tensor(STK, q3(PB[2][:, :]), per(sden[:, :]), ALU.mult))
            step(nc.vector.tensor_tensor(STK, STK, each(bm[:, 0, :]), ALU.mult))
            dve.sem_inc(tok_dve, 1)
            dve.wait_ge(tok_pe, 3)
            step(nc.vector.tensor_copy(STT, q3(PB[3][:, :])))
            dve.sem_inc(tok_dve, 1)
            dve.wait_ge(tok_pe, 4)
            step(nc.vector.tensor_copy(QT, q3(PB[4][:, :])))
            step(nc.vector.tensor_copy(KT, q3(PB[5][:, :])))
            step(nc.vector.tensor_copy(VS, q3(PB[6][:, :])))
            dve.sem_inc(tok_dve, 1)
            dve.wait_ge(tok_pe, 5)
            step(nc.vector.scalar_tensor_tensor(AT, q3(PB[7][:, :]), float(64 ** -0.5), each(bm[:, 1, :]), ALU.mult, ALU.add))
            step(nc.vector.tensor_reduce(sden[:, :], AT, AX.X, ALU.max))
            step(nc.vector.tensor_tensor(AT, AT, per(sden[:, :]), ALU.subtract))
            dve.sem_inc(tok_dve, 1)
            dve.wait_ge(tok_exp, 1)
            step(nc.vector.tensor_reduce(sden[:, :], AT, AX.X, ALU.add))
            step(nc.vector.reciprocal(sden[:, :], sden[:, :]))
            step(nc.vector.tensor_tensor(AT, AT, per(sden[:, :]), ALU.mult))
            dve.sem_inc(tok_dve, 1)
            dve.wait_ge(tok_pe, 6)
            step(nc.vector.tensor_copy(ATT, q3(PB[0][:, :])))
            dve.sem_inc(tok_dve, 1)
            dve.wait_ge(tok_pe, 7)
            step(nc.vector.tensor_copy(OST, q3(PB[1][:, :])))
            dve.sem_inc(tok_dve, 1)
            dve.wait_ge(tok_pe, 8)
            for i in range(2):
                step(nc.vector.tensor_copy(VV[:, 2 * i:2 * i + 2, :], PB[2 + i][:, :].rearrange("p (q d) -> p q d", q=2)))
            dve.sem_inc(tok_dve, 1)

            def finish(t, s, warm):
                dve.wait_ge(mix_ready, t + 1)
                nc.vector.tensor_tensor(XH[:, ds(t, 1), :], XH[:, ds(t, 1), :], PB[4 + s][:, 0:D].rearrange("p (a d) -> p a d", a=1), ALU.add).then_inc(dve_step, 1)
                dve.wait_ge(dve_step, step.at + t + 1)
                nc.vector.tensor_tensor(XH[:, ds(t, 1), :], XH[:, ds(t, 1), :], boutB[:, :].rearrange("p (a d) -> p a d", a=1), ALU.add).then_inc(fin_ready, 1)
            over_pairs(dve, (T - 1) // 2, 1, finish)

        @block.scalar
        def _(act):
            for j in range(GC):
                act.wait_ge(tab_turned, j + 1)
                bank = 5 + (j % 2)
                dstc = (DLT, SRCT, WT)
                for a in range(3):
                    pb = PB[bank] if a < 2 else PB[7]
                    o0 = (a % 2) * 256 if a < 2 else (j % 2) * 256
                    nc.scalar.copy(dstc[a][:, j * BLK:(j + 1) * BLK].rearrange("p (k b) -> p b k", b=SUB),
                                   pb[:, o0:o0 + 256].rearrange("p (b k) -> p b k", b=SUB)).then_inc(tab_kept, 1)
            act.wait_ge(veps_ready, 1)
            nc.scalar.sqrt(RS[:, :], RS[:, :]).then_inc(sqrt_ready, 1)
            act.wait_ge(par_in, 16 * NPAR)

            def keep_h(t, j, i):
                wait_apart(act, h_turned, t + 1, act_turn)
                nc.scalar.mul(YD[:, ds(t, 1), 0:2, :], PB[j % 4][:, 0:D].rearrange("p (a c n) -> p a c n", a=1, c=2), bnp[:, 4, 0:1]).then_inc(h_kept, 1)
            over(act, T, 8, keep_h)

            act.wait_ge(tab_kept, 3 * GC)

            def columns(n, j, i):
                if past(n, 4):
                    wait_apart(act, part_ready, UG * (n - 3), act_turn)
                c, o = ds(n * NU, NU), slice(j * NU, (j + 1) * NU)
                nc.scalar.activation(DLU[:, o], DLT[:, c], ACT.Copy).then_inc(act_step, 1)
                nc.scalar.activation(WS[:, o], WT[:, c], ACT.Copy).then_inc(act_step, 1)
                nc.scalar.activation(IDXU[:, o], SRCT[:, c], ACT.Copy).then_inc(act_step, 1)
                act.wait_ge(act_step, (n + 1) * 3)
                act.sem_inc(idx_ready, 1)
            over(act, UNITS, 4, columns)

            act.wait_ge(degmax, 1)
            nc.scalar.sqrt(YD[:, :, 2, :], YD[:, :, 2, :]).then_inc(degsqrt, 1)

            def keep_lin(q, base):
                def f(c, s, warm, n=512):
                    for k in range(KC):
                        act.wait_ge(lin_stat, base + KC * c + k + 1)
                        wait_apart(act, lin_ready, base + KC * c + KC, act_turn)
                        if n == 512:
                            o = YD[:, ds(c * 4, 4), k, :]
                            i = PB[2 * s + k][:, :].rearrange("p (t n) -> p t n", n=P)
                        else:
                            o, i = YD[:, T - 1, k, 0:n], PB[2 * s + k][:, 0:n]
                        nc.scalar.activation(o, i, ACT.Copy).then_inc(lin_kept, 1)
                return f
            for q in range(2):
                base = q * KC * (CHUNKS + 1)
                if q == 1:
                    act.wait_ge(bn_ready, 1)
                    act.wait_ge(lin_kept, KC * (CHUNKS + 1))

                    def relu(c, n=512):
                        for k in range(KC):
                            y = YD[:, ds(c * 4, 4), k, :] if n == 512 else YD[:, T - 1, k, 0:n]
                            nc.scalar.activation(y, y, ACT.Relu, bias=bns[:, 3, k:k + 1], scale=bns[:, 1, k:k + 1]).then_inc(relu_ready, 1)
                    kl = keep_lin(q, base)
                    relu(0)

                    def both(c, s, warm):
                        if isinstance(c, int) and c + 1 >= CHUNKS:
                            relu(c + 1, LAST)
                        else:
                            relu(c + 1)
                        kl(c, s, warm)
                    over_pairs(act, CHUNKS // 2 - 1, 2, both)
                    kl(CHUNKS, 0, True, LAST)
                else:
                    kl = keep_lin(q, base)
                    over_pairs(act, CHUNKS // 2, 0, kl)
                    kl(CHUNKS, 0, True, LAST)
                act.wait_ge(bn_var, q + 1)
                nc.scalar.sqrt(bns[:, 0, :], bns[:, 0, :]).then_inc(bn_sqrt, 1)
            act.wait_ge(bn_ready, 2)
            act.wait_ge(lin_kept, 2 * KC * (CHUNKS + 1))

            def relu2(c, s, warm, n=4):
                if warm:
                    wait_apart(act, r_turned, 4 * (c - 1), act_turn)
                for k in range(KC):
                    nc.scalar.activation(R8[:, s, k, 0:n, :], YD[:, ds(c * 4, n), k, :], ACT.Relu,
                                         bias=bns[:, 3, k:k + 1], scale=bns[:, 1, k:k + 1]).then_inc(r_ready, 1)
            over_pairs(act, CHUNKS // 2, 0, relu2)
            relu2(CHUNKS, 0, True, 1)

            act.wait_ge(veps_ready, 2)
            nc.scalar.sqrt(RS[:, :], RS[:, :]).then_inc(sqrt_ready, 1)
            act.wait_ge(r_turned, T)

            def keep_t1(t, j, i):
                wait_apart(act, t1_turned, t + 1, act_turn)
                nc.scalar.activation(T1T[:, :, ds(t * P, P)], PB[j][:, 0:D].rearrange("p (k n) -> p k n", k=KC), ACT.Copy).then_inc(t1_kept, 1)
            over(act, T, 4, keep_t1)
            for i in range(2):
                act.wait_ge(exp_in, i + 1)
                nc.scalar.activation(rt[:, 2, :], rt[:, 1, :], ACT.Exp).then_inc(exp_out, 1)
            act.wait_ge(exp_in, 3)
            nc.scalar.activation(r1[:, 7:8], r1[:, 6:7], ACT.Exp).then_inc(exp_out, 1)
            act.wait_ge(b_kept, 1)

            def gelu(c, s, warm, n=512):
                for j in range(TOPK):
                    if warm or s == 1:
                        act.wait_ge(hid_used, TOPK * (c - 1) + j + 1)
                    for q in range(FQ):
                        act.wait_ge(s1_ready, (TOPK * c + j) * FQ + q + 1)
                        nc.scalar.activation(HID[:, j, q, 0:n], PB[q][:, 0:n], ACT.Gelu, bias=b1c[:, j * FQ + q:j * FQ + q + 1]).then_inc(gelu_ready, 1)
            over_pairs(act, CHUNKS // 2, 0, gelu)
            gelu(CHUNKS, 0, True, P)
            act.wait_ge(veps_ready, 3)
            nc.scalar.sqrt(RS[:, :], RS[:, :]).then_inc(sqrt_ready, 1)

            def keep_t2(t, s):
                if past(t, 2):
                    act.wait_ge(z_ready, t - 1)
                wait_apart(act, t2_turned, t + 1, act_turn)
                nc.scalar.activation(TT[:, s, :, :], PB[s][:, 0:D].rearrange("p (k n) -> p k n", k=KC), ACT.Copy).then_inc(t2_kept, 1)

            def keep_z(t, j, i):
                if before(t, T - 1):
                    keep_t2(t + 1, (j + 1) % 2)
                if past(t, 4):
                    act.wait_ge(z_stored[j], i * 16)
                wait_apart(act, z_ready, t + 1, act_turn)
                nc.scalar.activation(Z4[:, j, :], PB[2 + j % 2][:, 0:D + 2 * GH], ACT.Copy).then_inc(z_kept, 1)
                nc.scalar.activation(EM[:, ds(t, 1), :], PB[2 + j % 2][:, D:D + 2 * GH].rearrange("p (a b) -> p a b", a=1), ACT.Copy).then_inc(z_kept, 1)
            keep_t2(0, 0)
            over(act, T, 4, keep_z, 1)

            act.wait_ge(z_kept, 2 * T)

            def index_columns(n, b3):
                nc.scalar.activation(IDX[:, b3, :], SRCT[:, ds(n * NS, NS)], ACT.Copy).then_inc(idx2_ready, 1)

            def dst_columns(n, b3):
                nc.scalar.activation(DLS[:, b3, :], DLT[:, ds(n * NS, NS)], ACT.Copy).then_inc(dls_ready, 1)
            for n in range(3):
                index_columns(n, n)
            for n in range(2):
                dst_columns(n, n)

            def expo(n, j, i):
                half, b3 = j % 2, j % 3
                act.wait_ge(expo_in, n + 1)
                if past(n, 2):
                    act.wait_ge(sum_ready, HALF * (n - 1))
                nc.scalar.activation(US[:, half * NS:(half + 1) * NS, D:ROW], sc[:, 0, :].rearrange("p (s h) -> p s h", h=GH), ACT.Exp).then_inc(expo_out, 1)
                wait_apart(act, rows2_in[b3], 16 * NS * (2 * i + j // 3 + 1), act_turn)
                if not (isinstance(n, int) and n + 3 >= BODIES):
                    index_columns(n + 3, b3)
                act.wait_ge(expo_out, n + 1)
                for s in range(NS - SUB, NS):
                    for h in range(GH):
                        c = slice(h * GO, (h + 1) * GO)
                        last = nc.scalar.activation(US[:, half * NS + s, c], ROWS2[b3][:, s, c], ACT.Copy, scale=US[:, half * NS + s, D + h:D + h + 1])
                last.then_inc(act_scaled, 1)
                if not (isinstance(n, int) and n + 2 >= BODIES):
                    if past(n, 1):
                        wait_apart(act, onehot2_ready, NS * n, act_turn)
                    dst_columns(n + 2, (b3 + 2) % 3)
            over(act, BODIES, 6, expo)

            act.wait_ge(veps_ready, 4)
            nc.scalar.sqrt(RS[:, :], RS[:, :]).then_inc(sqrt_ready, 1)

            def keep_t3(t, s):
                if past(t, 2):
                    act.wait_ge(l_ready, t - 1)
                wait_apart(act, t3_turned, t + 1, act_turn)
                nc.scalar.activation(TT[:, s, :, :], PB[s][:, 0:D].rearrange("p (k n) -> p k n", k=KC), ACT.Copy).then_inc(t3_kept, 1)

            def exp_sw(t, j):
                wait_apart(act, l_less, t + 1, act_turn)
                nc.scalar.activation(SW[j], SW[j], ACT.Exp).then_inc(l_exp, 1)

            def keep_sw(t, s):
                wait_apart(act, sw_turned, t + 1, act_turn)
                nc.scalar.activation(SWT[:, ds(t, 1), :, :].rearrange("p a q n -> p a (q n)"), PB[4 + s][:, :].rearrange("p (a n) -> p a n", a=1), ACT.Copy).then_inc(sw_kept, 1)

            def slice_copies(t, j, i):
                if before(t, T - 2):
                    keep_t3(t + 2, j % 2)
                if past(t, 1):
                    exp_sw(t - 1, (j - 1) % 4)
                if past(t, 2):
                    keep_sw(t - 2, j % 2)
            keep_t3(0, 0)
            keep_t3(1, 1)
            over(act, T, 8, slice_copies, 1)
            exp_sw(T - 1, (T - 1) % 4)
            keep_sw(T - 2, T % 2)
            keep_sw(T - 1, (T - 1) % 2)
            act.wait_ge(tok_dve, 5)
            nc.scalar.activation(AT, AT, ACT.Exp).then_inc(tok_exp, 1)
            act.wait_ge(tok_dve, 9)
            act.wait_ge(sw_kept, T)

            def stage_sw(t, s, warm):
                if warm:
                    wait_apart(act, mix_ready, t - 1, act_turn)
                nc.scalar.activation(SWS[:, s:s + 1, :], SWT[:, ds(t, 1), :, :].rearrange("p a q n -> p a (q n)"), ACT.Copy).then_inc(swt_staged, 1)
            over_pairs(act, (T - 1) // 2, 1, stage_sw)

        @block.tensor
        def _(pe):
            pe.wait_ge(consts_ready, 1)
            pe.wait_ge(lastf_ready, 1)
            h = NBP // 2
            for i in range(2):
                last = nc.tensor.matmul(PB[i][:, 0:h], ones[0:1, :], lastF[0:1, i * h:(i + 1) * h], start=True, stop=True)
            last.then_inc(lastrow_ready, 1)
            pe.wait_ge(tcmp_ready, 1)
            hk = GC * P // 2
            for i in range(2):
                nc.tensor.matmul(PB[2 + i][:, 0:hk], ones[0:T - 1, :], tcmp[:, i * hk:(i + 1) * hk], start=True, stop=True)
            for j in range(GC):
                last = nc.tensor.matmul(PB[4][:, j:j + 1], tcmp[:, j * P:(j + 1) * P], ones[0:T - 1, 0:1], start=True, stop=True)
            last.then_inc(tk_psum, 1)
            for j in range(GC):
                pe.wait_ge(tabf_ready, j + 1)
                if j >= 2:
                    pe.wait_ge(tab_kept, 3 * (j - 1))
                for a in range(3):
                    pb = PB[5 + (j % 2)] if a < 2 else PB[7]
                    o0 = (a % 2) * 256 if a < 2 else (j % 2) * 256
                    if a == 2 and j >= 1:
                        pe.wait_ge(tab_kept, 3 * j)
                    for b in range(SUB):
                        last = nc.tensor.transpose(pb[:, o0 + b * P:o0 + (b + 1) * P], tf[:, j % 2, a, b * P:(b + 1) * P], ident[:, :])
                last.then_inc(tab_turned, 1)

            def turn_h(t, j, i):
                pe.wait_ge(h_ready, t + 1)
                if past(t, 4):
                    pe.wait_ge(h_kept, t - 3)
                for k in range(KC):
                    last = nc.tensor.transpose(PB[j % 4][:, k * P:(k + 1) * P], HT[:, j, k * P:(k + 1) * P], ident[:, :])
                last.then_inc(h_turned, 1)
            over(pe, T, 8, turn_h)
            pe.wait_ge(h_kept, T)

            def edge_sum(n, j, i):
                pe.wait_ge(rows_in[j], (i + 1) * NU * 16)
                for g in range(UG):
                    gi = n * UG + g
                    pe.wait_ge(onehot_ready, (gi + 1) * 2 * SUB)
                    if past(n, 1):
                        pe.wait_ge(part_added, gi - 1)
                    for k in range(KC):
                        for b in range(SUB):
                            nc.tensor.matmul(PB[g][:, k * P:(k + 1) * P], GU[:, j * NU + g * SUB + b, k * P:(k + 1) * P],
                                             S[:, g, b, :], start=(b == 0), stop=(b == SUB - 1))
                    for b in range(SUB):
                        last = nc.tensor.matmul(PB[g][:, 256:384], onesb[:, :], S1[:, g, b, :], start=(b == 0), stop=(b == SUB - 1))
                    last.then_inc(part_ready, 1)
            over(pe, UNITS, 4, edge_sum)
            pe.wait_ge(part_added, GROUPS)

            pe.wait_ge(par_in, 16 * NPAR)
            for q in range(2):
                base = q * KC * (CHUNKS + 1)

                def lin(c, s, warm, n=512):
                    if q:
                        pe.wait_ge(relu_ready, KC * (c + 1))
                    for f in range(KC):
                        if warm:
                            pe.wait_ge(lin_kept, base + KC * (c - 2) + f + 1)
                            pe.wait_ge(lin_stat, base + KC * (c - 2) + f + 1)
                        for k in range(KC):
                            if n == 512:
                                r = YD[:, ds(c * 4, 4), k, :]
                                o = PB[2 * s + f][:, :].rearrange("p (t n) -> p t n", n=P)
                            else:
                                r, o = YD[:, T - 1, k, 0:n], PB[2 * s + f][:, 0:n]
                            last = nc.tensor.matmul(o, w12[:, q, k, f * P:(f + 1) * P], r, start=(k == 0), stop=(k == KC - 1))
                        last.then_inc(lin_ready, 1)
                if q:
                    pe.wait_ge(lin_kept, base)
                over_pairs(pe, CHUNKS // 2, 0, lin)
                lin(CHUNKS, 0, True, LAST)
            pe.wait_ge(lin_kept, 2 * KC * (CHUNKS + 1))
            def turn_r(c, s, warm, n=4):
                pe.wait_ge(r_ready, (c + 1) * KC)
                for m in range(n):
                    if warm or s == 1:
                        pe.wait_ge(x1_ready, 4 * (c - 1) + m + 1)
                    for k in range(KC):
                        last = nc.tensor.transpose(PB[m][:, k * P:(k + 1) * P], R8[:, s, k, m, :], ident[:, :])
                    last.then_inc(r_turned, 1)
            over_pairs(pe, CHUNKS // 2, 0, turn_r)
            turn_r(CHUNKS, 0, True, 1)

            pe.wait_ge(x1_ready, T)
            def turn_t1(t, j, i):
                pe.wait_ge(t1_ready, t + 1)
                if past(t, 4):
                    pe.wait_ge(t1_kept, t - 3)
                for k in range(KC):
                    last = nc.tensor.transpose(PB[j][:, k * P:(k + 1) * P], R4[:, j, k * P:(k + 1) * P], ident[:, :])
                last.then_inc(t1_turned, 1)
            over(pe, T, 4, turn_t1)
            pe.wait_ge(msb_ready, KC)
            pe.wait_ge(t1_kept, T)
            for k in range(KC):
                last = nc.tensor.matmul(PB[4][:, 0:NX], MSB[:, k, :], wr[:, k, :], start=(k == 0), stop=(k == KC - 1))
            last.then_inc(logits_ready, 1)
            pe.wait_ge(chosen, 2)
            for j in range(3):
                last = nc.tensor.transpose(PB[6][0:NX, j * P:(j + 1) * P], ohs[:, j, :], ident[:, :])
            last.then_inc(ohs_turned, 1)
            pe.wait_ge(ohT_ready, 1)
            for j in range(TOPK):
                for q in range(FQ):
                    nc.tensor.matmul(PB[5][:, j * FQ + q:j * FQ + q + 1], b1s[:, q * P:(q + 1) * P], ohT[:, j, 0:1], start=True, stop=True)
            nc.tensor.matmul(PB[7][:, 0:D], ohT[:, 2, :], b2s[:, :], start=True, stop=True).then_inc(b_picked, 1)

            def experts(c, s, warm, n=512):
                warm = warm or s == 1
                for j in range(TOPK):
                    if not warm:
                        pe.wait_ge(ew1_in[j], 16 * KC)
                    for q in range(FQ):
                        if warm or j:
                            pe.wait_ge(gelu_ready, (TOPK * c + j - 1) * FQ + q + 1)
                        for k in range(KC):
                            last = nc.tensor.matmul(PB[q][:, 0:n], EW1[:, j, k, q * P:(q + 1) * P], T1T[:, k, ds(c * 512, n)],
                                                    start=(k == 0), stop=(k == KC - 1))
                        last.then_inc(s1_ready, 1)
                if not warm:
                    pe.wait_ge(ew_ready, TOPK)
                    pe.wait_ge(b_kept, 1)
                for j in range(TOPK):
                    pe.wait_ge(gelu_ready, (TOPK * c + j + 1) * FQ)
                    for m in range(n // P):
                        if warm and j == 0:
                            pe.wait_ge(moe_kept, 4 * (c - 1) + m + 1)
                        for q in range(FQ):
                            last = nc.tensor.matmul(PB[4 + m][:, 0:D], HID[:, j, q, m * P:(m + 1) * P], EW2[:, j, q, :],
                                                    start=(j == 0 and q == 0), stop=(j == 1 and q == FQ - 1))
                        if j == TOPK - 1:
                            last.then_inc(moe_ready, 1)
                        elif m == n // P - 1:
                            last.then_inc(hid_used, 1)
                pe.wait_ge(moe_ready, 4 * c + n // P)
                pe.sem_inc(hid_used, 1)
            over_pairs(pe, CHUNKS // 2, 0, experts)
            experts(CHUNKS, 0, True, P)

            def turn2(t, j):
                pe.wait_ge(t2_ready, t + 1)
                if past(t, 2):
                    pe.wait_ge(t2_kept, t - 1)
                for k in range(KC):
                    last = nc.tensor.transpose(PB[j % 2][:, k * P:(k + 1) * P], R4[:, j, k * P:(k + 1) * P], ident[:, :])
                last.then_inc(t2_turned, 1)

            def project(t, j, i):
                pe.wait_ge(t2_kept, t + 1)
                if past(t, 2):
                    pe.wait_ge(z_kept, 2 * (t - 1))
                for k in range(KC):
                    last = nc.tensor.matmul(PB[2 + j % 2][:, 0:D + 2 * GH], TT[:, j % 2, k, :], WZ[:, k, :], start=(k == 0), stop=(k == KC - 1))
                last.then_inc(z_ready, 1)
                if before(t, T - 2):
                    turn2(t + 2, (j + 2) % 4)
            pe.wait_ge(gelu_ready, TOPK * FQ * (CHUNKS + 1))
            turn2(0, 0)
            turn2(1, 1)
            over(pe, T, 4, project, 1)

            pe.wait_ge(gm_step, 1)
            pe.wait_ge(z_kept, 2 * T)
            nc.tensor.transpose(PB[4][0:2 * GH, 0:P], gm[:, :], ident[:, :]).then_inc(gm_turned, 1)
            pe.wait_ge(gm_step, 2)
            nc.tensor.matmul(PB[4][:, 0:2 * GH], ones[0:2 * GH, :], gm4[:, 1:1 + 2 * GH], start=True, stop=True).then_inc(gm_spread, 1)
            pe.wait_ge(wide_ready, 1)
            is_wide = load_wide(mybir.EngineType.PE)
            with pe.If(is_wide > 0):
                with pe.Fori(0, SUB * GROUPS) as c:
                    pe.wait_ge(msc_ready, (c + 1) * GH)
                    for h in range(GH):
                        last = nc.tensor.transpose(PB[4][:, h * P:(h + 1) * P], msc[:, h, :], ident[:, :])
                    last.then_inc(msc_turned, 1)
            pe.wait_ge(em_ready, 1)

            def spread(gi, half, g, tk):
                pe.wait_ge(st_ready, gi + 1)
                for b in range(SUB):
                    c = g * SUB + b
                    for i in range(3):
                        last = nc.tensor.matmul(PB[2 + half][:, c * 2 * GH:(c + 1) * 2 * GH].rearrange("p (a v) -> p a v", a=1), ST[:, g, b * P:(b + 1) * P],
                                                EM3[:, ds(tk, 1), i, :], start=(i == 0), stop=(i == 2))
                last.then_inc(edm_ready, 1)

            v = tiles_of(0, HALF, mybir.EngineType.PE)
            for g in range(HALF):
                spread(g, 0, g, v[g])
            v = tiles_of(HALF, HALF, mybir.EngineType.PE)
            for g in range(HALF):
                spread(HALF + g, 1, g, v[g])

            def weighted_sum(n, j, i):
                half = j % 2
                more = not (isinstance(n, int) and n + 2 >= BODIES)
                if more:
                    v = tiles_of((n + 2) * HALF, HALF, mybir.EngineType.PE)
                for g in range(HALF):
                    gi = n * HALF + g
                    pe.wait_ge(onehot2_ready, SUB * (gi + 1))
                    if g < HALF - 1:
                        pe.wait_ge(us_ready, (HALF - 1) * n + g + 1)
                    else:
                        pe.wait_ge(act_scaled, n + 1)
                    if past(n, 1):
                        pe.wait_ge(sum_added, gi - HALF + 1)
                    for b in range(SUB):
                        last = nc.tensor.matmul(SUMS[g][:, 0:ROW], SR[g][:, b, :], US[:, half * NS + g * SUB + b, :], start=(b == 0), stop=(b == SUB - 1))
                    last.then_inc(sum_ready, 1)
                    if g >= 2 and more:
                        if g == 2:
                            pe.wait_ge(edm_used, n + 1)
                        for m in range(2 * g - 4, 2 * g - 2):
                            spread((n + 2) * HALF + m, half, m, v[m])
            over(pe, BODIES, 6, weighted_sum)

            pe.wait_ge(slp_turn, 1)
            for k in range(KC):
                for q in range(PAIRS):
                    nc.tensor.matmul(PB[4 + k][:, q * P:(q + 1) * P], WXT[:, q, k * P:(k + 1) * P], WBD[:, 0, :], start=True, stop=True)
            for q in range(PAIRS):
                last = nc.tensor.matmul(PB[6][:, q * P:(q + 1) * P], bxB[:, q, :], WBD[:, 0, :], start=True, stop=True)
            last.then_inc(wsl_psum, 1)
            pe.wait_ge(wsl_ready, 1)

            def turn3(t, j):
                pe.wait_ge(t3_ready, t + 1)
                if past(t, 2):
                    pe.wait_ge(t3_kept, t - 1)
                for k in range(KC):
                    last = nc.tensor.transpose(PB[j % 2][:, k * P:(k + 1) * P], T3[j][:, k * P:(k + 1) * P], ident[:, :])
                last.then_inc(t3_turned, 1)

            def logits(t, j):
                pe.wait_ge(t3_kept, t + 1)
                if past(t, 2):
                    pe.wait_ge(l_kept, t - 1)
                for k in range(KC):
                    last = nc.tensor.matmul(PB[2 + j % 2][:, :], TT[:, j % 2, k, :], WSL[:, k, :], start=(k == 0), stop=(k == KC - 1))
                last.then_inc(l_ready, 1)

            def tokens(t, j, np_=P):
                first, end = isinstance(t, int) and t == 0, np_ < P
                pe.wait_ge(sw_ready, t + 1)
                for k in range(KC):
                    nc.tensor.matmul(PB[6 + k][:, :], T3[j][0:np_, k * P:(k + 1) * P], SW[j % 4][0:np_, :], start=first, stop=end)
                if past(t, 2):
                    pe.wait_ge(sw_kept, t - 1)
                for q in range(PAIRS):
                    last = nc.tensor.transpose(PB[4 + j % 2][:, q * P:(q + 1) * P], SW[j % 4][:, q * P:(q + 1) * P], ident[:, :])
                last.then_inc(sw_turned, 1)

            def slices(t, j, i):
                if before(t, T - 2):
                    turn3(t + 2, (j + 2) % 8)
                if before(t, T - 1):
                    logits(t + 1, (j + 1) % 8)
                if past(t, 2):
                    tokens(t - 2, (j - 2) % 8)
            turn3(0, 0)
            turn3(1, 1)
            logits(0, 0)
            over(pe, T, 8, slices, 1)
            tokens(T - 2, (T - 2) % 8)
            tokens(T - 1, (T - 1) % 8, LAST)

            pe.wait_ge(sw_summed, T + 1)
            pe.wait_ge(t3_kept, T)
            pe.wait_ge(l_kept, T)
            for q in range(PAIRS):
                nc.tensor.matmul(PB[0][:, q:q + 1], SWsum[:, q * P:(q + 1) * P], ones[:, 0:1], start=True, stop=True)
            nc.tensor.matmul(PB[1][0:1, :], ones[:, 0:1], SWsum, start=True, stop=True).then_inc(tok_pe, 1)
            pe.wait_ge(tok_dve, 1)
            for q in range(PAIRS):
                c = slice(q * P, (q + 1) * P)
                for k in range(KC):
                    nc.tensor.matmul(PB[2][:, c], XS[:, k, c], WFX[:, k, c], start=(k == 0), stop=False)
                last = nc.tensor.matmul(PB[2][:, c], nrow[:, c], bfx[:, c], start=False, stop=True)
            last.then_inc(tok_pe, 1)
            pe.wait_ge(tok_dve, 2)
            for q in range(PAIRS):
                last = nc.tensor.transpose(PB[3][:, q * P:(q + 1) * P], STK[:, q, :], ident[:, :])
            last.then_inc(tok_pe, 1)
            pe.wait_ge(tok_dve, 3)
            pe.wait_ge(sw_kept, T)
            for i in range(2):
                nc.tensor.matmul(PB[4 + i][:, :], WBD[:, 1 + i, :], STT.rearrange("p q n -> p (q n)"), start=True, stop=True)
            for q in range(PAIRS):
                last = nc.tensor.matmul(PB[6][:, q * P:(q + 1) * P], STT[:, q, :], WBD[:, 3, :], start=True, stop=True)
            last.then_inc(tok_pe, 1)
            pe.wait_ge(tok_dve, 4)
            for q in range(PAIRS):
                last = nc.tensor.matmul(PB[7][:, q * P:(q + 1) * P], QT[:, q, :], KT[:, q, :], start=True, stop=True)
            last.then_inc(tok_pe, 1)
            pe.wait_ge(tok_dve, 6)
            for q in range(PAIRS):
                last = nc.tensor.transpose(PB[0][:, q * P:(q + 1) * P], AT[:, q, :], ident[:, :])
            last.then_inc(tok_pe, 1)
            pe.wait_ge(tok_dve, 7)
            for q in range(PAIRS):
                last = nc.tensor.matmul(PB[1][:, q * P:(q + 1) * P], VS[:, q, :], ATT[:, q, :], start=True, stop=True)
            last.then_inc(tok_pe, 1)
            pe.wait_ge(tok_dve, 8)
            for q in range(PAIRS):
                last = nc.tensor.matmul(PB[2 + q // 2][:, (q % 2) * D:(q % 2 + 1) * D], OST[:, q, :], WOUT[:, q, :], start=True, stop=True)
            last.then_inc(tok_pe, 1)
            pe.wait_ge(tok_dve, 9)

            def mix(t, s, warm):
                pe.wait_ge(swt_staged, t + 1)
                if warm:
                    pe.wait_ge(fin_ready, t - 1)
                for q in range(PAIRS):
                    last = nc.tensor.matmul(PB[4 + s][:, 0:D], SWS[:, s, q * P:(q + 1) * P], VV[:, q, :], start=(q == 0), stop=(q == PAIRS - 1))
                last.then_inc(mix_ready, 1)
            over_pairs(pe, (T - 1) // 2, 1, mix)


_INS = ["x", "src", "dst", "edge_weight", "L0_gnn_w1", "L0_gnn_w2", "L0_gnn_gamma1", "L0_gnn_beta1", "L0_gnn_eps_weight",
        "L0_gnn_gamma_h", "L0_gnn_beta_h", "L0_ffn_Wr", "L0_ffn_br", "L0_ffn_W1", "L0_ffn_b1", "L0_ffn_W2", "L0_ffn_b2",
        "L0_ffn_gamma", "L0_ffn_beta", "L1_gnn_W", "L1_gnn_a_src", "L1_gnn_a_dst", "L1_ffn_W_fx", "L1_ffn_b_fx",
        "L1_ffn_W_x", "L1_ffn_b_x", "L1_ffn_W_slice", "L1_ffn_b_slice", "L1_ffn_W_q", "L1_ffn_W_k", "L1_ffn_W_v",
        "L1_ffn_W_out", "L1_ffn_b_out", "L1_ffn_temperature"]
_TURNED = ("L0_gnn_w1", "L0_gnn_w2", "L1_ffn_W_x")


def kernel(**inputs):
    import numpy as _np
    import concourse.bacc as _bacc
    from concourse import mybir as _mybir
    from concourse.bass_utils import run_bass_kernel_spmd as _run

    nc = _bacc.Bacc("TRN2", target_bir_lowering=False, num_devices=1)
    pad = {"src": (NBP * BLK - E, 0), "dst": (NBP * BLK - E, NODST), "edge_weight": (NBP * BLK - E, 0)}
    arrays, args = {}, []
    for name in _INS:
        a = _np.asarray(inputs[name])
        if name in pad:
            a = _np.concatenate([a, _np.full((pad[name][0],), pad[name][1], a.dtype)])
        if name == "x":
            a = _np.concatenate([a, _np.zeros((T * P - N, D), a.dtype)])
        if name in _TURNED:
            a = a.T
        a = _np.ascontiguousarray(a)
        arrays[f"in_{name}_dram"] = a
        args.append(nc.dram_tensor(f"in_{name}_dram", a.shape, _mybir.dt.from_np(a.dtype), kind="ExternalInput").ap())
    args.append(nc.dram_tensor("out_0_dram", (N, D), _mybir.dt.float32, kind="ExternalOutput").ap())
    build(nc, *args)
    r = _run(nc, [arrays], core_ids=[0])
    return r.results[0]["out_0_dram"]
```
